# Optimizing a Trainium2 kernel written in Bass

```python
import numpy as np
import jax
import jax.numpy as jnp

def _softmax(x, axis=-1):
    return jax.nn.softmax(x, axis=axis)

def _gelu(x):
    return jax.nn.gelu(x, approximate=True)

def _silu(x):
    return jax.nn.silu(x)

def _sigmoid(x):
    return jax.nn.sigmoid(x)

def _layernorm(x, axis=-1, eps=1e-05):
    m = jnp.mean(x, axis=axis, keepdims=True)
    v = jnp.var(x, axis=axis, keepdims=True)
    return (x - m) / jnp.sqrt(v + eps)

def _scatter_add(tgt, idx, src, axis=0):
    return tgt.at[idx].add(src)

def _segment_sum(src, seg, n):
    return jax.ops.segment_sum(src, seg, n)
kernel_name = 'mk_xattn_seq_d2_seqx_r4_65101f'

def setup_inputs(seed: int=0):
    np.random.seed(seed)
    _w = jnp.asarray

    def _rec_inputs():
        import jax
        import jax.numpy as jnp
        _rk = jax.random.key(seed)
        x = 7.22e-05 + 1 * jax.random.normal(jax.random.fold_in(_rk, 1), (32, 128, 1024), jnp.float32)
        _lenS = 128 - jax.random.randint(jax.random.fold_in(_rk, 7), (32,), 0, max(1, 128 // 4) + 1, jnp.int32)
        _lenS2 = 128 - jax.random.randint(jax.random.fold_in(_rk, 8), (32,), 0, max(1, 128 // 4) + 1, jnp.int32)
        _ctx_4096P = jax.random.normal(jax.random.fold_in(_rk, 11), (32, 16, 1024), jnp.float32)
        _ctx_4096c = jax.random.dirichlet(jax.random.fold_in(_rk, 511), 0.3 * jnp.ones((16,), jnp.float32), (32, 128))
        _ctx_4096t = jnp.einsum('bsk,bkd->bsd', _ctx_4096c, _ctx_4096P)
        _ctx_4096t = _ctx_4096t * jax.lax.rsqrt(jnp.mean(jnp.square(_ctx_4096t)) + 1e-12) * 0.953939
        ctx_4096 = 4.13588e-05 + 0.999923 * (_ctx_4096t + 0.3 * jax.random.normal(jax.random.fold_in(_rk, 611), (32, 128, 1024), jnp.float32))
        _validS = jnp.arange(128)[None, :] < _lenS[:, None]
        _validS2 = jnp.arange(128)[None, :] < _lenS2[:, None]
        _causal = jnp.tril(jnp.ones((128, 128), dtype=bool))
        mask_Bx1x4096_ff1 = jnp.where(jnp.ones((32, 1, 1024), dtype=bool), 1.0, 0.0).astype(jnp.float32)
        return (x, ctx_4096, mask_Bx1x4096_ff1)
    x, ctx_4096, mask_Bx1x4096_ff1 = _rec_inputs()

    def _L0_xattn_setup():
        import jax, jax.numpy as jnp
        import numpy as np
        NUM_HEADS = 8
        CHUNK = 64
        EPS = 1e-05
        NEG = -1000000000.0

        def _chunk_attn(q, k, v, masks, W_in, b_in, W_out, b_out):
            N, C, T = q.shape
            H, Dh = (NUM_HEADS, C // NUM_HEADS)
            nc = T // CHUNK
            Wq, Wk, Wv = jnp.split(W_in, 3, axis=0)
            bq, bk, bv = jnp.split(b_in, 3, axis=0)

            def proj(t, W, b):
                t = t.transpose(0, 2, 1) @ W.T + b
                return t.reshape(N, nc, CHUNK, H, Dh)
            qh = proj(q, Wq, bq)
            kh = proj(k, Wk, bk)
            vh = proj(v, Wv, bv)
            scale = 1.0 / jnp.sqrt(jnp.asarray(Dh, q.dtype))
            scores = jnp.einsum('bnqhd,bnkhd->bnhqk', qh, kh) * scale
            km = masks[:, 0, :].reshape(N, nc, CHUNK)
            scores = scores + jnp.where(km[:, :, None, None, :] > 0, 0.0, NEG)
            attn = jax.nn.softmax(scores, axis=-1)
            out = jnp.einsum('bnhqk,bnkhd->bnqhd', attn, vh).reshape(N, T, C)
            out = out @ W_out.T + b_out
            out = out.transpose(0, 2, 1) * masks
            return out
        key = jax.random.key(seed)
        ks = jax.random.split(key, 8)
        N, C, T = (4, 128, 1024)
        x = jax.random.normal(ks[0], (N, C, T), dtype=jnp.float32)
        q = jax.random.normal(ks[1], (N, C, T), dtype=jnp.float32)
        k = jax.random.normal(ks[2], (N, C, T), dtype=jnp.float32)
        v = jax.random.normal(ks[3], (N, C, T), dtype=jnp.float32)
        masks = jnp.ones((N, 1, T), dtype=jnp.float32)
        s = 1.0 / np.sqrt(C)
        W_in = jax.random.normal(ks[4], (3 * C, C), dtype=jnp.float32) * s
        b_in = jnp.zeros((3 * C,), dtype=jnp.float32)
        W_out = jax.random.normal(ks[5], (C, C), dtype=jnp.float32) * s
        b_out = jnp.zeros((C,), dtype=jnp.float32)
        return {'x': x, 'q': q, 'k': k, 'v': v, 'masks': masks, 'W_in': W_in, 'b_in': b_in, 'W_out': W_out, 'b_out': b_out}
    _L0_xattn_all = _L0_xattn_setup()
    _L0_xattn_in = {k: v for k, v in _L0_xattn_all.items() if k in ('W_in', 'b_in', 'W_out', 'b_out')}
    del _L0_xattn_all

    def _L1_xattn_setup():
        import jax, jax.numpy as jnp
        import numpy as np
        B, N, C, K = (8, 1024, 64, 30)
        EPS_BN = 1e-05
        TINY = 1e-20

        def _knn(p, k):
            xx = jnp.sum(p * p, axis=1)
            pd = 2.0 * jnp.einsum('bdn,bdm->bnm', p, p) - xx[:, :, None] - xx[:, None, :]
            return jax.lax.top_k(pd, k)[1]

        def _bn(h, g, b):
            mu = jnp.mean(h, axis=(0, 1, 2), keepdims=True)
            var = jnp.var(h, axis=(0, 1, 2), keepdims=True)
            return (h - mu) * jax.lax.rsqrt(var + EPS_BN) * g + b

        def _forward(x_loc, x, W1, g1, b1, W2, g2, b2, W3, g3, b3, k):
            Bsz = x.shape[0]
            idx = _knn(x_loc, k)
            bidx = jnp.arange(Bsz)[:, None, None]
            pts = x_loc.transpose(0, 2, 1)
            rel = pts[bidx, idx] - pts[:, :, None, :]
            xr, yr, zr = (rel[..., 0], rel[..., 1], rel[..., 2])
            sxy2 = xr * xr + yr * yr
            r2 = sxy2 + zr * zr
            rho = jnp.sqrt(jnp.maximum(r2, TINY))
            sxy = jnp.sqrt(jnp.maximum(sxy2, TINY))
            deg_r = r2 < TINY
            deg_p = sxy2 < TINY
            theta = jnp.arctan2(jnp.where(deg_r, 0.0, zr), jnp.where(deg_r, 1.0, sxy))
            phi = jnp.arctan2(jnp.where(deg_p, 0.0, yr), jnp.where(deg_p, 1.0, xr))
            sph = jnp.stack([rho, theta, phi], axis=-1)
            feat = jnp.concatenate([sph, sph - jnp.mean(sph, axis=-1, keepdims=True)], axis=-1)
            lrelu = lambda h: jax.nn.leaky_relu(h, 0.2)
            h = lrelu(_bn(feat @ W1.T, g1, b1))
            h = lrelu(_bn(h @ W2.T, g2, b2))
            h = lrelu(_bn(h @ W3.T, g3, b3))
            att = jax.nn.softmax(h[..., 0], axis=-1)
            xk = x.transpose(0, 2, 1)[bidx, idx]
            agg = jnp.einsum('bnkc,bnk->bnc', xk, att)
            return x + agg.transpose(0, 2, 1)
        key = jax.random.key(seed)
        ks = jax.random.split(key, 12)
        return {'x_loc': jax.random.normal(ks[0], (B, 3, N), jnp.float32), 'x': jax.random.normal(ks[1], (B, C, N), jnp.float32), 'W1': jax.random.normal(ks[2], (6, 6), jnp.float32) * 0.4, 'g1': 1.0 + 0.1 * jax.random.normal(ks[3], (6,), jnp.float32), 'b1': 0.1 * jax.random.normal(ks[4], (6,), jnp.float32), 'W2': jax.random.normal(ks[5], (3, 6), jnp.float32) * 0.4, 'g2': 1.0 + 0.1 * jax.random.normal(ks[6], (3,), jnp.float32), 'b2': 0.1 * jax.random.normal(ks[7], (3,), jnp.float32), 'W3': jax.random.normal(ks[8], (1, 3), jnp.float32) * 0.4, 'g3': 1.0 + 0.1 * jax.random.normal(ks[9], (1,), jnp.float32), 'b3': 0.1 * jax.random.normal(ks[10], (1,), jnp.float32), 'k': K}
    _L1_xattn_all = _L1_xattn_setup()
    _L1_xattn_in = {k: v for k, v in _L1_xattn_all.items() if k in ('W1', 'g1', 'b1', 'W2', 'g2', 'b2', 'W3', 'g3', 'b3')}
    del _L1_xattn_all
    return {'x': x, 'ctx_4096': ctx_4096, 'mask_Bx1x4096_ff1': mask_Bx1x4096_ff1, 'L0_xattn_W_in': _L0_xattn_in['W_in'], 'L0_xattn_b_in': _L0_xattn_in['b_in'], 'L0_xattn_W_out': _L0_xattn_in['W_out'], 'L0_xattn_b_out': _L0_xattn_in['b_out'], 'L1_xattn_W1': _L1_xattn_in['W1'], 'L1_xattn_g1': _L1_xattn_in['g1'], 'L1_xattn_b1': _L1_xattn_in['b1'], 'L1_xattn_W2': _L1_xattn_in['W2'], 'L1_xattn_g2': _L1_xattn_in['g2'], 'L1_xattn_b2': _L1_xattn_in['b2'], 'L1_xattn_W3': _L1_xattn_in['W3'], 'L1_xattn_g3': _L1_xattn_in['g3'], 'L1_xattn_b3': _L1_xattn_in['b3']}

def reference(x, ctx_4096, mask_Bx1x4096_ff1, L0_xattn_W_in, L0_xattn_b_in, L0_xattn_W_out, L0_xattn_b_out, L1_xattn_W1, L1_xattn_g1, L1_xattn_b1, L1_xattn_W2, L1_xattn_g2, L1_xattn_b2, L1_xattn_W3, L1_xattn_g3, L1_xattn_b3):
    import jax
    import jax.numpy as jnp

    def _L0_xattn_ref(x, q, k, v, masks, W_in, b_in, W_out, b_out):
        import jax, jax.numpy as jnp
        import numpy as np
        NUM_HEADS = 8
        CHUNK = 64
        EPS = 1e-05
        NEG = -1000000000.0

        def _chunk_attn(q, k, v, masks, W_in, b_in, W_out, b_out):
            N, C, T = q.shape
            H, Dh = (NUM_HEADS, C // NUM_HEADS)
            nc = T // CHUNK
            Wq, Wk, Wv = jnp.split(W_in, 3, axis=0)
            bq, bk, bv = jnp.split(b_in, 3, axis=0)

            def proj(t, W, b):
                t = t.transpose(0, 2, 1) @ W.T + b
                return t.reshape(N, nc, CHUNK, H, Dh)
            qh = proj(q, Wq, bq)
            kh = proj(k, Wk, bk)
            vh = proj(v, Wv, bv)
            scale = 1.0 / jnp.sqrt(jnp.asarray(Dh, q.dtype))
            scores = jnp.einsum('bnqhd,bnkhd->bnhqk', qh, kh) * scale
            km = masks[:, 0, :].reshape(N, nc, CHUNK)
            scores = scores + jnp.where(km[:, :, None, None, :] > 0, 0.0, NEG)
            attn = jax.nn.softmax(scores, axis=-1)
            out = jnp.einsum('bnhqk,bnkhd->bnqhd', attn, vh).reshape(N, T, C)
            out = out @ W_out.T + b_out
            out = out.transpose(0, 2, 1) * masks
            return out
        out = _chunk_attn(q, k, v, masks, W_in, b_in, W_out, b_out) + x
        mu = jnp.mean(out, axis=2, keepdims=True)
        var = jnp.mean(jnp.square(out - mu), axis=2, keepdims=True)
        return (out - mu) * jax.lax.rsqrt(var + EPS)

    def _L1_xattn_ref(x_loc, x, W1, g1, b1, W2, g2, b2, W3, g3, b3, k):
        import jax, jax.numpy as jnp
        import numpy as np
        B, N, C, K = (8, 1024, 64, 30)
        EPS_BN = 1e-05
        TINY = 1e-20

        def _knn(p, k):
            xx = jnp.sum(p * p, axis=1)
            pd = 2.0 * jnp.einsum('bdn,bdm->bnm', p, p) - xx[:, :, None] - xx[:, None, :]
            return jax.lax.top_k(pd, k)[1]

        def _bn(h, g, b):
            mu = jnp.mean(h, axis=(0, 1, 2), keepdims=True)
            var = jnp.var(h, axis=(0, 1, 2), keepdims=True)
            return (h - mu) * jax.lax.rsqrt(var + EPS_BN) * g + b

        def _forward(x_loc, x, W1, g1, b1, W2, g2, b2, W3, g3, b3, k):
            Bsz = x.shape[0]
            idx = _knn(x_loc, k)
            bidx = jnp.arange(Bsz)[:, None, None]
            pts = x_loc.transpose(0, 2, 1)
            rel = pts[bidx, idx] - pts[:, :, None, :]
            xr, yr, zr = (rel[..., 0], rel[..., 1], rel[..., 2])
            sxy2 = xr * xr + yr * yr
            r2 = sxy2 + zr * zr
            rho = jnp.sqrt(jnp.maximum(r2, TINY))
            sxy = jnp.sqrt(jnp.maximum(sxy2, TINY))
            deg_r = r2 < TINY
            deg_p = sxy2 < TINY
            theta = jnp.arctan2(jnp.where(deg_r, 0.0, zr), jnp.where(deg_r, 1.0, sxy))
            phi = jnp.arctan2(jnp.where(deg_p, 0.0, yr), jnp.where(deg_p, 1.0, xr))
            sph = jnp.stack([rho, theta, phi], axis=-1)
            feat = jnp.concatenate([sph, sph - jnp.mean(sph, axis=-1, keepdims=True)], axis=-1)
            lrelu = lambda h: jax.nn.leaky_relu(h, 0.2)
            h = lrelu(_bn(feat @ W1.T, g1, b1))
            h = lrelu(_bn(h @ W2.T, g2, b2))
            h = lrelu(_bn(h @ W3.T, g3, b3))
            att = jax.nn.softmax(h[..., 0], axis=-1)
            xk = x.transpose(0, 2, 1)[bidx, idx]
            agg = jnp.einsum('bnkc,bnk->bnc', xk, att)
            return x + agg.transpose(0, 2, 1)
        return _forward(x_loc, x, W1, g1, b1, W2, g2, b2, W3, g3, b3, k)
    x = _L0_xattn_ref(x, ctx_4096, ctx_4096, ctx_4096, mask_Bx1x4096_ff1, L0_xattn_W_in, L0_xattn_b_in, L0_xattn_W_out, L0_xattn_b_out)
    x = _L1_xattn_ref(ctx_4096, x, L1_xattn_W1, L1_xattn_g1, L1_xattn_b1, L1_xattn_W2, L1_xattn_g2, L1_xattn_b2, L1_xattn_W3, L1_xattn_g3, L1_xattn_b3, 30)
    return x

_drawn_inputs = setup_inputs


def setup_inputs(seed=0):
    import zlib

    import numpy as np

    out = dict(_drawn_inputs(seed))
    spreads = {'L0_xattn_b_in': (0.0, 0.272), 'L0_xattn_b_out': (0.0, 0.401)}
    factors = {'L1_xattn_g1': 8.0,
     'L1_xattn_b1': 8.0,
     'L1_xattn_g2': 8.0,
     'L1_xattn_b2': 8.0,
     'L1_xattn_W3': 4.189}
    for name, (base, spread) in spreads.items():
        noise = np.random.default_rng([zlib.crc32(name.encode()), seed]).standard_normal(out[name].shape)
        drawn = base * np.exp(spread * noise) if base else spread * noise
        out[name] = jnp.asarray(drawn.astype(out[name].dtype))
    for name, factor in factors.items():
        out[name] = (out[name] * factor).astype(out[name].dtype)
    return out
```

```python
from contextlib import ExitStack

import numpy as np
import concourse.bass as bass
from concourse import mybir

ALU = mybir.AluOpType
ACT = mybir.ActivationFunctionType
AX = mybir.AxisListType
F32 = mybir.dt.float32
BF16 = mybir.dt.bfloat16
U16 = mybir.dt.uint16
I32 = mybir.dt.int32

B, C, T = 32, 128, 1024
P = 128
HEADS, CHUNK = 8, 64
DH = C // HEADS
NEG_MASK = -1.0e9
K = 30
EPS = 1e-5
TINY = 1e-20
TILES = T // P
QUADS = 2
QT = TILES // QUADS
KP = 32
RANKS = KP // 8
LO, HI = 128, T // 128
BITS = 8
KT = 16
GK = 5
GROUPS = K // GK
QCOLS = K * QT
BCOLS = QUADS * QCOLS
N = B * BCOLS
PAIRS = float(N * P)
HALF = T // 2
HCH = HALF // CHUNK
REMOVED = -3.0e38
PI = float(np.pi)
SIGN = -(1 << 31)
RING = 2
SLOPE = 0.2
DEN_FLOOR = 1e-11

_at = {}
_end = 0
for _name, _w in (("ident", P), ("ones", P), ("iota", LO), ("lobias", 1), ("bitval", BITS),
                  ("hival", HI), ("hiiota", HI), ("tmask", QT), ("negs", CHUNK), ("headmask", HEADS)):
    _at[_name] = (_end, _end + _w)
    _end += _w
NCONST = _end
NCODE = KT * LO


def shape_constants():
    c = np.zeros((P, NCONST + NCODE), np.float32)

    def put(name, a):
        c[:, _at[name][0]:_at[name][1]] = a

    lo = np.arange(LO)
    put("ident", np.eye(P))
    put("ones", 1.0)
    put("iota", lo[None, :])
    code = np.zeros((KT, BITS, KT, LO))
    for k in range(KT):
        for b in range(BITS - 1):
            code[k, b, k, :] = np.where((lo >> b) & 1, 1.0, -1.0) / 2.0 ** b
    c[:, NCONST:] = code.reshape(P, NCODE)
    put("lobias", (1.0 - np.array([bin(v).count("1") for v in lo]))[:, None])
    put("bitval", np.array([2.0 ** b if b < BITS - 1 else 0.0 for b in range(BITS)])[None, :])
    put("hival", (np.arange(HI) * LO)[None, :])
    put("hiiota", np.arange(HI)[None, :])
    put("tmask", (np.arange(P)[:, None] % QT == np.arange(QT)[None, :]))
    m = int(-NEG_MASK)
    parts = []
    for _ in range(3):
        e = max(m.bit_length() - 8, 0)
        parts.append((m >> e) << e)
        m -= parts[-1]
    assert m == 0
    put("negs", -np.repeat(np.array(parts + [0]) / 32.0, 32)[:, None])
    put("headmask", (np.arange(C)[:, None] // DH == np.arange(HEADS)[None, :]))
    return c


def gate(eng, sem, value, passed):
    eng.wait_ge(sem, value)
    eng.sem_inc(passed, 1)


class Ticks:

    def __init__(self, eng, sem, base=0):
        self.eng, self.sem, self.base, self.n = eng, sem, base, 0

    def __call__(self, ins):
        ins.then_inc(self.sem, 1)
        self.n += 1
        return ins

    def settle(self):
        self.eng.wait_ge(self.sem, self.base + self.n)


def build(nc, x, ctx, mask, w_in, b_in, w_out, b_out, w1, g1, b1, w2, g2, b2, w3, g3, b3, consts, out):
    y_dram = nc.dram_tensor("y_spill", [B, C, T], F32, kind="Internal").ap()
    with ExitStack() as whole:
        def held(name, shape, dt=F32):
            return whole.enter_context(nc.sbuf_tensor(name, shape, dt))

        cst = held("cst", [P, NCONST])
        con = {n: cst[:, a:b] for n, (a, b) in _at.items()}
        planes = held("planes", [P, 3, N])
        idx_all = held("idx_all", [P, N], U16)
        stats_all = held("stats_all", [P, B, 2])
        stage_a(nc, x, ctx, mask, w_in, b_in, w_out, b_out, consts, y_dram, cst, con, planes, idx_all, stats_all)
        stage_b(nc, con, planes, w1, g1, b1, w2, g2, b2, w3, g3, b3)
        stage_e(nc, con, planes, idx_all, stats_all, y_dram, out)


def stage_a(nc, x, ctx, mask, w_in, b_in, w_out, b_out, consts, y_dram, cst, con, planes, idx_all, stats_all):
    with ExitStack() as st:
        def sb(name, shape, dt=F32):
            return st.enter_context(nc.sbuf_tensor(name, shape, dt))

        def sem(name):
            return st.enter_context(nc.semaphore(name))

        wT = sb("wT", [P, 4, C])
        bias = sb("bias", [P, 4])
        qbias = sb("qbias", [P, 1])
        code = sb("code", [P, KT, LO], BF16)
        identb = sb("identb", [P, P], BF16)
        negs = sb("negs", [P, CHUNK], BF16)
        neghalf = sb("neghalf", [P, P])
        bitval = sb("bitval", [P, BITS], U16)
        hival = sb("hival", [P, HI], U16)
        ctx_s = sb("ctx_s", [P, 2, T])
        sq = sb("sq", [P, T])
        maskb = sb("maskb", [P, 2, T])
        minv = sb("minv", [P, 2, T], BF16)
        x_s = sb("x_s", [P, T])
        nxx = sb("nxx", [P, 2, TILES])
        table = sb("table", [P, 2, HI * 3])
        pd_sb = sb("pd_sb", [P, RING, T])
        vals = sb("vals", [P, RANKS, 8])
        idx16 = sb("idx16", [P, 2, TILES, KP], U16)
        bits16 = sb("bits16", [P, QT, KP, BITS], U16)
        bitsb = sb("bitsb", [P, QT, KP * BITS], BF16)
        hi16 = sb("hi16", [P, QT, KP], U16)
        hi1h = sb("hi1h", [P, QUADS, K * QT, HI], BF16)
        bitsT = sb("bitsT", [P, 2, QT * P], BF16)
        ohT = sb("ohT", [P, 2, QT * P])
        gsb = sb("gsb", [P, 2, GK * QT * HI * 3])
        gm = sb("gm", [P, GK * QT, HI * 3])
        g12 = sb("g12", [P, GK * QT, 12])
        g6 = sb("g6", [P, GK * QT, 6])
        g3c = sb("g3c", [P, GK, QT, 3])
        qs = sb("qs", [P, HALF])
        kt = sb("kt", [P, HALF])
        kz = sb("kz", [P, 2, 2, HEADS, CHUNK])
        vz = sb("vz", [P, 2, HCH, C])
        sS = sb("sS", [P, 2, HEADS, CHUNK])
        mx = sb("mx", [P, 2, HEADS])
        rs = sb("rs", [P, 2, HEADS])
        rr = sb("rr", [P, 2, HEADS])
        pT = sb("pT", [P, HEADS // 2, 2 * CHUNK])
        oT = sb("oT", [P, HALF])
        y_s = sb("y_s", [P, 2, HALF])
        bnst = sb("bnst", [P, 2, 6])
        mv = sb("mv", [P, 2])
        pd_ps = st.enter_context(nc.psum_tensor("pd_ps", [P, 2, HALF], F32))
        s_ps = st.enter_context(nc.psum_tensor("s_ps", [P, HEADS, CHUNK], F32))
        g_ps = st.enter_context(nc.psum_tensor("g_ps", [P, GK, QT, HI * 3 + 0], F32))
        oh_ps = [st.enter_context(nc.psum_tensor(f"oh_ps{i}", [P, QT * P], F32)) for i in range(2)]
        mi_ps = [st.enter_context(nc.psum_tensor(f"mi_ps{i}", [P, 512], F32)) for i in range(2)]
        w_in_landed = sem("w_in_landed")
        ctx_landed = [sem(f"ctx_landed{i}") for i in range(2)]
        mask_landed = [sem(f"mask_landed{i}") for i in range(2)]
        x_landed = sem("x_landed")
        y_stored = sem("y_stored")
        setup_done = sem("setup_done")
        act_setup = sem("act_setup")
        w_turned = sem("w_turned")
        dve_gates = sem("dve_gates")
        sp_gates = sem("sp_gates")
        pool_gates = sem("pool_gates")
        sq_ready = sem("sq_ready")
        minv_ready = sem("minv_ready")
        pd_ready = sem("pd_ready")
        pd_moved = sem("pd_moved")
        topk_done = sem("topk_done")
        topk_step = sem("topk_step")
        misc_ready = sem("misc_ready")
        misc_moved = sem("misc_moved")
        kz_ready = sem("kz_ready")
        s_ready = sem("s_ready")
        max_ready = sem("max_ready")
        shifted = sem("shifted")
        exp_ready = sem("exp_ready")
        sum_ready = sem("sum_ready")
        rcp_ready = sem("rcp_ready")
        probs_ready = sem("probs_ready")
        masked_y = sem("masked_y")
        y_ready = sem("y_ready")
        bn_step = sem("bn_step")
        mv_ready = sem("mv_ready")
        mv_kept = sem("mv_kept")
        bits_ready = sem("bits_ready")
        hi_cut = sem("hi_cut")
        hi_ready = sem("hi_ready")
        bitsb_ready = sem("bitsb_ready")
        idx_kept = sem("idx_kept")
        oh_ready = sem("oh_ready")
        oh_moved = sem("oh_moved")
        g_ready = sem("g_ready")
        g_moved = sem("g_moved")
        pool_step = sem("pool_step")
        g_done = sem("g_done")

        code_in = pd_sb[:].rearrange("p r t -> p (r t)")[:, 0:NCODE]
        wnat = y_s[:].rearrange("p h t -> p (h t)")[:, 0:4 * C].rearrange("p (g c) -> p g c", g=4)
        wi = w_in.rearrange("(g o) c -> o g c", g=3)
        UNITS = QUADS * K
        NG = QUADS * GROUPS
        slot_groups = [(0,), (1, 2), (3, 4), (5,)]

        FILLS = 30

        def misc_base(b):
            return 5 if isinstance(b, int) and b == 0 else b * FILLS

        def first_bank(b):
            return 1 if isinstance(b, int) and b == 0 else 0

        TAIL = misc_base(B) - 5

        def batches(eng, emit):
            emit(0, 0, 0, True, False)
            emit(1, 0, 1, False, False)
            with eng.Fori(1, B // 2 - 1) as j:
                emit(j * 2, j, 0, False, False)
                emit(j * 2 + 1, j, 1, False, False)
            emit(B - 2, B // 2 - 1, 0, False, False)
            emit(B - 1, B // 2 - 1, 1, False, True)

        block = st.enter_context(nc.Block())

        @block.sync
        def _(sp):
            sp.dma_start(cst[:], consts[:, 0:NCONST]).then_inc(w_in_landed, 16)
            sp.dma_start(code_in, consts[:, NCONST:]).then_inc(w_in_landed, 16)
            sp.dma_start(wnat[:, 0:3, :], wi).then_inc(w_in_landed, 16)
            sp.dma_start(wnat[:, 3, :], w_out).then_inc(w_in_landed, 16)
            sp.dma_start(bias[:, 0:3], b_in.rearrange("(g o) -> o g", g=3), allow_slow_non_contiguous=True).then_inc(w_in_landed, 16)
            sp.dma_start(bias[:, 3:4], b_out.rearrange("(o g) -> o g", g=1), allow_slow_non_contiguous=True).then_inc(w_in_landed, 16)

            def load(b, par):
                sp.dma_start(ctx_s[:, par, :], ctx[b]).then_inc(ctx_landed[par], 16)
                sp.dma_start(maskb[:, par, :], mask[b].to_broadcast([P, T])).then_inc(mask_landed[par], 16)

            load(0, 0)

            def emit(b, j, par, first, last):
                if not last:
                    if not first:
                        gate(sp, y_ready, b * 2, sp_gates)
                        gate(sp, misc_ready, misc_base(b), sp_gates)
                    load(b + 1, 1 - par)
                if not first:
                    gate(sp, y_ready, b * 2, sp_gates)
                sp.dma_start(x_s[:], x[b]).then_inc(x_landed, 16)
                gate(sp, y_ready, b * 2 + 2, sp_gates)
                sp.dma_start(y_dram[b], y_s[:].rearrange("p h t -> p (h t)")).then_inc(y_stored, 16)

            batches(sp, emit)
            sp.wait_ge(y_stored, 16 * B)

        @block.tensor
        def _(pe):
            pe.wait_ge(w_in_landed, 96)
            for g in range(4):
                m = nc.tensor.transpose(mi_ps[0][:, g * C:(g + 1) * C], wnat[:, g, :], con["ident"])
            m.then_inc(w_turned, 1)
            pe.wait_ge(act_setup, 5)
            pe.wait_ge(setup_done, 4)

            class Misc:

                def __init__(self, base, bank):
                    self.base, self.bank, self.n = base, bank, 0

                def open(self):
                    if not (isinstance(self.base, int) and self.base + self.n < 2):
                        pe.wait_ge(misc_moved, self.base + self.n - 1)
                    return mi_ps[(self.bank + self.n) % 2]

                def close(self, ins):
                    ins.then_inc(misc_ready, 1)
                    self.n += 1
                    return self.base + self.n

            def norms(misc, b):
                pe.wait_ge(sq_ready, b + 1)
                ps = misc.open()
                for t in range(TILES):
                    m = nc.tensor.matmul(ps[:, t:t + 1], sq[:, bass.ts(t, P)], neghalf[:, 0:1], start=True, stop=True)
                misc.close(m)

            def coordinates(misc, par):
                ps = misc.open()
                for t in range(TILES):
                    m = nc.tensor.matmul(ps[:, 3 * t:3 * t + 3], ctx_s[:, par, bass.ts(t, P)], con["ident"][:, 0:3],
                                         start=True, stop=True)
                misc.close(m)

            def distances(b, par, t):
                s = b * TILES + t
                for h in range(2):
                    if not (isinstance(s, int) and s == 0):
                        pe.wait_ge(pd_moved, s * 2 + h - 1)
                    nc.tensor.matmul(pd_ps[:, h, :], ctx_s[:, par, bass.ts(t, P)], ctx_s[:, par, bass.ts(h, HALF)],
                                     start=True, stop=False)
                    nc.tensor.matmul(pd_ps[:, h, :], neghalf[:], sq[:, bass.ts(h, HALF)],
                                     start=False, stop=True).then_inc(pd_ready, 1)

            def project(misc, par, h):
                cols = bass.ts(h, HALF)
                for g in range(2):
                    misc.close(nc.tensor.matmul(misc.open()[:], wT[:, g, :], ctx_s[:, par, cols], start=True, stop=True))
                for v in range(2):
                    ps = misc.open()
                    for c in range(4):
                        at = h * HALF + (4 * v + c) * CHUNK
                        for a in range(2):
                            m = nc.tensor.matmul(ps[64 * a:64 * a + 64, c * C:(c + 1) * C],
                                                 ctx_s[:, par, at:at + CHUNK], wT[:, 2, :], start=True, stop=True)
                    misc.close(m)

            def scores(b, par, t):
                s = b * TILES + t
                if not (isinstance(s, int) and s == 0):
                    pe.wait_ge(shifted, s)
                pe.wait_ge(kz_ready, s + 1)
                if t == 0:
                    pe.wait_ge(minv_ready, b + 1)
                for e in range(2):
                    ch = 2 * (t % QT) + e
                    keys = minv[:, par, (2 * t + e) * CHUNK:(2 * t + e + 1) * CHUNK]
                    nc.tensor.matmul(s_ps[64 * e:64 * e + 64], negs[:],
                                     keys.rearrange("p (o k) -> p o k", o=1).to_broadcast([P, HEADS, CHUNK]),
                                     start=True, stop=False)
                    m = nc.tensor.matmul(s_ps[64 * e:64 * e + 64], qs[:, bass.ts(ch, CHUNK)], kz[:, t % 2, e],
                                         start=False, stop=True)
                m.then_inc(s_ready, 1)

            def values(misc, b, t):
                s = b * TILES + t
                ps = misc.open()
                pe.wait_ge(probs_ready, s + 1)
                for g in range(HEADS // 2):
                    m = nc.tensor.transpose(ps[:, bass.ts(g, P)],
                                            sS[:, t % 2, 2 * g:2 * g + 2, :].rearrange("p a k -> p (a k)"), con["ident"])
                turned = misc.close(m)
                ps = misc.open()
                pe.wait_ge(misc_moved, turned)
                for e in range(2):
                    for g in range(HEADS // 2):
                        m = nc.tensor.matmul(ps[32 * g:32 * g + 32, bass.ts(e, CHUNK)],
                                             vz[:, t // QT, 2 * (t % QT) + e, 32 * g:32 * g + 32],
                                             pT[:, g, bass.ts(e, CHUNK)], start=True, stop=True)
                return misc.close(m)

            def turn_bits(misc, b, q):
                pe.wait_ge(bitsb_ready, b * QUADS + q + 1)
                ps = misc.open()[:].bitcast(BF16)
                for kk in range(2):
                    for t in range(QT):
                        m = nc.tensor.transpose(ps[:, (kk * QT + t) * P:(kk * QT + t + 1) * P],
                                                bitsb[:, t, kk * P:(kk + 1) * P], identb[:])
                return misc.close(m)

            def gather(b, par, q, groups, turned):
                units = [(q, g * GK + k) for g in groups for k in range(GK)]

                def fill(i):
                    u = q * K + units[i][1]
                    gu = b * UNITS + u
                    if not (isinstance(gu, int) and gu < 2):
                        pe.wait_ge(oh_moved, gu - 1)
                    k = units[i][1]
                    nc.tensor.matmul(oh_ps[u % 2][:], code[:, k % KT, :], bitsT[:, k // KT, :],
                                     start=True, stop=True).then_inc(oh_ready, 1)

                pe.wait_ge(misc_moved, turned)
                fill(0)
                for i, (_, k) in enumerate(units):
                    if i + 1 < len(units):
                        fill(i + 1)
                    u = q * K + k
                    gu = b * UNITS + u
                    gg = b * NG + q * GROUPS + k // GK
                    if k % GK == 0 and not (isinstance(gg, int) and gg == 0):
                        pe.wait_ge(g_moved, gg)
                    pe.wait_ge(oh_moved, gu + 1)
                    for t in range(QT):
                        m = nc.tensor.matmul(g_ps[:, k % GK, t, :], ohT[:, u % 2, bass.ts(t, P)], table[:, par, :],
                                             start=True, stop=True)
                    if k % GK == GK - 1:
                        m.then_inc(g_ready, 1)

            def emit(b, j, par, first, last):
                misc = Misc(misc_base(b), first_bank(b))
                turned = None
                for t in range(TILES):
                    h = t // QT
                    if t < TILES - 1:
                        distances(b, par, t + 1)
                    elif not last:
                        norms(misc, b + 1)
                        distances(b + 1, 1 - par, 0)
                    if t > 0:
                        moved = values(misc, b, t - 1)
                    elif not first:
                        moved = values(misc, b - 1, TILES - 1)
                    if t == 1:
                        coordinates(misc, par)
                    if t == QT or (t == 0 and not first):
                        rows(misc, moved)
                    if not first:
                        if t % QT == 0:
                            turned = turn_bits(misc, b - 1, h)
                        gather(b - 1, 1 - par, h, slot_groups[t % QT], turned)
                    if t == QT - 1:
                        project(misc, par, 1)
                    elif t == TILES - 1 and not last:
                        project(misc, 1 - par, 0)
                    if t < TILES - 1:
                        scores(b, par, t + 1)
                    elif not last:
                        scores(b + 1, 1 - par, 0)

            def rows(misc, moved):
                ps = misc.open()
                pe.wait_ge(misc_moved, moved)
                misc.close(nc.tensor.matmul(ps[:], wT[:, 3, :], oT[:], start=True, stop=True))

            misc0 = Misc(0, 0)
            norms(misc0, 0)
            distances(0, 0, 0)
            project(misc0, 0, 0)
            scores(0, 0, 0)
            batches(pe, emit)
            tail = Misc(TAIL, TAIL % 2)
            rows(tail, values(tail, B - 1, TILES - 1))
            for q in range(QUADS):
                turned = turn_bits(tail, B - 1, q)
                for groups in slot_groups:
                    gather(B - 1, 1, q, groups, turned)

        @block.scalar
        def _(act):
            def move(dst, src, scale=1.0, bias=0.0, func=ACT.Identity):
                return nc.scalar.activation(dst, src, func, scale=scale, bias=bias)

            act.wait_ge(w_in_landed, 96)
            move(code[:].rearrange("p a b -> p (a b)"), code_in).then_inc(act_setup, 1)
            move(identb[:], con["ident"]).then_inc(act_setup, 1)
            move(negs[:], con["negs"]).then_inc(act_setup, 1)
            move(qbias[:], bias[:, 0:1], scale=DH ** -0.5).then_inc(act_setup, 1)
            act.wait_ge(w_turned, 1)
            move(wT[:].rearrange("p a b -> p (a b)"), mi_ps[0][:]).then_inc(act_setup, 1)
            act.wait_ge(act_setup, 5)
            act.wait_ge(setup_done, 4)

            class Moves:

                def __init__(self, base, bank):
                    self.base, self.bank, self.n = base, bank, 0

                def next(self):
                    act.wait_ge(misc_ready, self.base + self.n + 1)
                    self.n += 1
                    return mi_ps[(self.bank + self.n - 1) % 2]

            def norms(mv_, par):
                move(nxx[:, par, :], mv_.next()[:, 0:TILES], scale=2.0).then_inc(misc_moved, 1)
                return mv_.base + mv_.n

            def coordinates(mv_, b, par):
                if not (isinstance(b, int) and b < 2):
                    act.wait_ge(g_done, (b - 1) * NG)
                move(table[:, par, :], mv_.next()[:, 0:3 * TILES]).then_inc(misc_moved, 1)

            def distances(b, par, t, ready=None):
                s = b * TILES + t
                if ready is not None:
                    act.wait_ge(misc_moved, ready)
                if not (isinstance(s, int) and s < RING):
                    act.wait_ge(topk_done, s - RING + 1)
                for h in range(2):
                    act.wait_ge(pd_ready, s * 2 + h + 1)
                    move(pd_sb[:, t % RING, bass.ts(h, HALF)], pd_ps[:, h, :], scale=2.0,
                         bias=nxx[:, par, t:t + 1]).then_inc(pd_moved, 1)

            def project(mv_, b, h):
                move(qs[:], mv_.next()[:], scale=DH ** -0.5, bias=qbias[:]).then_inc(misc_moved, 1)
                if not (isinstance(b, int) and b == 0 and h == 0):
                    act.wait_ge(kz_ready, b * TILES + h * QT)
                move(kt[:], mv_.next()[:], bias=bias[:, 1:2]).then_inc(misc_moved, 1)
                for v in range(2):
                    ps = mv_.next()[:].rearrange("p (m r) -> p m r", r=2 * DH)
                    for a in range(2):
                        zone = vz[64 * a:64 * a + 64, h, 4 * v:4 * v + 4, :].rearrange("p c (g r) -> p (c g) r", r=2 * DH)
                        m = nc.scalar.copy(zone[:, :, a * DH:(a + 1) * DH], ps[64 * a:64 * a + 64, :, a * DH:(a + 1) * DH])
                    m.then_inc(misc_moved, 1)

            def gather(b, groups, q):
                for g in groups:
                    for k in range(g * GK, (g + 1) * GK):
                        u = q * K + k
                        act.wait_ge(oh_ready, b * UNITS + u + 1)
                        move(ohT[:, u % 2, :], oh_ps[u % 2][:], bias=con["lobias"], func=ACT.Relu).then_inc(oh_moved, 1)
                    gi = q * GROUPS + g
                    gg = b * NG + gi
                    act.wait_ge(g_ready, gg + 1)
                    if not (isinstance(gg, int) and gg < 2):
                        act.wait_ge(g_done, gg - 1)
                    nc.scalar.copy(gsb[:, gi % 2, :], g_ps[:].rearrange("p k t c -> p (k t c)")).then_inc(g_moved, 1)

            def emit(b, j, par, first, last):
                mv_ = Moves(misc_base(b), first_bank(b))
                for t in range(TILES):
                    h = t // QT
                    s = b * TILES + t
                    if t < TILES - 1:
                        distances(b, par, t + 1)
                    elif not last:
                        ready = norms(mv_, 1 - par)
                        distances(b + 1, 1 - par, 0, ready)
                    if t > 0 or not first:
                        values(mv_, (t - 1) % TILES)
                    if t == 1:
                        coordinates(mv_, b, par)
                    if t == QT:
                        rows(mv_, b, 0)
                    elif t == 0 and not first:
                        rows(mv_, b - 1, 1)
                    if not first:
                        if t % QT == 0:
                            bits(mv_)
                        gather(b - 1, slot_groups[t % QT], h)
                    if t == QT - 1:
                        project(mv_, b, 1)
                    elif t == TILES - 1 and not last:
                        project(mv_, b + 1, 0)
                    act.wait_ge(shifted, s + 1)
                    flat = sS[:, t % 2].rearrange("p h k -> p (h k)")
                    nc.scalar.activation(flat, flat, ACT.Exp).then_inc(exp_ready, 1)

            def values(mv_, t):
                nc.scalar.copy(pT[:].rearrange("p g k -> p (g k)"), mv_.next()[:]).then_inc(misc_moved, 1)
                move(oT[:, bass.ts(t % QT, P)], mv_.next()[:, 0:P], bias=bias[:, 2:3]).then_inc(misc_moved, 1)

            def rows(mv_, b, h):
                ps = mv_.next()
                if h == 0 and not (isinstance(b, int) and b == 0):
                    act.wait_ge(y_stored, b * 16)
                move(y_s[:, h, :], ps[:], bias=bias[:, 3:4]).then_inc(misc_moved, 1)

            def bits(mv_):
                nc.scalar.copy(bitsT[:].rearrange("p a b -> p (a b)"), mv_.next()[:].bitcast(BF16)).then_inc(misc_moved, 1)

            mv0 = Moves(0, 0)
            ready = norms(mv0, 0)
            distances(0, 0, 0, ready)
            project(mv0, 0, 0)
            batches(act, emit)
            tail = Moves(TAIL, TAIL % 2)
            values(tail, TILES - 1)
            rows(tail, B - 1, 1)
            for q in range(QUADS):
                bits(tail)
                for groups in slot_groups:
                    gather(B - 1, groups, q)

        STEPS = TILES * 7

        @block.vector
        def _(dve):
            dve.wait_ge(w_in_landed, 96)
            nc.vector.tensor_scalar(neghalf[:], con["ones"], -0.5, None, ALU.mult).then_inc(setup_done, 1)
            nc.vector.tensor_copy(bitval[:], con["bitval"]).then_inc(setup_done, 1)
            nc.vector.tensor_copy(hival[:], con["hival"]).then_inc(setup_done, 1)
            nc.vector.memset(vz[:], 0.0).then_inc(setup_done, 1)
            dve.wait_ge(setup_done, 4)

            def invert(b, j, par):
                dve.wait_ge(mask_landed[par], (j + 1) * 16)
                nc.vector.tensor_scalar(minv[:, par, :], maskb[:, par, :], 0.0, None, ALU.is_le).then_inc(minv_ready, 1)

            def digits(b, par, q):
                n = b * QUADS + q
                if not (isinstance(n, int) and n == 0):
                    dve.wait_ge(bitsb_ready, n)
                    dve.wait_ge(hi_ready, n)
                if not (isinstance(b, int) and b == 0):
                    dve.wait_ge(g_done, b * NG - (QUADS - 1 - q) * GROUPS)
                dve.wait_ge(topk_done, (b + 1) * TILES)
                m = QT * KP
                flat = idx16[:, par, q * QT:(q + 1) * QT].rearrange("p t k -> p (t k)")
                nc.vector.tensor_tensor(bits16[:].rearrange("p t k e -> p (t k) e"),
                                        flat.rearrange("p (m o) -> p m o", o=1).to_broadcast([P, m, BITS]),
                                        bitval[:].rearrange("p (o e) -> p o e", o=1).to_broadcast([P, m, BITS]),
                                        ALU.bitwise_and).then_inc(bits_ready, 1)
                nc.vector.tensor_scalar(hi16[:].rearrange("p t k -> p (t k)"), flat, (HI - 1) * LO, None,
                                        ALU.bitwise_and).then_inc(hi_cut, 1)
                dve.wait_ge(hi_cut, n + 1)
                src = hi16[:, :, 0:K].rearrange("p t (k o) -> p k t o", o=1)
                nc.vector.tensor_tensor(hi1h[:, q].rearrange("p (k t) e -> p k t e", t=QT),
                                        src.to_broadcast([P, K, QT, HI]),
                                        hival[:].rearrange("p (o u e) -> p o u e", o=1, u=1).to_broadcast([P, K, QT, HI]),
                                        ALU.is_equal).then_inc(hi_ready, 1)

            def row_stats(b, h):
                dve.wait_ge(y_ready, b * 2 + h + 1)
                nc.vector.bn_stats(bnst[:, h, :], y_s[:, h, :]).then_inc(bn_step, 1)
                if h == 1:
                    if not (isinstance(b, int) and b == 0):
                        dve.wait_ge(mv_kept, b)
                    gate(dve, bn_step, b * 2 + 2, dve_gates)
                    nc.vector.bn_aggr(mv[:], bnst[:].rearrange("p h s -> p (h s)")).then_inc(mv_ready, 1)

            def emit(b, j, par, first, last):
                step = b * STEPS
                if not (isinstance(b, int) and b < 2):
                    dve.wait_ge(idx_kept, (b - 1) * QUADS)
                for t in range(TILES):
                    s = b * TILES + t
                    if t % QT == 0 and not first:
                        digits(b - 1, 1 - par, t // QT)
                    if t == 6:
                        row_stats(b, 0)
                    if t == 5:
                        if not last:
                            invert(b + 1, (b + 1) // 2 if isinstance(b, int) else (j if par == 0 else j + 1), 1 - par)
                    if t == 2 and not first:
                        row_stats(b - 1, 1)
                    gate(dve, pd_moved, s * 2 + 2, dve_gates)
                    work = pd_sb[:, t % RING, :]
                    for r in range(RANKS):
                        nc.vector.max(vals[:, r, :], work).then_inc(topk_step, 1)
                        step = step + 1
                        gate(dve, topk_step, step, dve_gates)
                        found = nc.vector.max_index(idx16[:, par, t, 8 * r:8 * r + 8], vals[:, r, :], work)
                        if r < RANKS - 1:
                            nc.vector.match_replace(work, vals[:, r, :], work, REMOVED).then_inc(topk_step, 1)
                            step = step + 1
                            gate(dve, topk_step, step, dve_gates)
                        else:
                            found.then_inc(topk_done, 1)
                        if r == 0:
                            dve.wait_ge(s_ready, s + 1)
                            nc.vector.tensor_reduce(mx[:, t % 2, :], s_ps[:], AX.X, ALU.max).then_inc(max_ready, 1)
                            dve.wait_ge(max_ready, s + 1)
                            nc.vector.tensor_tensor(sS[:, t % 2], s_ps[:],
                                                    mx[:, t % 2, :].rearrange("p (h o) -> p h o", o=1).to_broadcast([P, HEADS, CHUNK]),
                                                    ALU.subtract).then_inc(shifted, 1)
                    dve.wait_ge(exp_ready, s + 1)
                    nc.vector.tensor_reduce(rs[:, t % 2, :], sS[:, t % 2], AX.X, ALU.add).then_inc(sum_ready, 1)
                    dve.wait_ge(sum_ready, s + 1)
                    nc.vector.reciprocal(rr[:, t % 2, :], rs[:, t % 2, :]).then_inc(rcp_ready, 1)

            invert(0, 0, 0)
            batches(dve, emit)
            for q in range(QUADS):
                digits(B - 1, 1, q)
            row_stats(B - 1, 1)

        @block.gpsimd
        def _(pool):
            pool.wait_ge(w_in_landed, 96)

            def square(b, j, par):
                pool.wait_ge(ctx_landed[par], (j + 1) * 16)
                if not (isinstance(b, int) and b == 0):
                    pool.wait_ge(pd_ready, b * TILES * 2)
                nc.gpsimd.tensor_tensor(sq[:], ctx_s[:, par, :], ctx_s[:, par, :], ALU.mult).then_inc(sq_ready, 1)

            class Steps:
                def __init__(self, base):
                    self.base, self.n = base, 0

                def __call__(self, ins):
                    ins.then_inc(pool_step, 1)
                    self.n += 1
                    pool.wait_ge(pool_step, self.base + self.n)

            def gather(b, par, q, groups, steps):
                for g in groups:
                    gi = q * GROUPS + g
                    gg = b * NG + gi
                    pool.wait_ge(g_moved, gg + 1)
                    rows = GK * QT
                    hot = hi1h[:, q, g * rows:(g + 1) * rows, :].rearrange("p m (e o) -> p (m e) o", o=1)
                    steps(nc.gpsimd.tensor_tensor(gm[:].rearrange("p m (e c) -> p (m e) c", c=3),
                                                  gsb[:, gi % 2, :].rearrange("p (m c) -> p m c", c=3),
                                                  hot.to_broadcast([P, rows * HI, 3]), ALU.mult))
                    steps(nc.gpsimd.tensor_tensor(g12[:], gm[:, :, 0:12], gm[:, :, 12:24], ALU.add))
                    steps(nc.gpsimd.tensor_tensor(g6[:], g12[:, :, 0:6], g12[:, :, 6:12], ALU.add))
                    steps(nc.gpsimd.tensor_tensor(g3c[:].rearrange("p k t c -> p (k t) c"), g6[:, :, 0:3], g6[:, :, 3:6], ALU.add))
                    centre = table[:, par, q * QT * 3:(q + 1) * QT * 3].rearrange("p (o t c) -> p o t c", o=1, c=3)
                    at = b * BCOLS + q * QCOLS + g * rows
                    dst = planes[:, :, bass.ds(at, rows)].rearrange("p c (k t) -> p k t c", t=QT)
                    nc.gpsimd.tensor_tensor(dst, g3c[:], centre.to_broadcast([P, GK, QT, 3]),
                                            ALU.subtract).then_inc(g_done, 1)

            GSTEPS = NG * 4

            def emit(b, j, par, first, last):
                steps = Steps((b - 1) * GSTEPS)
                for t in range(TILES):
                    h = t // QT
                    s = b * TILES + t
                    if t > 0 or not first:
                        normalise(s - 1, (t - 1) % TILES)
                    if t == QT:
                        rows(b, j, par, 0, misc_base(b) + (14 if first else 18))
                    elif t == 0 and not first:
                        rows(b - 1, (b - 1) // 2 if isinstance(b, int) else (j - 1 if par == 0 else j), 1 - par, 1, misc_base(b) + 3)
                    if t % QT == 0 and not first:
                        convert(b - 1, h)
                        if t == 0:
                            keep(b - 1, 1 - par)
                    if t == 3 and not first:
                        gate(pool, mv_ready, b, pool_gates)
                        nc.gpsimd.tensor_copy(stats_all[:, bass.ds(b - 1, 1), :].rearrange("p b s -> p (b s)"),
                                              mv[:]).then_inc(mv_kept, 1)
                    if t % QT != QT - 1:
                        spread_keys(b, t + 1)
                    if t == TILES - 2 and not last:
                        square(b + 1, (b + 1) // 2 if isinstance(b, int) else (j if par == 0 else j + 1), 1 - par)
                    if not first:
                        gather(b - 1, 1 - par, h, slot_groups[t % QT], steps)
                    if t == QT - 1:
                        pool.wait_ge(misc_moved, misc_base(b) + (9 if first else 13))
                        spread_keys(b, t + 1)
                    elif t == TILES - 1 and not last:
                        pool.wait_ge(misc_moved, misc_base(b) + (23 if first else 28))
                        spread_keys(b + 1, 0)

            def normalise(s, t):
                pool.wait_ge(rcp_ready, s + 1)
                nc.gpsimd.tensor_tensor(sS[:, t % 2], sS[:, t % 2],
                                        rr[:, t % 2, :].rearrange("p (h o) -> p h o", o=1).to_broadcast([P, HEADS, CHUNK]),
                                        ALU.mult).then_inc(probs_ready, 1)

            def rows(b, j, par, h, moved):
                pool.wait_ge(misc_moved, moved)
                if h == 0:
                    pool.wait_ge(mask_landed[par], (j + 1) * 16)
                    pool.wait_ge(x_landed, b * 16 + 16)
                cols = bass.ts(h, HALF)
                nc.gpsimd.tensor_tensor(y_s[:, h, :], y_s[:, h, :], maskb[:, par, cols], ALU.mult).then_inc(masked_y, 1)
                pool.wait_ge(masked_y, b * 2 + h + 1)
                nc.gpsimd.tensor_tensor(y_s[:, h, :], y_s[:, h, :], x_s[:, cols], ALU.add).then_inc(y_ready, 1)

            def spread_keys(b, t):
                s = b * TILES + t
                if not (isinstance(s, int) and s < 2):
                    pool.wait_ge(s_ready, s - 1)
                c = t % QT
                src = kt[:, 2 * c * CHUNK:2 * (c + 1) * CHUNK].rearrange("p (e o k) -> p e o k", e=2, o=1)
                heads = con["headmask"].rearrange("p (o h u) -> p o h u", o=1, u=1)
                nc.gpsimd.tensor_tensor(kz[:, t % 2], src.to_broadcast([P, 2, HEADS, CHUNK]),
                                        heads.to_broadcast([P, 2, HEADS, CHUNK]), ALU.mult).then_inc(kz_ready, 1)

            def convert(b, q):
                n = b * QUADS + q
                gate(pool, bits_ready, n + 1, pool_gates)
                if not (isinstance(n, int) and n == 0):
                    gate(pool, oh_ready, n * K, pool_gates)
                nc.gpsimd.tensor_copy(bitsb[:].rearrange("p t m -> p (t m)"),
                                      bits16[:].rearrange("p t k e -> p (t k e)")).then_inc(bitsb_ready, 1)
                pool.wait_ge(hi_ready, n + 1)

            def keep(b, par):
                gate(pool, topk_done, (b + 1) * TILES, pool_gates)
                for q in range(QUADS):
                    dst = idx_all[:, bass.ds(b * BCOLS + q * QCOLS, QCOLS)].rearrange("p (k t) -> p k t", t=QT)
                    nc.gpsimd.tensor_copy(dst, idx16[:, par, q * QT:(q + 1) * QT, 0:K].rearrange("p t k -> p k t")).then_inc(idx_kept, 1)

            square(0, 0, 0)
            pool.wait_ge(misc_moved, 3)
            spread_keys(0, 0)
            batches(pool, emit)
            normalise(B * TILES - 1, TILES - 1)
            rows(B - 1, B // 2 - 1, 1, 1, TAIL + 3)
            keep(B - 1, 1)
            steps = Steps((B - 1) * GSTEPS)
            for q in range(QUADS):
                convert(B - 1, q)
                for groups in slot_groups:
                    gather(B - 1, 1, q, groups, steps)
            pool.wait_ge(mv_ready, B)
            nc.gpsimd.tensor_copy(stats_all[:, B - 1, :], mv[:]).then_inc(mv_kept, 1)
            pool.wait_ge(g_done, B * NG)
            pool.wait_ge(mv_kept, B)


def stage_b(nc, con, planes, w1, g1, b1, w2, g2, b2, w3, g3, b3):
    CH = 4
    W = N // CH
    C1, C2 = 6, 3
    HN = N // 2
    BN = 512
    NB = N // BN
    with ExitStack() as st:
        def sb(name, shape, dt=F32):
            return st.enter_context(nc.sbuf_tensor(name, shape, dt))

        def sem(name):
            return st.enter_context(nc.semaphore(name))

        w1b = sb("w1b", [P, C1, 2, 3])
        gb1 = sb("gb1", [P, 2, C1])
        w2b = sb("w2b", [P, C2, C1])
        gb2 = sb("gb2", [P, 2, C2])
        w3b = sb("w3b", [P, C2])
        gb3 = sb("gb3", [P, 2])
        small = {n: sb("sm_" + n, s) for n, s in dict(
            sum3=[P, 3], mean=[P, 3], cov=[P, 6], covf=[P, 3, 3], rs=[P, C1], mat=[P, C1, 3], ab=[P, C1, 3], mm=[P, C1, 3],
            mh=[P, C1], tri=[P, C1, 3, 3], tm=[P, C1, 3], tv=[P, C1, 3], var=[P, C1], sd=[P, C1], a1=[P, C1], ma=[P, C1],
            bb=[P, C1], mat2=[P, C1, 3], eps=[P, 1], mv2=[P, C2, 2], pm=[P, C2], dv=[P, C2], d2=[P, C2], vv=[P, C2],
            sd2=[P, C2], a2=[P, C2], ma2=[P, C2], bb2=[P, C2], mv3=[P, 2], pm3=[P, 1], dv3=[P, 1], d3=[P, 1], vv3=[P, 1],
            sd3=[P, 1], a3=[P, 1], ma3=[P, 1], bb3=[P, 1], ar2=[P, C2], am2=[P, C2], tot=[P, 8]).items()}
        loaded = sem("b_loaded")
        vstep = sem("b_vstep")
        astep = sem("b_astep")
        pstep = sem("b_pstep")
        tot_ps = st.enter_context(nc.psum_tensor("tot_ps", [P, 4, 512], F32))

        def bc(ap):
            return ap

        with ExitStack() as s1:
            def sb1(name, shape, dt=F32):
                return s1.enter_context(nc.sbuf_tensor(name, shape, dt))

            ab3 = sb1("ab3", [P, 3, W])
            two = sb1("two", [P, 2, W])
            root = sb1("root", [P, 2, W])
            mn = sb1("mn", [P, 2, W])
            mxx = sb1("mxx", [P, 2, W])
            block = s1.enter_context(nc.Block())

            @block.sync
            def _(sp):
                def spread(ap, n):
                    return ap.rearrange("(o n) -> o n", o=1).to_broadcast([P, n])
                sp.dma_start(w1b[:].rearrange("p a b c -> p (a b c)"),
                             spread(w1.rearrange("a b -> (a b)"), C1 * 6)).then_inc(loaded, 16)
                sp.dma_start(gb1[:, 0, :], spread(g1, C1)).then_inc(loaded, 16)
                sp.dma_start(gb1[:, 1, :], spread(b1, C1)).then_inc(loaded, 16)
                sp.dma_start(w2b[:].rearrange("p a b -> p (a b)"),
                             spread(w2.rearrange("a b -> (a b)"), C2 * C1)).then_inc(loaded, 16)
                sp.dma_start(gb2[:, 0, :], spread(g2, C2)).then_inc(loaded, 16)
                sp.dma_start(gb2[:, 1, :], spread(b2, C2)).then_inc(loaded, 16)
                sp.dma_start(w3b[:], spread(w3.rearrange("a b -> (a b)"), C2)).then_inc(loaded, 16)
                sp.dma_start(gb3[:, 0:1], spread(g3, 1)).then_inc(loaded, 16)
                sp.dma_start(gb3[:, 1:2], spread(b3, 1)).then_inc(loaded, 16)
                sp.wait_ge(loaded, 9 * 16)

            A_PER, V_PER = 6, 19

            @block.scalar
            def _(act):
                with act.Fori(0, CH) as c:
                    rel = planes[:, :, bass.ds(c * W, W)]
                    va = c * V_PER + 1
                    act.wait_ge(vstep, va)
                    nc.scalar.activation(ab3[:], rel, ACT.Square).then_inc(astep, 1)
                    act.wait_ge(vstep, va + 3)
                    nc.scalar.activation(root[:], mn[:], ACT.Sqrt).then_inc(astep, 1)
                    nc.scalar.activation(ab3[:], rel, ACT.Abs).then_inc(astep, 1)
                    act.wait_ge(vstep, va + 9)
                    nc.scalar.activation(mn[:], mn[:], ACT.Arctan).then_inc(astep, 1)
                    act.wait_ge(vstep, va + 12)
                    nc.scalar.activation(mn[:], mn[:], ACT.Abs).then_inc(astep, 1)
                    act.wait_ge(vstep, va + 14)
                    nc.scalar.activation(mn[:, 1, :], mxx[:, 1, :], ACT.Abs).then_inc(astep, 1)
                act.wait_ge(vstep, CH * V_PER + 1)
                for i in range(3):
                    nc.scalar.activation(planes[:, i, :], planes[:, i, :], ACT.Identity,
                                         accum_out=small["sum3"][:, i:i + 1]).then_inc(astep, 1)
                act.wait_ge(astep, CH * A_PER + 3)

            @block.vector
            def _(dve):
                v = nc.vector
                v.memset(small["eps"][:], EPS).then_inc(vstep, 1)
                with dve.Fori(0, CH) as c:
                    base, aa = c * V_PER + 1, c * A_PER
                    tick = Ticks(dve, vstep, base)
                    px = planes[:, 0, bass.ds(c * W, W)]
                    py = planes[:, 1, bass.ds(c * W, W)]
                    pz = planes[:, 2, bass.ds(c * W, W)]
                    dve.wait_ge(astep, aa + 1)
                    tick(v.tensor_tensor(two[:, 0, :], ab3[:, 0, :], ab3[:, 1, :], ALU.add))
                    tick.settle()
                    tick(v.tensor_tensor(two[:, 1, :], two[:, 0, :], ab3[:, 2, :], ALU.add))
                    tick.settle()
                    tick(v.tensor_scalar(mn[:], two[:], TINY, None, ALU.max))
                    dve.wait_ge(astep, aa + 3)
                    tick(v.tensor_tensor(mn[:, 0, :], ab3[:, 2, :], root[:, 0, :], ALU.min))
                    tick(v.tensor_tensor(mn[:, 1, :], ab3[:, 1, :], ab3[:, 0, :], ALU.min))
                    tick(v.tensor_tensor(mxx[:, 0, :], ab3[:, 2, :], root[:, 0, :], ALU.max))
                    tick(v.scalar_tensor_tensor(mxx[:, 1, :], ab3[:, 0, :], DEN_FLOOR, ab3[:, 1, :], ALU.max, ALU.max))
                    tick.settle()
                    tick(v.reciprocal(mxx[:], mxx[:]))
                    tick.settle()
                    tick(v.tensor_tensor(mn[:], mn[:], mxx[:], ALU.mult))
                    tick.settle()
                    tick(v.tensor_tensor(mxx[:, 0, :], ab3[:, 2, :], root[:, 0, :], ALU.is_gt))
                    tick(v.tensor_tensor(mxx[:, 1, :], ab3[:, 1, :], ab3[:, 0, :], ALU.is_gt))
                    tick.settle()
                    dve.wait_ge(astep, aa + 4)
                    tick(v.scalar_tensor_tensor(mn[:].rearrange("p a w -> p (a w)"), mxx[:].rearrange("p a w -> p (a w)"),
                                                PI / 2, mn[:].rearrange("p a w -> p (a w)"), ALU.mult, ALU.subtract))
                    tick.settle()
                    tick(v.tensor_scalar(mxx[:, 1, :], px, 0.0, PI, ALU.is_lt, ALU.mult))
                    dve.wait_ge(astep, aa + 5)
                    tick.settle()
                    tick(v.tensor_tensor(mxx[:, 1, :], mxx[:, 1, :], mn[:, 1, :], ALU.subtract))
                    tick(v.scalar_tensor_tensor(mn[:, 0, :].bitcast(I32), pz.bitcast(I32), SIGN, mn[:, 0, :].bitcast(I32),
                                                ALU.bitwise_and, ALU.bitwise_or))
                    dve.wait_ge(astep, aa + 6)
                    tick(v.scalar_tensor_tensor(mn[:, 1, :].bitcast(I32), py.bitcast(I32), SIGN, mn[:, 1, :].bitcast(I32),
                                                ALU.bitwise_and, ALU.bitwise_or))
                    tick.settle()
                    tick(v.scalar_tensor_tensor(py, two[:, 1, :], TINY, mn[:, 0, :], ALU.is_ge, ALU.mult))
                    tick(v.scalar_tensor_tensor(pz, two[:, 0, :], TINY, mn[:, 1, :], ALU.is_ge, ALU.mult))
                    tick(v.tensor_copy(px, root[:, 1, :]))
                    tick.settle()
                    assert tick.n == V_PER, tick.n

        with ExitStack() as s2:
            def sb2(name, shape, dt=F32):
                return s2.enter_context(nc.sbuf_tensor(name, shape, dt))

            def sem2(name):
                return s2.enter_context(nc.semaphore(name))

            th = sb2("th", [P, 2, HN])
            h2 = sb2("h2", [P, C2, HN])
            bst = sb2("bst", [P, C2, NB, 6])
            S = small
            vs = sem2("c_vstep")
            summed = sem2("c_summed")
            mean_in = sem2("c_mean_in")
            cov_in = sem2("c_cov_in")
            var_in = sem2("c_var_in")
            sd_out = sem2("c_sd_out")
            mat_in = sem2("c_mat_in")
            t_out = sem2("c_t_out")
            t_mixed = sem2("c_t_mixed")
            h_out = sem2("c_h_out")
            h_used = sem2("c_h_used")
            w_out_ = sem2("c_w_out")
            h2_in = sem2("c_h2_in")
            pm_in = sem2("c_pm_in")
            bn_in = sem2("c_bn_in")
            g_out = sem2("c_g_out")
            h3_in = sem2("c_h3_in")
            e_in = sem2("c_e_in")
            e_out = sem2("c_e_out")
            mxp = sb2("mxp", [P, B * QUADS, QT])
            smp = sb2("smp", [P, B * QUADS, QT])
            block = s2.enter_context(nc.Block())

            @block.tensor
            def _(pe):
                ones = con["ones"]
                nc.tensor.matmul(tot_ps[:, 0, 0:3], ones, S["sum3"][:], start=True, stop=True).then_inc(summed, 1)
                pe.wait_ge(cov_in, 1)
                nc.tensor.matmul(tot_ps[:, 1, 0:6], ones, S["cov"][:], start=True, stop=True).then_inc(summed, 1)
                for n, (a, b, w, bank) in enumerate((("pm", "d2", C2, 2), ("pm3", "d3", 1, 3))):
                    pe.wait_ge(pm_in, 2 * n + 1)
                    nc.tensor.matmul(tot_ps[:, bank, 0:w], ones, S[a][:], start=True, stop=True).then_inc(summed, 1)
                    pe.wait_ge(pm_in, 2 * n + 2)
                    nc.tensor.matmul(tot_ps[:, bank, 8:8 + w], ones, S[b][:], start=True, stop=True).then_inc(summed, 1)

            @block.scalar
            def _(act):
                a = nc.scalar
                act.wait_ge(var_in, 1)
                a.activation(S["sd"][:], S["var"][:], ACT.Sqrt, bias=S["eps"][:]).then_inc(sd_out, 1)
                act.wait_ge(mat_in, 1)
                def first_term(n):
                    jj, hf = n % C1, n // C1
                    if n >= 2:
                        act.wait_ge(h_used, n - 1)
                    a.activation(th[:, n % 2, :], planes[:, 0, bass.ts(hf, HN)], ACT.Identity,
                                 scale=S["mat2"][:, jj, 0:1], bias=S["bb"][:, jj:jj + 1]).then_inc(t_out, 1)

                for hf in range(2):
                    for jj in range(C1):
                        first_term(hf * C1 + jj)
                    for i in range(C2):
                        act.wait_ge(h2_in, hf * C2 + i + 1)
                        a.copy(planes[:, i, bass.ts(hf, HN)], h2[:, i, :]).then_inc(w_out_, 1)
                act.wait_ge(var_in, 2)
                a.activation(S["sd2"][:], S["vv"][:], ACT.Sqrt, bias=S["eps"][:]).then_inc(sd_out, 1)
                act.wait_ge(bn_in, 1)
                for i in range(C2):
                    a.activation(planes[:, i, :], planes[:, i, :], ACT.Identity,
                                 scale=S["a2"][:, i:i + 1], bias=S["bb2"][:, i:i + 1]).then_inc(g_out, 1)
                act.wait_ge(var_in, 3)
                a.activation(S["sd3"][:], S["vv3"][:], ACT.Sqrt, bias=S["eps"][:]).then_inc(sd_out, 1)
                act.wait_ge(bn_in, 2)
                a.activation(planes[:, 0, :], planes[:, 0, :], ACT.Identity,
                             scale=S["a3"][:], bias=S["bb3"][:]).then_inc(g_out, 1)
                act.wait_ge(e_in, 1)
                a.activation(planes[:, 0, :], planes[:, 0, :], ACT.Exp).then_inc(e_out, 1)

            @block.vector
            def _(dve):
                v = nc.vector
                tick = Ticks(dve, vs)

                def do(ins):
                    tick(ins)
                    tick.settle()

                def over(ap, shape):
                    return ap.to_broadcast(shape)

                def inner(ap, w):
                    return ap.rearrange("p (n o) -> p n o", o=1).to_broadcast([P, ap.shape[1], w])

                A, Bm = w1b[:, :, 0, :], w1b[:, :, 1, :]
                do(v.tensor_reduce(S["rs"][:], Bm, AX.X, ALU.add))
                do(v.tensor_scalar(S["rs"][:], S["rs"][:], 1.0 / 3.0, None, ALU.mult))
                do(v.tensor_tensor(S["ab"][:], A, Bm, ALU.add))
                do(v.tensor_tensor(S["mat"][:], S["ab"][:], inner(S["rs"][:], 3), ALU.subtract))
                dve.wait_ge(summed, 1)
                do(v.tensor_scalar(S["mean"][:], tot_ps[:, 0, 0:3], 1.0 / PAIRS, None, ALU.mult))
                junk = th[:].rearrange("p a w -> p (a w)")
                order = [(0, 0), (0, 1), (0, 2), (1, 1), (1, 2), (2, 2)]
                for n, (i, k) in enumerate(order):
                    do(v.scalar_tensor_tensor(junk, planes[:, i, :], S["mean"][:, i:i + 1], planes[:, k, :],
                                              ALU.subtract, ALU.mult, accum_out=S["cov"][:, n:n + 1]))
                v.memset(S["tot"][:], 0.0).then_inc(cov_in, 1)
                dve.wait_ge(summed, 2)
                for n, (i, k) in enumerate(order):
                    do(v.tensor_scalar(S["covf"][:, i, k:k + 1], tot_ps[:, 1, n:n + 1], 1.0 / PAIRS, None, ALU.mult))
                    if i != k:
                        do(v.tensor_scalar(S["covf"][:, k, i:i + 1], tot_ps[:, 1, n:n + 1], 1.0 / PAIRS, None, ALU.mult))
                do(v.tensor_tensor(S["mm"][:], S["mat"][:], over(S["mean"][:].rearrange("p (o i) -> p o i", o=1), [P, C1, 3]), ALU.mult))
                do(v.tensor_reduce(S["mh"][:], S["mm"][:], AX.X, ALU.add))
                for k in range(3):
                    do(v.tensor_tensor(S["tri"][:, :, k, :], S["mat"][:],
                                       over(S["covf"][:, k, :].rearrange("p (o i) -> p o i", o=1), [P, C1, 3]), ALU.mult))
                do(v.tensor_reduce(S["tm"][:], S["tri"][:], AX.X, ALU.add))
                do(v.tensor_tensor(S["tv"][:], S["tm"][:], S["mat"][:], ALU.mult))
                do(v.tensor_reduce(S["var"][:], S["tv"][:], AX.X, ALU.add))
                do(v.tensor_scalar(S["var"][:], S["var"][:], 0.0, None, ALU.max))
                v.memset(S["tot"][:], 0.0).then_inc(var_in, 1)
                dve.wait_ge(sd_out, 1)
                do(v.reciprocal(S["a1"][:], S["sd"][:]))
                do(v.tensor_tensor(S["a1"][:], S["a1"][:], gb1[:, 0, :], ALU.mult))
                do(v.tensor_tensor(S["ma"][:], S["mh"][:], S["a1"][:], ALU.mult))
                do(v.tensor_tensor(S["bb"][:], gb1[:, 1, :], S["ma"][:], ALU.subtract))
                do(v.tensor_tensor(S["mat2"][:], S["mat"][:], inner(S["a1"][:], 3), ALU.mult))
                v.memset(S["tot"][:], 0.0).then_inc(mat_in, 1)
                n = 0
                for hf in range(2):
                    cols = bass.ts(hf, HN)

                    for jj in range(C1):
                        dve.wait_ge(t_out, n + 1)
                        t = th[:, n % 2, :]
                        for i in (1, 2):
                            do(v.scalar_tensor_tensor(t, planes[:, i, cols], S["mat2"][:, jj, i:i + 1], t, ALU.mult, ALU.add))
                        do(v.scalar_tensor_tensor(t, t, SLOPE, t, ALU.mult, ALU.max))
                        if jj == 0 and hf == 1:
                            dve.wait_ge(w_out_, C2)
                        for i in range(C2):
                            wij = w2b[:, i, jj:jj + 1]
                            if jj == 0:
                                ins = v.tensor_scalar(h2[:, i, :], t, wij, None, ALU.mult)
                            else:
                                ins = v.scalar_tensor_tensor(h2[:, i, :], t, wij, h2[:, i, :], ALU.mult, ALU.add)
                            if jj < C1 - 1:
                                tick(ins)
                            else:
                                ins.then_inc(h2_in, 1)
                        if jj < C1 - 1:
                            tick.settle()
                        else:
                            dve.wait_ge(h2_in, (hf + 1) * C2)
                        v.memset(S["tot"][:], 0.0).then_inc(h_used, 1)
                        n += 1

                def batch_norm(planes_n, mvx, pm, dv, d2, vv, sd, a, ma, bb, gb, at, base, bank, w):
                    for i in range(planes_n):
                        for s in range(NB):
                            tick(v.bn_stats(bst[:, i, s, :], planes[:, i, bass.ts(s, BN)]))
                    tick.settle()
                    for i in range(planes_n):
                        tick(v.bn_aggr(mvx[:, i, :], bst[:, i].rearrange("p s e -> p (s e)")))
                    tick.settle()
                    v.tensor_scalar(pm, mvx[:, :, 0], 1.0 / P, None, ALU.mult).then_inc(pm_in, 1)
                    dve.wait_ge(summed, base)
                    do(v.tensor_tensor(dv, mvx[:, :, 0], tot_ps[:, bank, 0:w], ALU.subtract))
                    do(v.tensor_tensor(d2, dv, dv, ALU.mult))
                    do(v.tensor_tensor(d2, d2, mvx[:, :, 1], ALU.add))
                    v.tensor_scalar(d2, d2, 1.0 / P, None, ALU.mult).then_inc(pm_in, 1)
                    dve.wait_ge(summed, base + 1)
                    v.tensor_copy(vv, tot_ps[:, bank, 8:8 + w]).then_inc(var_in, 1)
                    dve.wait_ge(sd_out, at)
                    do(v.reciprocal(a, sd))
                    do(v.tensor_tensor(a, a, gb[0], ALU.mult))
                    do(v.tensor_tensor(ma, tot_ps[:, bank, 0:w], a, ALU.mult))
                    v.tensor_tensor(bb, gb[1], ma, ALU.subtract).then_inc(bn_in, 1)

                dve.wait_ge(w_out_, 2 * C2)
                batch_norm(C2, S["mv2"][:], S["pm"][:], S["dv"][:], S["d2"][:], S["vv"][:], S["sd2"][:], S["a2"][:], S["ma2"][:],
                           S["bb2"][:], (gb2[:, 0, :], gb2[:, 1, :]), 2, 3, 2, C2)
                dve.wait_ge(g_out, 1)
                do(v.scalar_tensor_tensor(planes[:, 0, :], planes[:, 0, :], SLOPE, planes[:, 0, :], ALU.mult, ALU.max))
                do(v.tensor_scalar(planes[:, 0, :], planes[:, 0, :], w3b[:, 0:1], None, ALU.mult))
                for i in (1, 2):
                    dve.wait_ge(g_out, i + 1)
                    do(v.scalar_tensor_tensor(planes[:, i, :], planes[:, i, :], SLOPE, planes[:, i, :], ALU.mult, ALU.max))
                    do(v.scalar_tensor_tensor(planes[:, 0, :], planes[:, i, :], w3b[:, i:i + 1], planes[:, 0, :], ALU.mult, ALU.add))
                batch_norm(1, S["mv3"][:].rearrange("p (o s) -> p o s", o=1), S["pm3"][:], S["dv3"][:], S["d3"][:], S["vv3"][:], S["sd3"][:],
                           S["a3"][:], S["ma3"][:], S["bb3"][:], (gb3[:, 0:1], gb3[:, 1:2]), 3, 5, 3, 1)
                dve.wait_ge(g_out, C2 + 1)
                do(v.scalar_tensor_tensor(planes[:, 0, :], planes[:, 0, :], SLOPE, planes[:, 0, :], ALU.mult, ALU.max))
                m = B * QUADS
                att = planes[:, 0, :].rearrange("p (m k t) -> p m t k", m=m, t=QT)
                flat = planes[:, 0, :].rearrange("p (m k t) -> p m k t", m=m, t=QT)
                do(v.tensor_reduce(mxp[:], att, AX.X, ALU.max))
                v.tensor_tensor(flat, flat, mxp[:].rearrange("p m (o t) -> p m o t", o=1).to_broadcast([P, m, K, QT]),
                                ALU.subtract).then_inc(e_in, 1)
                dve.wait_ge(e_out, 1)
                do(v.tensor_reduce(smp[:], att, AX.X, ALU.add))
                do(v.reciprocal(smp[:], smp[:]))
                do(v.tensor_tensor(flat, flat, smp[:].rearrange("p m (o t) -> p m o t", o=1).to_broadcast([P, m, K, QT]), ALU.mult))


def stage_e(nc, con, planes, idx_all, stats_all, y_dram, out):
    NB = 16
    NGR = P // NB
    RING = 3
    with ExitStack() as st:
        def sb(name, shape, dt=F32):
            return st.enter_context(nc.sbuf_tensor(name, shape, dt))

        def sem(name):
            return st.enter_context(nc.semaphore(name))

        y_s = sb("e_y", [P, 2, T])
        x1 = sb("e_x1", [P, T])
        xT = sb("e_xT", [P, TILES, C])
        rstd = sb("e_rstd", [P, B])
        nmr = sb("e_nmr", [P, B])
        nrm = sb("e_nrm", [P, 2])
        epsc = sb("e_eps", [P, 1])
        dig16 = sb("e_dig16", [P, 2, BCOLS], U16)
        row3 = sb("e_row3", [P, 3, BCOLS])
        pr3 = sb("e_pr3", [P, 2, 3, P])
        hot = sb("e_hot", [P, P, HI])
        wgt = sb("e_wgt", [P, P, HI])
        spr = sb("e_spr", [P, P, QT, HI])
        oh = sb("e_oh", [P, RING, NB, LO])
        at = sb("e_at", [P, HI, QT, P])
        o_s = sb("e_o", [P, 2, HALF])
        tr_ps = st.enter_context(nc.psum_tensor("e_tr_ps", [P, 2, 512], F32))
        pr_ps = st.enter_context(nc.psum_tensor("e_pr_ps", [P, 3, P], F32))
        a_ps = [st.enter_context(nc.psum_tensor(f"e_a_ps{i}", [P, NB, QT, HI], F32)) for i in range(2)]
        o_ps = st.enter_context(nc.psum_tensor("e_o_ps", [P, HALF], F32))
        y_landed = [sem(f"e_y_landed{i}") for i in range(2)]
        ln_step = sem("e_ln_step")
        sd_ready = sem("e_sd_ready")
        norm_ready = sem("e_norm_ready")
        x1_ready = sem("e_x1_ready")
        x1_turned = sem("e_x1_turned")
        xT_ready = sem("e_xT_ready")
        digits_cut = sem("e_digits_cut")
        rows_ready = sem("e_rows_ready")
        pairs_turned = sem("e_pairs_turned")
        pairs_ready = sem("e_pairs_ready")
        hot_ready = sem("e_hot_ready")
        weighted = sem("e_weighted")
        spread_ready = sem("e_spread_ready")
        oh_ready = sem("e_oh_ready")
        a_ready = sem("e_a_ready")
        a_moved = sem("e_a_moved")
        o_ready = sem("e_o_ready")
        o_added = sem("e_o_added")
        e_sp_gates = sem("e_sp_gates")
        e_pool_gates = sem("e_pool_gates")
        stored = [sem(f"e_stored{i}") for i in range(2)]
        pp = slice(0, QCOLS)

        def batches(eng, emit):
            emit(0, 0, 0, True)
            emit(1, 0, 1, False)
            with eng.Fori(1, B // 2) as j:
                emit(j * 2, j, 0, False)
                emit(j * 2 + 1, j, 1, False)

        block = st.enter_context(nc.Block())

        @block.sync
        def _(sp):
            def emit(b, j, par, first):
                if not (isinstance(b, int) and b < 2):
                    gate(sp, x1_ready, b - 1, e_sp_gates)
                sp.dma_start(y_s[:, par, :], y_dram[b]).then_inc(y_landed[par], 16)
                if not first:
                    store(b - 1)

            def store(b):
                for q in range(QUADS):
                    gate(sp, o_added, b * QUADS + q + 1, e_sp_gates)
                    sp.dma_start(out[b][:, bass.ts(q, HALF)], o_s[:, q, :]).then_inc(stored[q], 16)

            batches(sp, emit)
            store(B - 1)
            for q in range(QUADS):
                sp.wait_ge(stored[q], 16 * B)

        @block.scalar
        def _(act):
            a = nc.scalar
            act.wait_ge(ln_step, 1)
            a.activation(rstd[:], stats_all[:, :, 1], ACT.Sqrt, bias=epsc[:]).then_inc(sd_ready, 1)

            def emit(b, j, par, first):
                act.wait_ge(y_landed[par], (j + 1) * 16)
                act.wait_ge(norm_ready, b + 1)
                if not first:
                    act.wait_ge(o_added, b * QUADS)
                a.activation(x1[:], y_s[:, par, :], ACT.Identity, scale=nrm[:, 0:1], bias=nrm[:, 1:2]).then_inc(x1_ready, 1)
                act.wait_ge(x1_turned, b + 1)
                a.copy(xT[:].rearrange("p t c -> p (t c)"), tr_ps[:].rearrange("p a b -> p (a b)")).then_inc(xT_ready, 1)
                for q in range(QUADS):
                    n = b * QUADS + q
                    act.wait_ge(pairs_turned, n + 1)
                    a.copy(pr3[pp, q], pr_ps[pp]).then_inc(pairs_ready, 1)
                    act.wait_ge(weighted, n + 1)
                    if not (first and q == 0):
                        act.wait_ge(a_ready, n * NGR)
                    for t in range(QT):
                        m = a.activation(spr[pp, :, t, :], wgt[pp], ACT.Copy, scale=con["tmask"][pp, t:t + 1])
                    m.then_inc(spread_ready, 1)
                    for g in range(NGR):
                        act.wait_ge(a_ready, n * NGR + g + 1)
                        if g == 0 and not (first and q == 0):
                            act.wait_ge(o_ready, n)
                        dst = at[:, :, :, bass.ts(g, NB)].rearrange("p e t n -> p n t e")
                        a.copy(dst, a_ps[g % 2][:]).then_inc(a_moved, 1)

            batches(act, emit)

        @block.gpsimd
        def _(pool):
            def emit(b, j, par, first):
                cols = bass.ds(b * BCOLS, BCOLS)
                pool.wait_ge(ln_step, 3)
                if not first:
                    pool.wait_ge(x1_ready, b)
                    gate(pool, pairs_turned, b * QUADS, e_pool_gates)
                nc.gpsimd.tensor_copy(nrm[:, 0:1], rstd[:, bass.ds(b, 1)])
                nc.gpsimd.tensor_copy(nrm[:, 1:2], nmr[:, bass.ds(b, 1)]).then_inc(norm_ready, 1)
                nc.gpsimd.tensor_copy(row3[:, 2, :], planes[:, 0, cols])
                gate(pool, digits_cut, b * 2 + 2, e_pool_gates)
                nc.gpsimd.tensor_copy(row3[:, 0:2, :], dig16[:]).then_inc(rows_ready, 1)
                for q in range(QUADS):
                    n = b * QUADS + q
                    pool.wait_ge(hot_ready, n + 1)
                    if not (first and q == 0):
                        pool.wait_ge(spread_ready, n)
                    att = pr3[pp, q, 2, :].rearrange("p (n o) -> p n o", o=1)
                    nc.gpsimd.tensor_tensor(wgt[pp], hot[pp], att.to_broadcast([QCOLS, P, HI]), ALU.mult).then_inc(weighted, 1)

            batches(pool, emit)

        @block.vector
        def _(dve):
            v = nc.vector
            v.memset(epsc[:], EPS).then_inc(ln_step, 1)
            dve.wait_ge(sd_ready, 1)
            v.reciprocal(rstd[:], rstd[:]).then_inc(ln_step, 1)
            dve.wait_ge(ln_step, 2)
            v.scalar_tensor_tensor(nmr[:], stats_all[:, :, 0], -1.0, rstd[:], ALU.mult, ALU.mult).then_inc(ln_step, 1)

            def cut(b, first):
                cols = bass.ds(b * BCOLS, BCOLS)
                if not first:
                    dve.wait_ge(rows_ready, b)
                v.tensor_scalar(dig16[:, 0, :], idx_all[:, cols], LO - 1, None, ALU.bitwise_and).then_inc(digits_cut, 1)
                v.tensor_scalar(dig16[:, 1, :], idx_all[:, cols], 7, None, ALU.logical_shift_right).then_inc(digits_cut, 1)

            def emit(b, j, par, first):
                cut(b, first)
                for q in range(QUADS):
                    n = b * QUADS + q
                    dve.wait_ge(pairs_ready, n + 1)
                    if not (first and q == 0):
                        dve.wait_ge(weighted, n)
                    high = pr3[pp, q, 1, :].rearrange("p (n o) -> p n o", o=1)
                    v.tensor_tensor(hot[pp], high.to_broadcast([QCOLS, P, HI]),
                                    con["hiiota"][pp].rearrange("p (o e) -> p o e", o=1).to_broadcast([QCOLS, P, HI]),
                                    ALU.is_equal).then_inc(hot_ready, 1)
                    for g in range(NGR):
                        gg = n * NGR + g
                        if not (first and q == 0 and g < 2):
                            dve.wait_ge(a_ready, gg - 1)
                        for i in range(NB):
                            at_n = g * NB + i
                            m = v.tensor_scalar(oh[pp, g % 2, i, :], con["iota"][pp], pr3[pp, q, 0, at_n:at_n + 1], None, ALU.is_equal)
                        m.then_inc(oh_ready, 1)
                    dve.wait_ge(o_ready, n + 1)
                    if not first:
                        dve.wait_ge(stored[q], b * 16)
                    v.tensor_tensor(o_s[:, q, :], o_ps[:], x1[:, bass.ts(q, HALF)], ALU.add).then_inc(o_added, 1)

            batches(dve, emit)

        @block.tensor
        def _(pe):
            def emit(b, j, par, first):
                pe.wait_ge(x1_ready, b + 1)
                if not first:
                    pe.wait_ge(xT_ready, b)
                for t in range(TILES):
                    m = nc.tensor.transpose(tr_ps[:, t // 4, bass.ts(t % 4, C)], x1[:, bass.ts(t, P)], con["ident"])
                m.then_inc(x1_turned, 1)
                pe.wait_ge(rows_ready, b + 1)
                for q in range(QUADS):
                    n = b * QUADS + q
                    if not (first and q == 0):
                        pe.wait_ge(pairs_ready, n)
                    for i in range(3):
                        m = nc.tensor.transpose(pr_ps[pp, i, :], row3[:, i, bass.ts(q, QCOLS)], con["ident"])
                    m.then_inc(pairs_turned, 1)
                    pe.wait_ge(spread_ready, n + 1)
                    for g in range(NGR):
                        gg = n * NGR + g
                        pe.wait_ge(oh_ready, gg + 1)
                        if not (first and q == 0 and g < 2):
                            pe.wait_ge(a_moved, gg - 1)
                        for i in range(NB):
                            m = nc.tensor.matmul(a_ps[g % 2][:, i].rearrange("p t e -> p (t e)"), oh[pp, g % 2, i, :],
                                                 spr[pp, g * NB + i].rearrange("p t e -> p (t e)"), start=True, stop=True)
                        m.then_inc(a_ready, 1)
                    pe.wait_ge(a_moved, (n + 1) * NGR)
                    if q == 0:
                        pe.wait_ge(xT_ready, b + 1)
                    if not (first and q == 0):
                        pe.wait_ge(o_added, n)
                    for e in range(HI):
                        m = nc.tensor.matmul(o_ps[:], xT[:, e, :], at[:, e].rearrange("p t n -> p (t n)"),
                                             start=(e == 0), stop=(e == HI - 1))
                    m.then_inc(o_ready, 1)

            batches(pe, emit)


_INS = ['x', 'ctx_4096', 'mask_Bx1x4096_ff1', 'L0_xattn_W_in', 'L0_xattn_b_in', 'L0_xattn_W_out', 'L0_xattn_b_out',
        'L1_xattn_W1', 'L1_xattn_g1', 'L1_xattn_b1', 'L1_xattn_W2', 'L1_xattn_g2', 'L1_xattn_b2', 'L1_xattn_W3',
        'L1_xattn_g3', 'L1_xattn_b3']


def kernel(**inputs):
    import numpy as _np
    import concourse.bacc as _bacc
    from concourse import mybir as _mybir
    from concourse.bass_utils import run_bass_kernel_spmd as _run

    nc = _bacc.Bacc("TRN2", target_bir_lowering=False, num_devices=1)
    arrays, args = {}, []
    for name in _INS + ["shape_constants"]:
        a = shape_constants() if name == "shape_constants" else _np.ascontiguousarray(inputs[name])
        arrays[f"in_{name}"] = a
        args.append(nc.dram_tensor(f"in_{name}", a.shape, _mybir.dt.from_np(a.dtype), kind="ExternalInput").ap())
    o = nc.dram_tensor("out_0", [B, C, T], _mybir.dt.float32, kind="ExternalOutput").ap()
    build(nc, *args, o)
    r = _run(nc, [arrays], core_ids=[0])
    return r.results[0]["out_0"]
```

```python
from contextlib import ExitStack

import numpy as np
import concourse.bass as bass
from concourse import mybir

ALU = mybir.AluOpType
ACT = mybir.ActivationFunctionType
AX = mybir.AxisListType
F32 = mybir.dt.float32
BF16 = mybir.dt.bfloat16
U16 = mybir.dt.uint16
I32 = mybir.dt.int32

B, C, T = 32, 128, 1024
P = 128
HEADS, CHUNK = 8, 64
DH = C // HEADS
NEG_MASK = -1.0e9
K = 30
EPS = 1e-5
TINY = 1e-20
TILES = T // P
QUADS = 2
QT = TILES // QUADS
KP = 32
RANKS = KP // 8
LO, HI = 128, T // 128
BITS = 8
KT = 16
PARTS = 3
GK = 5
GROUPS = K // GK
QCOLS = K * QT
BCOLS = QUADS * QCOLS
N = B * BCOLS
PAIRS = float(N * P)
HALF = T // 2
HCH = HALF // CHUNK
REMOVED = -3.0e38
PI = float(np.pi)
SIGN = -(1 << 31)
RING = 2
SLOPE = 0.2
DEN_FLOOR = 1e-11

_at = {}
_end = 0
for _name, _w in (("ident", P), ("ones", P), ("iota", LO), ("lobias", 1), ("bitval", BITS),
                  ("hival", HI), ("hiiota", HI), ("tmask", QT), ("negs", CHUNK), ("headmask", HEADS)):
    _at[_name] = (_end, _end + _w)
    _end += _w
NCONST = _end
NCODE = KT * LO


def shape_constants():
    c = np.zeros((P, NCONST + NCODE), np.float32)

    def put(name, a):
        c[:, _at[name][0]:_at[name][1]] = a

    lo = np.arange(LO)
    put("ident", np.eye(P))
    put("ones", 1.0)
    put("iota", lo[None, :])
    code = np.zeros((KT, BITS, KT, LO))
    for k in range(KT):
        for b in range(BITS - 1):
            code[k, b, k, :] = np.where((lo >> b) & 1, 1.0, -1.0) / 2.0 ** b
    c[:, NCONST:] = code.reshape(P, NCODE)
    put("lobias", (1.0 - np.array([bin(v).count("1") for v in lo]))[:, None])
    put("bitval", np.array([2.0 ** b if b < BITS - 1 else 0.0 for b in range(BITS)])[None, :])
    put("hival", (np.arange(HI) * LO)[None, :])
    put("hiiota", np.arange(HI)[None, :])
    put("tmask", (np.arange(P)[:, None] % QT == np.arange(QT)[None, :]))
    m = int(-NEG_MASK)
    parts = []
    for _ in range(3):
        e = max(m.bit_length() - 8, 0)
        parts.append((m >> e) << e)
        m -= parts[-1]
    assert m == 0
    put("negs", -np.repeat(np.array(parts + [0]) / 32.0, 32)[:, None])
    put("headmask", (np.arange(C)[:, None] // DH == np.arange(HEADS)[None, :]))
    return c


def gate(eng, sem, value, passed):
    eng.wait_ge(sem, value)
    eng.sem_inc(passed, 1)


class Ticks:

    def __init__(self, eng, sem, base=0):
        self.eng, self.sem, self.base, self.n = eng, sem, base, 0

    def __call__(self, ins):
        ins.then_inc(self.sem, 1)
        self.n += 1
        return ins

    def settle(self):
        self.eng.wait_ge(self.sem, self.base + self.n)


def build(nc, x, ctx, mask, w_in, b_in, w_out, b_out, w1, g1, b1, w2, g2, b2, w3, g3, b3, consts, out):
    y_dram = nc.dram_tensor("y_spill", [B, C, T], F32, kind="Internal").ap()
    with ExitStack() as whole:
        def held(name, shape, dt=F32):
            return whole.enter_context(nc.sbuf_tensor(name, shape, dt))

        cst = held("cst", [P, NCONST])
        con = {n: cst[:, a:b] for n, (a, b) in _at.items()}
        planes = held("planes", [P, 3, N])
        idx_all = held("idx_all", [P, N], U16)
        stats_all = held("stats_all", [P, B, 2])
        stage_a(nc, x, ctx, mask, w_in, b_in, w_out, b_out, consts, y_dram, cst, con, planes, idx_all, stats_all)
        stage_b(nc, con, planes, w1, g1, b1, w2, g2, b2, w3, g3, b3)
        stage_e(nc, con, planes, idx_all, stats_all, y_dram, out)


def stage_a(nc, x, ctx, mask, w_in, b_in, w_out, b_out, consts, y_dram, cst, con, planes, idx_all, stats_all):
    with ExitStack() as st:
        def sb(name, shape, dt=F32):
            return st.enter_context(nc.sbuf_tensor(name, shape, dt))

        def sem(name):
            return st.enter_context(nc.semaphore(name))

        wT = sb("wT", [P, 4, C])
        bias = sb("bias", [P, 4])
        qbias = sb("qbias", [P, 1])
        code = sb("code", [P, KT, LO], BF16)
        identb = sb("identb", [P, P], BF16)
        negs = sb("negs", [P, CHUNK], BF16)
        neghalf = sb("neghalf", [P, P])
        bitval = sb("bitval", [P, BITS], U16)
        hival = sb("hival", [P, HI], U16)
        ctx_s = sb("ctx_s", [P, 2, T])
        sq = sb("sq", [P, T])
        maskb = sb("maskb", [P, 2, T])
        minv = sb("minv", [P, 2, T], BF16)
        x_s = sb("x_s", [P, T])
        nxx = sb("nxx", [P, 2, TILES])
        table = sb("table", [P, 2, HI * 3])
        tparts = sb("tparts", [P, 2, PARTS, HI * 3], BF16)
        trest = sb("trest", [P, HI * 3])
        pd_sb = sb("pd_sb", [P, RING, T])
        vals = sb("vals", [P, RANKS, 8])
        idx16 = sb("idx16", [P, 2, TILES, KP], U16)
        bits16 = sb("bits16", [P, QT, KP, BITS], U16)
        bitsb = sb("bitsb", [P, QT, KP * BITS], BF16)
        hi16 = sb("hi16", [P, QT, KP], U16)
        hi1h = sb("hi1h", [P, QUADS, K * QT, HI], BF16)
        bitsT = sb("bitsT", [P, 2, QT * P], BF16)
        ohT = sb("ohT", [P, 2, QT * P], BF16)
        gsb = sb("gsb", [P, 2, GK * QT * HI * 3])
        gm = sb("gm", [P, GK * QT, HI * 3])
        g12 = sb("g12", [P, GK * QT, 12])
        g6 = sb("g6", [P, GK * QT, 6])
        g3c = sb("g3c", [P, GK, QT, 3])
        qs = sb("qs", [P, HALF])
        kt = sb("kt", [P, HALF])
        kz = sb("kz", [P, 2, 2, HEADS, CHUNK])
        vz = sb("vz", [P, 2, HCH, C])
        sS = sb("sS", [P, 2, HEADS, CHUNK])
        mx = sb("mx", [P, 2, HEADS])
        rs = sb("rs", [P, 2, HEADS])
        rr = sb("rr", [P, 2, HEADS])
        pT = sb("pT", [P, HEADS // 2, 2 * CHUNK])
        oT = sb("oT", [P, HALF])
        y_s = sb("y_s", [P, 2, HALF])
        bnst = sb("bnst", [P, 2, 6])
        mv = sb("mv", [P, 2])
        pd_ps = st.enter_context(nc.psum_tensor("pd_ps", [P, 2, HALF], F32))
        s_ps = st.enter_context(nc.psum_tensor("s_ps", [P, HEADS, CHUNK], F32))
        g_ps = st.enter_context(nc.psum_tensor("g_ps", [P, GK, QT, HI * 3 + 0], F32))
        oh_ps = [st.enter_context(nc.psum_tensor(f"oh_ps{i}", [P, QT * P], F32)) for i in range(2)]
        mi_ps = [st.enter_context(nc.psum_tensor(f"mi_ps{i}", [P, 512], F32)) for i in range(2)]
        w_in_landed = sem("w_in_landed")
        ctx_landed = [sem(f"ctx_landed{i}") for i in range(2)]
        mask_landed = [sem(f"mask_landed{i}") for i in range(2)]
        x_landed = sem("x_landed")
        y_stored = sem("y_stored")
        setup_done = sem("setup_done")
        act_setup = sem("act_setup")
        w_turned = sem("w_turned")
        dve_gates = sem("dve_gates")
        sp_gates = sem("sp_gates")
        pool_gates = sem("pool_gates")
        sq_ready = sem("sq_ready")
        minv_ready = sem("minv_ready")
        pd_ready = sem("pd_ready")
        pd_moved = sem("pd_moved")
        topk_done = sem("topk_done")
        topk_step = sem("topk_step")
        misc_ready = sem("misc_ready")
        misc_moved = sem("misc_moved")
        kz_ready = sem("kz_ready")
        s_ready = sem("s_ready")
        max_ready = sem("max_ready")
        shifted = sem("shifted")
        exp_ready = sem("exp_ready")
        sum_ready = sem("sum_ready")
        rcp_ready = sem("rcp_ready")
        probs_ready = sem("probs_ready")
        masked_y = sem("masked_y")
        y_ready = sem("y_ready")
        bn_step = sem("bn_step")
        mv_ready = sem("mv_ready")
        mv_kept = sem("mv_kept")
        bits_ready = sem("bits_ready")
        hi_cut = sem("hi_cut")
        hi_ready = sem("hi_ready")
        bitsb_ready = sem("bitsb_ready")
        idx_kept = sem("idx_kept")
        oh_ready = sem("oh_ready")
        oh_moved = sem("oh_moved")
        split_step = sem("split_step")
        g_ready = sem("g_ready")
        g_moved = sem("g_moved")
        pool_step = sem("pool_step")
        g_done = sem("g_done")

        code_in = pd_sb[:].rearrange("p r t -> p (r t)")[:, 0:NCODE]
        wnat = y_s[:].rearrange("p h t -> p (h t)")[:, 0:4 * C].rearrange("p (g c) -> p g c", g=4)
        wi = w_in.rearrange("(g o) c -> o g c", g=3)
        UNITS = QUADS * K
        NG = QUADS * GROUPS
        slot_groups = [(0,), (1, 2), (3, 4), (5,)]

        FILLS = 30

        def misc_base(b):
            return 5 if isinstance(b, int) and b == 0 else b * FILLS

        def first_bank(b):
            return 1 if isinstance(b, int) and b == 0 else 0

        TAIL = misc_base(B) - 5
        SPLITS = 4

        def batches(eng, emit):
            emit(0, 0, 0, True, False)
            emit(1, 0, 1, False, False)
            with eng.Fori(1, B // 2 - 1) as j:
                emit(j * 2, j, 0, False, False)
                emit(j * 2 + 1, j, 1, False, False)
            emit(B - 2, B // 2 - 1, 0, False, False)
            emit(B - 1, B // 2 - 1, 1, False, True)

        block = st.enter_context(nc.Block())

        @block.sync
        def _(sp):
            sp.dma_start(cst[:], consts[:, 0:NCONST]).then_inc(w_in_landed, 16)
            sp.dma_start(code_in, consts[:, NCONST:]).then_inc(w_in_landed, 16)
            sp.dma_start(wnat[:, 0:3, :], wi).then_inc(w_in_landed, 16)
            sp.dma_start(wnat[:, 3, :], w_out).then_inc(w_in_landed, 16)
            sp.dma_start(bias[:, 0:3], b_in.rearrange("(g o) -> o g", g=3), allow_slow_non_contiguous=True).then_inc(w_in_landed, 16)
            sp.dma_start(bias[:, 3:4], b_out.rearrange("(o g) -> o g", g=1), allow_slow_non_contiguous=True).then_inc(w_in_landed, 16)

            def load(b, par):
                sp.dma_start(ctx_s[:, par, :], ctx[b]).then_inc(ctx_landed[par], 16)
                sp.dma_start(maskb[:, par, :], mask[b].to_broadcast([P, T])).then_inc(mask_landed[par], 16)

            load(0, 0)

            def emit(b, j, par, first, last):
                if not last:
                    if not first:
                        gate(sp, y_ready, b * 2, sp_gates)
                        gate(sp, misc_ready, misc_base(b), sp_gates)
                    load(b + 1, 1 - par)
                if not first:
                    gate(sp, y_ready, b * 2, sp_gates)
                sp.dma_start(x_s[:], x[b]).then_inc(x_landed, 16)
                gate(sp, y_ready, b * 2 + 2, sp_gates)
                sp.dma_start(y_dram[b], y_s[:].rearrange("p h t -> p (h t)")).then_inc(y_stored, 16)

            batches(sp, emit)
            sp.wait_ge(y_stored, 16 * B)

        @block.tensor
        def _(pe):
            pe.wait_ge(w_in_landed, 96)
            for g in range(4):
                m = nc.tensor.transpose(mi_ps[0][:, g * C:(g + 1) * C], wnat[:, g, :], con["ident"])
            m.then_inc(w_turned, 1)
            pe.wait_ge(act_setup, 5)
            pe.wait_ge(setup_done, 4)

            class Misc:

                def __init__(self, base, bank):
                    self.base, self.bank, self.n = base, bank, 0

                def open(self):
                    if not (isinstance(self.base, int) and self.base + self.n < 2):
                        pe.wait_ge(misc_moved, self.base + self.n - 1)
                    return mi_ps[(self.bank + self.n) % 2]

                def close(self, ins):
                    ins.then_inc(misc_ready, 1)
                    self.n += 1
                    return self.base + self.n

            def norms(misc, b):
                pe.wait_ge(sq_ready, b + 1)
                ps = misc.open()
                for t in range(TILES):
                    m = nc.tensor.matmul(ps[:, t:t + 1], sq[:, bass.ts(t, P)], neghalf[:, 0:1], start=True, stop=True)
                misc.close(m)

            def coordinates(misc, par):
                ps = misc.open()
                for t in range(TILES):
                    m = nc.tensor.matmul(ps[:, 3 * t:3 * t + 3], ctx_s[:, par, bass.ts(t, P)], con["ident"][:, 0:3],
                                         start=True, stop=True)
                misc.close(m)

            def distances(b, par, t):
                s = b * TILES + t
                for h in range(2):
                    if not (isinstance(s, int) and s == 0):
                        pe.wait_ge(pd_moved, s * 2 + h - 1)
                    nc.tensor.matmul(pd_ps[:, h, :], ctx_s[:, par, bass.ts(t, P)], ctx_s[:, par, bass.ts(h, HALF)],
                                     start=True, stop=False)
                    nc.tensor.matmul(pd_ps[:, h, :], neghalf[:], sq[:, bass.ts(h, HALF)],
                                     start=False, stop=True).then_inc(pd_ready, 1)

            def project(misc, par, h):
                cols = bass.ts(h, HALF)
                for g in range(2):
                    misc.close(nc.tensor.matmul(misc.open()[:], wT[:, g, :], ctx_s[:, par, cols], start=True, stop=True))
                for v in range(2):
                    ps = misc.open()
                    for c in range(4):
                        at = h * HALF + (4 * v + c) * CHUNK
                        for a in range(2):
                            m = nc.tensor.matmul(ps[64 * a:64 * a + 64, c * C:(c + 1) * C],
                                                 ctx_s[:, par, at:at + CHUNK], wT[:, 2, :], start=True, stop=True)
                    misc.close(m)

            def scores(b, par, t):
                s = b * TILES + t
                if not (isinstance(s, int) and s == 0):
                    pe.wait_ge(shifted, s)
                pe.wait_ge(kz_ready, s + 1)
                if t == 0:
                    pe.wait_ge(minv_ready, b + 1)
                for e in range(2):
                    ch = 2 * (t % QT) + e
                    keys = minv[:, par, (2 * t + e) * CHUNK:(2 * t + e + 1) * CHUNK]
                    nc.tensor.matmul(s_ps[64 * e:64 * e + 64], negs[:],
                                     keys.rearrange("p (o k) -> p o k", o=1).to_broadcast([P, HEADS, CHUNK]),
                                     start=True, stop=False)
                    m = nc.tensor.matmul(s_ps[64 * e:64 * e + 64], qs[:, bass.ts(ch, CHUNK)], kz[:, t % 2, e],
                                         start=False, stop=True)
                m.then_inc(s_ready, 1)

            def values(misc, b, t):
                s = b * TILES + t
                ps = misc.open()
                pe.wait_ge(probs_ready, s + 1)
                for g in range(HEADS // 2):
                    m = nc.tensor.transpose(ps[:, bass.ts(g, P)],
                                            sS[:, t % 2, 2 * g:2 * g + 2, :].rearrange("p a k -> p (a k)"), con["ident"])
                turned = misc.close(m)
                ps = misc.open()
                pe.wait_ge(misc_moved, turned)
                for e in range(2):
                    for g in range(HEADS // 2):
                        m = nc.tensor.matmul(ps[32 * g:32 * g + 32, bass.ts(e, CHUNK)],
                                             vz[:, t // QT, 2 * (t % QT) + e, 32 * g:32 * g + 32],
                                             pT[:, g, bass.ts(e, CHUNK)], start=True, stop=True)
                return misc.close(m)

            def turn_bits(misc, b, q):
                pe.wait_ge(bitsb_ready, b * QUADS + q + 1)
                ps = misc.open()[:].bitcast(BF16)
                for kk in range(2):
                    for t in range(QT):
                        m = nc.tensor.transpose(ps[:, (kk * QT + t) * P:(kk * QT + t + 1) * P],
                                                bitsb[:, t, kk * P:(kk + 1) * P], identb[:])
                return misc.close(m)

            def gather(b, par, q, groups, turned):
                units = [(q, g * GK + k) for g in groups for k in range(GK)]

                def fill(i):
                    u = q * K + units[i][1]
                    gu = b * UNITS + u
                    if not (isinstance(gu, int) and gu < 2):
                        pe.wait_ge(oh_moved, gu - 1)
                    k = units[i][1]
                    nc.tensor.matmul(oh_ps[u % 2][:], code[:, k % KT, :], bitsT[:, k // KT, :],
                                     start=True, stop=True).then_inc(oh_ready, 1)

                pe.wait_ge(misc_moved, turned)
                pe.wait_ge(split_step, (b + 1) * SPLITS)
                fill(0)
                for i, (_, k) in enumerate(units):
                    if i + 1 < len(units):
                        fill(i + 1)
                    u = q * K + k
                    gu = b * UNITS + u
                    gg = b * NG + q * GROUPS + k // GK
                    if k % GK == 0 and not (isinstance(gg, int) and gg == 0):
                        pe.wait_ge(g_moved, gg)
                    pe.wait_ge(oh_moved, gu + 1)
                    for t in range(QT):
                        for part in range(PARTS):
                            m = nc.tensor.matmul(g_ps[:, k % GK, t, :], ohT[:, u % 2, bass.ts(t, P)], tparts[:, par, part, :],
                                                 start=(part == 0), stop=(part == PARTS - 1))
                    if k % GK == GK - 1:
                        m.then_inc(g_ready, 1)

            def emit(b, j, par, first, last):
                misc = Misc(misc_base(b), first_bank(b))
                turned = None
                for t in range(TILES):
                    h = t // QT
                    if t < TILES - 1:
                        distances(b, par, t + 1)
                    elif not last:
                        norms(misc, b + 1)
                        distances(b + 1, 1 - par, 0)
                    if t > 0:
                        moved = values(misc, b, t - 1)
                    elif not first:
                        moved = values(misc, b - 1, TILES - 1)
                    if t == 1:
                        coordinates(misc, par)
                    if t == QT or (t == 0 and not first):
                        rows(misc, moved)
                    if not first:
                        if t % QT == 0:
                            turned = turn_bits(misc, b - 1, h)
                        gather(b - 1, 1 - par, h, slot_groups[t % QT], turned)
                    if t == QT - 1:
                        project(misc, par, 1)
                    elif t == TILES - 1 and not last:
                        project(misc, 1 - par, 0)
                    if t < TILES - 1:
                        scores(b, par, t + 1)
                    elif not last:
                        scores(b + 1, 1 - par, 0)

            def rows(misc, moved):
                ps = misc.open()
                pe.wait_ge(misc_moved, moved)
                misc.close(nc.tensor.matmul(ps[:], wT[:, 3, :], oT[:], start=True, stop=True))

            misc0 = Misc(0, 0)
            norms(misc0, 0)
            distances(0, 0, 0)
            project(misc0, 0, 0)
            scores(0, 0, 0)
            batches(pe, emit)
            tail = Misc(TAIL, TAIL % 2)
            rows(tail, values(tail, B - 1, TILES - 1))
            for q in range(QUADS):
                turned = turn_bits(tail, B - 1, q)
                for groups in slot_groups:
                    gather(B - 1, 1, q, groups, turned)

        @block.scalar
        def _(act):
            def move(dst, src, scale=1.0, bias=0.0, func=ACT.Identity):
                return nc.scalar.activation(dst, src, func, scale=scale, bias=bias)

            act.wait_ge(w_in_landed, 96)
            move(code[:].rearrange("p a b -> p (a b)"), code_in).then_inc(act_setup, 1)
            move(identb[:], con["ident"]).then_inc(act_setup, 1)
            move(negs[:], con["negs"]).then_inc(act_setup, 1)
            move(qbias[:], bias[:, 0:1], scale=DH ** -0.5).then_inc(act_setup, 1)
            act.wait_ge(w_turned, 1)
            move(wT[:].rearrange("p a b -> p (a b)"), mi_ps[0][:]).then_inc(act_setup, 1)
            act.wait_ge(act_setup, 5)
            act.wait_ge(setup_done, 4)

            class Moves:

                def __init__(self, base, bank):
                    self.base, self.bank, self.n = base, bank, 0

                def next(self):
                    act.wait_ge(misc_ready, self.base + self.n + 1)
                    self.n += 1
                    return mi_ps[(self.bank + self.n - 1) % 2]

            def norms(mv_, par):
                move(nxx[:, par, :], mv_.next()[:, 0:TILES], scale=2.0).then_inc(misc_moved, 1)
                return mv_.base + mv_.n

            def coordinates(mv_, b, par):
                if not (isinstance(b, int) and b < 2):
                    act.wait_ge(g_done, (b - 1) * NG)
                move(table[:, par, :], mv_.next()[:, 0:3 * TILES]).then_inc(misc_moved, 1)

            def distances(b, par, t, ready=None):
                s = b * TILES + t
                if ready is not None:
                    act.wait_ge(misc_moved, ready)
                if not (isinstance(s, int) and s < RING):
                    act.wait_ge(topk_done, s - RING + 1)
                for h in range(2):
                    act.wait_ge(pd_ready, s * 2 + h + 1)
                    move(pd_sb[:, t % RING, bass.ts(h, HALF)], pd_ps[:, h, :], scale=2.0,
                         bias=nxx[:, par, t:t + 1]).then_inc(pd_moved, 1)

            def project(mv_, b, h):
                move(qs[:], mv_.next()[:], scale=DH ** -0.5, bias=qbias[:]).then_inc(misc_moved, 1)
                if not (isinstance(b, int) and b == 0 and h == 0):
                    act.wait_ge(kz_ready, b * TILES + h * QT)
                move(kt[:], mv_.next()[:], bias=bias[:, 1:2]).then_inc(misc_moved, 1)
                for v in range(2):
                    ps = mv_.next()[:].rearrange("p (m r) -> p m r", r=2 * DH)
                    for a in range(2):
                        zone = vz[64 * a:64 * a + 64, h, 4 * v:4 * v + 4, :].rearrange("p c (g r) -> p (c g) r", r=2 * DH)
                        m = nc.scalar.copy(zone[:, :, a * DH:(a + 1) * DH], ps[64 * a:64 * a + 64, :, a * DH:(a + 1) * DH])
                    m.then_inc(misc_moved, 1)

            def gather(b, groups, q):
                for g in groups:
                    for k in range(g * GK, (g + 1) * GK):
                        u = q * K + k
                        act.wait_ge(oh_ready, b * UNITS + u + 1)
                        move(ohT[:, u % 2, :], oh_ps[u % 2][:], bias=con["lobias"], func=ACT.Relu).then_inc(oh_moved, 1)
                    gi = q * GROUPS + g
                    gg = b * NG + gi
                    act.wait_ge(g_ready, gg + 1)
                    if not (isinstance(gg, int) and gg < 2):
                        act.wait_ge(g_done, gg - 1)
                    nc.scalar.copy(gsb[:, gi % 2, :], g_ps[:].rearrange("p k t c -> p (k t c)")).then_inc(g_moved, 1)

            def emit(b, j, par, first, last):
                mv_ = Moves(misc_base(b), first_bank(b))
                for t in range(TILES):
                    h = t // QT
                    s = b * TILES + t
                    if t < TILES - 1:
                        distances(b, par, t + 1)
                    elif not last:
                        ready = norms(mv_, 1 - par)
                        distances(b + 1, 1 - par, 0, ready)
                    if t > 0 or not first:
                        values(mv_, (t - 1) % TILES)
                    if t == 1:
                        coordinates(mv_, b, par)
                    if t == QT:
                        rows(mv_, b, 0)
                    elif t == 0 and not first:
                        rows(mv_, b - 1, 1)
                    if not first:
                        if t % QT == 0:
                            bits(mv_)
                        gather(b - 1, slot_groups[t % QT], h)
                    if t == QT - 1:
                        project(mv_, b, 1)
                    elif t == TILES - 1 and not last:
                        project(mv_, b + 1, 0)
                    act.wait_ge(shifted, s + 1)
                    flat = sS[:, t % 2].rearrange("p h k -> p (h k)")
                    nc.scalar.activation(flat, flat, ACT.Exp).then_inc(exp_ready, 1)

            def values(mv_, t):
                nc.scalar.copy(pT[:].rearrange("p g k -> p (g k)"), mv_.next()[:]).then_inc(misc_moved, 1)
                move(oT[:, bass.ts(t % QT, P)], mv_.next()[:, 0:P], bias=bias[:, 2:3]).then_inc(misc_moved, 1)

            def rows(mv_, b, h):
                ps = mv_.next()
                if h == 0 and not (isinstance(b, int) and b == 0):
                    act.wait_ge(y_stored, b * 16)
                move(y_s[:, h, :], ps[:], bias=bias[:, 3:4]).then_inc(misc_moved, 1)

            def bits(mv_):
                nc.scalar.copy(bitsT[:].rearrange("p a b -> p (a b)"), mv_.next()[:].bitcast(BF16)).then_inc(misc_moved, 1)

            mv0 = Moves(0, 0)
            ready = norms(mv0, 0)
            distances(0, 0, 0, ready)
            project(mv0, 0, 0)
            batches(act, emit)
            tail = Moves(TAIL, TAIL % 2)
            values(tail, TILES - 1)
            rows(tail, B - 1, 1)
            for q in range(QUADS):
                bits(tail)
                for groups in slot_groups:
                    gather(B - 1, groups, q)

        STEPS = TILES * 7

        @block.vector
        def _(dve):
            dve.wait_ge(w_in_landed, 96)
            nc.vector.tensor_scalar(neghalf[:], con["ones"], -0.5, None, ALU.mult).then_inc(setup_done, 1)
            nc.vector.tensor_copy(bitval[:], con["bitval"]).then_inc(setup_done, 1)
            nc.vector.tensor_copy(hival[:], con["hival"]).then_inc(setup_done, 1)
            nc.vector.memset(vz[:], 0.0).then_inc(setup_done, 1)
            dve.wait_ge(setup_done, 4)

            def invert(b, j, par):
                dve.wait_ge(mask_landed[par], (j + 1) * 16)
                nc.vector.tensor_scalar(minv[:, par, :], maskb[:, par, :], 0.0, None, ALU.is_le).then_inc(minv_ready, 1)

            def digits(b, par, q):
                n = b * QUADS + q
                if not (isinstance(n, int) and n == 0):
                    dve.wait_ge(bitsb_ready, n)
                    dve.wait_ge(hi_ready, n)
                if not (isinstance(b, int) and b == 0):
                    dve.wait_ge(g_done, b * NG - (QUADS - 1 - q) * GROUPS)
                dve.wait_ge(topk_done, (b + 1) * TILES)
                m = QT * KP
                flat = idx16[:, par, q * QT:(q + 1) * QT].rearrange("p t k -> p (t k)")
                nc.vector.tensor_tensor(bits16[:].rearrange("p t k e -> p (t k) e"),
                                        flat.rearrange("p (m o) -> p m o", o=1).to_broadcast([P, m, BITS]),
                                        bitval[:].rearrange("p (o e) -> p o e", o=1).to_broadcast([P, m, BITS]),
                                        ALU.bitwise_and).then_inc(bits_ready, 1)
                nc.vector.tensor_scalar(hi16[:].rearrange("p t k -> p (t k)"), flat, (HI - 1) * LO, None,
                                        ALU.bitwise_and).then_inc(hi_cut, 1)
                dve.wait_ge(hi_cut, n + 1)
                src = hi16[:, :, 0:K].rearrange("p t (k o) -> p k t o", o=1)
                nc.vector.tensor_tensor(hi1h[:, q].rearrange("p (k t) e -> p k t e", t=QT),
                                        src.to_broadcast([P, K, QT, HI]),
                                        hival[:].rearrange("p (o u e) -> p o u e", o=1, u=1).to_broadcast([P, K, QT, HI]),
                                        ALU.is_equal).then_inc(hi_ready, 1)

            def row_stats(b, h):
                dve.wait_ge(y_ready, b * 2 + h + 1)
                nc.vector.bn_stats(bnst[:, h, :], y_s[:, h, :]).then_inc(bn_step, 1)
                if h == 1:
                    if not (isinstance(b, int) and b == 0):
                        dve.wait_ge(mv_kept, b)
                    gate(dve, bn_step, b * 2 + 2, dve_gates)
                    nc.vector.bn_aggr(mv[:], bnst[:].rearrange("p h s -> p (h s)")).then_inc(mv_ready, 1)

            def emit(b, j, par, first, last):
                step = b * STEPS
                if not (isinstance(b, int) and b < 2):
                    dve.wait_ge(idx_kept, (b - 1) * QUADS)
                for t in range(TILES):
                    s = b * TILES + t
                    if t % QT == 0 and not first:
                        digits(b - 1, 1 - par, t // QT)
                    if t == 6:
                        row_stats(b, 0)
                    if t == 5:
                        if not last:
                            invert(b + 1, (b + 1) // 2 if isinstance(b, int) else (j if par == 0 else j + 1), 1 - par)
                    if t == 2 and not first:
                        row_stats(b - 1, 1)
                    gate(dve, pd_moved, s * 2 + 2, dve_gates)
                    work = pd_sb[:, t % RING, :]
                    for r in range(RANKS):
                        nc.vector.max(vals[:, r, :], work).then_inc(topk_step, 1)
                        step = step + 1
                        gate(dve, topk_step, step, dve_gates)
                        found = nc.vector.max_index(idx16[:, par, t, 8 * r:8 * r + 8], vals[:, r, :], work)
                        if r < RANKS - 1:
                            nc.vector.match_replace(work, vals[:, r, :], work, REMOVED).then_inc(topk_step, 1)
                            step = step + 1
                            gate(dve, topk_step, step, dve_gates)
                        else:
                            found.then_inc(topk_done, 1)
                        if r == 0:
                            dve.wait_ge(s_ready, s + 1)
                            nc.vector.tensor_reduce(mx[:, t % 2, :], s_ps[:], AX.X, ALU.max).then_inc(max_ready, 1)
                            dve.wait_ge(max_ready, s + 1)
                            nc.vector.tensor_tensor(sS[:, t % 2], s_ps[:],
                                                    mx[:, t % 2, :].rearrange("p (h o) -> p h o", o=1).to_broadcast([P, HEADS, CHUNK]),
                                                    ALU.subtract).then_inc(shifted, 1)
                    dve.wait_ge(exp_ready, s + 1)
                    nc.vector.tensor_reduce(rs[:, t % 2, :], sS[:, t % 2], AX.X, ALU.add).then_inc(sum_ready, 1)
                    dve.wait_ge(sum_ready, s + 1)
                    nc.vector.reciprocal(rr[:, t % 2, :], rs[:, t % 2, :]).then_inc(rcp_ready, 1)

            invert(0, 0, 0)
            batches(dve, emit)
            for q in range(QUADS):
                digits(B - 1, 1, q)
            row_stats(B - 1, 1)

        @block.gpsimd
        def _(pool):
            pool.wait_ge(w_in_landed, 96)

            def square(b, j, par):
                pool.wait_ge(ctx_landed[par], (j + 1) * 16)
                if not (isinstance(b, int) and b == 0):
                    pool.wait_ge(pd_ready, b * TILES * 2)
                nc.gpsimd.tensor_tensor(sq[:], ctx_s[:, par, :], ctx_s[:, par, :], ALU.mult).then_inc(sq_ready, 1)

            class Steps:
                def __init__(self, base):
                    self.base, self.n = base, 0

                def __call__(self, ins):
                    ins.then_inc(pool_step, 1)
                    self.n += 1
                    pool.wait_ge(pool_step, self.base + self.n)

            def gather(b, par, q, groups, steps):
                for g in groups:
                    gi = q * GROUPS + g
                    gg = b * NG + gi
                    pool.wait_ge(g_moved, gg + 1)
                    rows = GK * QT
                    hot = hi1h[:, q, g * rows:(g + 1) * rows, :].rearrange("p m (e o) -> p (m e) o", o=1)
                    steps(nc.gpsimd.tensor_tensor(gm[:].rearrange("p m (e c) -> p (m e) c", c=3),
                                                  gsb[:, gi % 2, :].rearrange("p (m c) -> p m c", c=3),
                                                  hot.to_broadcast([P, rows * HI, 3]), ALU.mult))
                    steps(nc.gpsimd.tensor_tensor(g12[:], gm[:, :, 0:12], gm[:, :, 12:24], ALU.add))
                    steps(nc.gpsimd.tensor_tensor(g6[:], g12[:, :, 0:6], g12[:, :, 6:12], ALU.add))
                    steps(nc.gpsimd.tensor_tensor(g3c[:].rearrange("p k t c -> p (k t) c"), g6[:, :, 0:3], g6[:, :, 3:6], ALU.add))
                    centre = table[:, par, q * QT * 3:(q + 1) * QT * 3].rearrange("p (o t c) -> p o t c", o=1, c=3)
                    at = b * BCOLS + q * QCOLS + g * rows
                    dst = planes[:, :, bass.ds(at, rows)].rearrange("p c (k t) -> p k t c", t=QT)
                    nc.gpsimd.tensor_tensor(dst, g3c[:], centre.to_broadcast([P, GK, QT, 3]),
                                            ALU.subtract).then_inc(g_done, 1)

            def split(b, par, moved):
                n = b * SPLITS
                parts, whole = tparts[:, par], table[:, par, :]
                gate(pool, misc_moved, moved, pool_gates)
                nc.gpsimd.tensor_copy(parts[:, 0, :], whole).then_inc(split_step, 1)
                pool.wait_ge(split_step, n + 1)
                nc.gpsimd.tensor_tensor(trest[:], whole, parts[:, 0, :], ALU.subtract).then_inc(split_step, 1)
                gate(pool, split_step, n + 2, pool_gates)
                nc.gpsimd.tensor_copy(parts[:, 1, :], trest[:]).then_inc(split_step, 1)
                pool.wait_ge(split_step, n + 3)
                nc.gpsimd.tensor_tensor(parts[:, 2, :], trest[:], parts[:, 1, :], ALU.subtract).then_inc(split_step, 1)

            GSTEPS = NG * 4

            def emit(b, j, par, first, last):
                steps = Steps((b - 1) * GSTEPS)
                for t in range(TILES):
                    h = t // QT
                    s = b * TILES + t
                    if t > 0 or not first:
                        normalise(s - 1, (t - 1) % TILES)
                    if t == QT:
                        rows(b, j, par, 0, misc_base(b) + (14 if first else 18))
                    elif t == 0 and not first:
                        rows(b - 1, (b - 1) // 2 if isinstance(b, int) else (j - 1 if par == 0 else j), 1 - par, 1, misc_base(b) + 3)
                    if t % QT == 0 and not first:
                        convert(b - 1, h)
                        if t == 0:
                            keep(b - 1, 1 - par)
                    if t == 2:
                        split(b, par, misc_base(b) + (3 if first else 7))
                    if t == 3 and not first:
                        gate(pool, mv_ready, b, pool_gates)
                        nc.gpsimd.tensor_copy(stats_all[:, bass.ds(b - 1, 1), :].rearrange("p b s -> p (b s)"),
                                              mv[:]).then_inc(mv_kept, 1)
                    if t % QT != QT - 1:
                        spread_keys(b, t + 1)
                    if t == TILES - 2 and not last:
                        square(b + 1, (b + 1) // 2 if isinstance(b, int) else (j if par == 0 else j + 1), 1 - par)
                    if not first:
                        gather(b - 1, 1 - par, h, slot_groups[t % QT], steps)
                    if t == QT - 1:
                        pool.wait_ge(misc_moved, misc_base(b) + (9 if first else 13))
                        spread_keys(b, t + 1)
                    elif t == TILES - 1 and not last:
                        pool.wait_ge(misc_moved, misc_base(b) + (23 if first else 28))
                        spread_keys(b + 1, 0)

            def normalise(s, t):
                pool.wait_ge(rcp_ready, s + 1)
                nc.gpsimd.tensor_tensor(sS[:, t % 2], sS[:, t % 2],
                                        rr[:, t % 2, :].rearrange("p (h o) -> p h o", o=1).to_broadcast([P, HEADS, CHUNK]),
                                        ALU.mult).then_inc(probs_ready, 1)

            def rows(b, j, par, h, moved):
                pool.wait_ge(misc_moved, moved)
                if h == 0:
                    pool.wait_ge(mask_landed[par], (j + 1) * 16)
                    pool.wait_ge(x_landed, b * 16 + 16)
                cols = bass.ts(h, HALF)
                nc.gpsimd.tensor_tensor(y_s[:, h, :], y_s[:, h, :], maskb[:, par, cols], ALU.mult).then_inc(masked_y, 1)
                pool.wait_ge(masked_y, b * 2 + h + 1)
                nc.gpsimd.tensor_tensor(y_s[:, h, :], y_s[:, h, :], x_s[:, cols], ALU.add).then_inc(y_ready, 1)

            def spread_keys(b, t):
                s = b * TILES + t
                if not (isinstance(s, int) and s < 2):
                    pool.wait_ge(s_ready, s - 1)
                c = t % QT
                src = kt[:, 2 * c * CHUNK:2 * (c + 1) * CHUNK].rearrange("p (e o k) -> p e o k", e=2, o=1)
                heads = con["headmask"].rearrange("p (o h u) -> p o h u", o=1, u=1)
                nc.gpsimd.tensor_tensor(kz[:, t % 2], src.to_broadcast([P, 2, HEADS, CHUNK]),
                                        heads.to_broadcast([P, 2, HEADS, CHUNK]), ALU.mult).then_inc(kz_ready, 1)

            def convert(b, q):
                n = b * QUADS + q
                gate(pool, bits_ready, n + 1, pool_gates)
                if not (isinstance(n, int) and n == 0):
                    gate(pool, oh_ready, n * K, pool_gates)
                nc.gpsimd.tensor_copy(bitsb[:].rearrange("p t m -> p (t m)"),
                                      bits16[:].rearrange("p t k e -> p (t k e)")).then_inc(bitsb_ready, 1)
                pool.wait_ge(hi_ready, n + 1)

            def keep(b, par):
                gate(pool, topk_done, (b + 1) * TILES, pool_gates)
                for q in range(QUADS):
                    dst = idx_all[:, bass.ds(b * BCOLS + q * QCOLS, QCOLS)].rearrange("p (k t) -> p k t", t=QT)
                    nc.gpsimd.tensor_copy(dst, idx16[:, par, q * QT:(q + 1) * QT, 0:K].rearrange("p t k -> p k t")).then_inc(idx_kept, 1)

            square(0, 0, 0)
            pool.wait_ge(misc_moved, 3)
            spread_keys(0, 0)
            batches(pool, emit)
            normalise(B * TILES - 1, TILES - 1)
            rows(B - 1, B // 2 - 1, 1, 1, TAIL + 3)
            keep(B - 1, 1)
            steps = Steps((B - 1) * GSTEPS)
            for q in range(QUADS):
                convert(B - 1, q)
                for groups in slot_groups:
                    gather(B - 1, 1, q, groups, steps)
            pool.wait_ge(mv_ready, B)
            nc.gpsimd.tensor_copy(stats_all[:, B - 1, :], mv[:]).then_inc(mv_kept, 1)
            pool.wait_ge(g_done, B * NG)
            pool.wait_ge(mv_kept, B)


def stage_b(nc, con, planes, w1, g1, b1, w2, g2, b2, w3, g3, b3):
    CH = 4
    W = N // CH
    C1, C2 = 6, 3
    HN = N // 2
    BN = 512
    NB = N // BN
    with ExitStack() as st:
        def sb(name, shape, dt=F32):
            return st.enter_context(nc.sbuf_tensor(name, shape, dt))

        def sem(name):
            return st.enter_context(nc.semaphore(name))

        w1b = sb("w1b", [P, C1, 2, 3])
        gb1 = sb("gb1", [P, 2, C1])
        w2b = sb("w2b", [P, C2, C1])
        gb2 = sb("gb2", [P, 2, C2])
        w3b = sb("w3b", [P, C2])
        gb3 = sb("gb3", [P, 2])
        small = {n: sb("sm_" + n, s) for n, s in dict(
            sum3=[P, 3], mean=[P, 3], cov=[P, 6], covf=[P, 3, 3], rs=[P, C1], mat=[P, C1, 3], ab=[P, C1, 3], mm=[P, C1, 3],
            mh=[P, C1], tri=[P, C1, 3, 3], tm=[P, C1, 3], tv=[P, C1, 3], var=[P, C1], sd=[P, C1], a1=[P, C1], ma=[P, C1],
            bb=[P, C1], mat2=[P, C1, 3], eps=[P, 1], mv2=[P, C2, 2], pm=[P, C2], dv=[P, C2], d2=[P, C2], vv=[P, C2],
            sd2=[P, C2], a2=[P, C2], ma2=[P, C2], bb2=[P, C2], mv3=[P, 2], pm3=[P, 1], dv3=[P, 1], d3=[P, 1], vv3=[P, 1],
            sd3=[P, 1], a3=[P, 1], ma3=[P, 1], bb3=[P, 1], ar2=[P, C2], am2=[P, C2], tot=[P, 8]).items()}
        loaded = sem("b_loaded")
        vstep = sem("b_vstep")
        astep = sem("b_astep")
        pstep = sem("b_pstep")
        tot_ps = st.enter_context(nc.psum_tensor("tot_ps", [P, 4, 512], F32))

        def bc(ap):
            return ap

        with ExitStack() as s1:
            def sb1(name, shape, dt=F32):
                return s1.enter_context(nc.sbuf_tensor(name, shape, dt))

            ab3 = sb1("ab3", [P, 3, W])
            two = sb1("two", [P, 2, W])
            root = sb1("root", [P, 2, W])
            mn = sb1("mn", [P, 2, W])
            mxx = sb1("mxx", [P, 2, W])
            block = s1.enter_context(nc.Block())

            @block.sync
            def _(sp):
                def spread(ap, n):
                    return ap.rearrange("(o n) -> o n", o=1).to_broadcast([P, n])
                sp.dma_start(w1b[:].rearrange("p a b c -> p (a b c)"),
                             spread(w1.rearrange("a b -> (a b)"), C1 * 6)).then_inc(loaded, 16)
                sp.dma_start(gb1[:, 0, :], spread(g1, C1)).then_inc(loaded, 16)
                sp.dma_start(gb1[:, 1, :], spread(b1, C1)).then_inc(loaded, 16)
                sp.dma_start(w2b[:].rearrange("p a b -> p (a b)"),
                             spread(w2.rearrange("a b -> (a b)"), C2 * C1)).then_inc(loaded, 16)
                sp.dma_start(gb2[:, 0, :], spread(g2, C2)).then_inc(loaded, 16)
                sp.dma_start(gb2[:, 1, :], spread(b2, C2)).then_inc(loaded, 16)
                sp.dma_start(w3b[:], spread(w3.rearrange("a b -> (a b)"), C2)).then_inc(loaded, 16)
                sp.dma_start(gb3[:, 0:1], spread(g3, 1)).then_inc(loaded, 16)
                sp.dma_start(gb3[:, 1:2], spread(b3, 1)).then_inc(loaded, 16)
                sp.wait_ge(loaded, 9 * 16)

            A_PER, V_PER = 6, 19

            @block.scalar
            def _(act):
                with act.Fori(0, CH) as c:
                    rel = planes[:, :, bass.ds(c * W, W)]
                    va = c * V_PER + 1
                    act.wait_ge(vstep, va)
                    nc.scalar.activation(ab3[:], rel, ACT.Square).then_inc(astep, 1)
                    act.wait_ge(vstep, va + 3)
                    nc.scalar.activation(root[:], mn[:], ACT.Sqrt).then_inc(astep, 1)
                    nc.scalar.activation(ab3[:], rel, ACT.Abs).then_inc(astep, 1)
                    act.wait_ge(vstep, va + 9)
                    nc.scalar.activation(mn[:], mn[:], ACT.Arctan).then_inc(astep, 1)
                    act.wait_ge(vstep, va + 12)
                    nc.scalar.activation(mn[:], mn[:], ACT.Abs).then_inc(astep, 1)
                    act.wait_ge(vstep, va + 14)
                    nc.scalar.activation(mn[:, 1, :], mxx[:, 1, :], ACT.Abs).then_inc(astep, 1)
                act.wait_ge(vstep, CH * V_PER + 1)
                for i in range(3):
                    nc.scalar.activation(planes[:, i, :], planes[:, i, :], ACT.Identity,
                                         accum_out=small["sum3"][:, i:i + 1]).then_inc(astep, 1)
                act.wait_ge(astep, CH * A_PER + 3)

            @block.vector
            def _(dve):
                v = nc.vector
                v.memset(small["eps"][:], EPS).then_inc(vstep, 1)
                with dve.Fori(0, CH) as c:
                    base, aa = c * V_PER + 1, c * A_PER
                    tick = Ticks(dve, vstep, base)
                    px = planes[:, 0, bass.ds(c * W, W)]
                    py = planes[:, 1, bass.ds(c * W, W)]
                    pz = planes[:, 2, bass.ds(c * W, W)]
                    dve.wait_ge(astep, aa + 1)
                    tick(v.tensor_tensor(two[:, 0, :], ab3[:, 0, :], ab3[:, 1, :], ALU.add))
                    tick.settle()
                    tick(v.tensor_tensor(two[:, 1, :], two[:, 0, :], ab3[:, 2, :], ALU.add))
                    tick.settle()
                    tick(v.tensor_scalar(mn[:], two[:], TINY, None, ALU.max))
                    dve.wait_ge(astep, aa + 3)
                    tick(v.tensor_tensor(mn[:, 0, :], ab3[:, 2, :], root[:, 0, :], ALU.min))
                    tick(v.tensor_tensor(mn[:, 1, :], ab3[:, 1, :], ab3[:, 0, :], ALU.min))
                    tick(v.tensor_tensor(mxx[:, 0, :], ab3[:, 2, :], root[:, 0, :], ALU.max))
                    tick(v.scalar_tensor_tensor(mxx[:, 1, :], ab3[:, 0, :], DEN_FLOOR, ab3[:, 1, :], ALU.max, ALU.max))
                    tick.settle()
                    tick(v.reciprocal(mxx[:], mxx[:]))
                    tick.settle()
                    tick(v.tensor_tensor(mn[:], mn[:], mxx[:], ALU.mult))
                    tick.settle()
                    tick(v.tensor_tensor(mxx[:, 0, :], ab3[:, 2, :], root[:, 0, :], ALU.is_gt))
                    tick(v.tensor_tensor(mxx[:, 1, :], ab3[:, 1, :], ab3[:, 0, :], ALU.is_gt))
                    tick.settle()
                    dve.wait_ge(astep, aa + 4)
                    tick(v.scalar_tensor_tensor(mn[:].rearrange("p a w -> p (a w)"), mxx[:].rearrange("p a w -> p (a w)"),
                                                PI / 2, mn[:].rearrange("p a w -> p (a w)"), ALU.mult, ALU.subtract))
                    tick.settle()
                    tick(v.tensor_scalar(mxx[:, 1, :], px, 0.0, PI, ALU.is_lt, ALU.mult))
                    dve.wait_ge(astep, aa + 5)
                    tick.settle()
                    tick(v.tensor_tensor(mxx[:, 1, :], mxx[:, 1, :], mn[:, 1, :], ALU.subtract))
                    tick(v.scalar_tensor_tensor(mn[:, 0, :].bitcast(I32), pz.bitcast(I32), SIGN, mn[:, 0, :].bitcast(I32),
                                                ALU.bitwise_and, ALU.bitwise_or))
                    dve.wait_ge(astep, aa + 6)
                    tick(v.scalar_tensor_tensor(mn[:, 1, :].bitcast(I32), py.bitcast(I32), SIGN, mn[:, 1, :].bitcast(I32),
                                                ALU.bitwise_and, ALU.bitwise_or))
                    tick.settle()
                    tick(v.scalar_tensor_tensor(py, two[:, 1, :], TINY, mn[:, 0, :], ALU.is_ge, ALU.mult))
                    tick(v.scalar_tensor_tensor(pz, two[:, 0, :], TINY, mn[:, 1, :], ALU.is_ge, ALU.mult))
                    tick(v.tensor_copy(px, root[:, 1, :]))
                    tick.settle()
                    assert tick.n == V_PER, tick.n

        with ExitStack() as s2:
            def sb2(name, shape, dt=F32):
                return s2.enter_context(nc.sbuf_tensor(name, shape, dt))

            def sem2(name):
                return s2.enter_context(nc.semaphore(name))

            th = sb2("th", [P, 2, HN])
            h2 = sb2("h2", [P, C2, HN])
            bst = sb2("bst", [P, C2, NB, 6])
            S = small
            vs = sem2("c_vstep")
            summed = sem2("c_summed")
            mean_in = sem2("c_mean_in")
            cov_in = sem2("c_cov_in")
            var_in = sem2("c_var_in")
            sd_out = sem2("c_sd_out")
            mat_in = sem2("c_mat_in")
            t_out = sem2("c_t_out")
            t_mixed = sem2("c_t_mixed")
            h_out = sem2("c_h_out")
            h_used = sem2("c_h_used")
            w_out_ = sem2("c_w_out")
            h2_in = sem2("c_h2_in")
            pm_in = sem2("c_pm_in")
            bn_in = sem2("c_bn_in")
            g_out = sem2("c_g_out")
            h3_in = sem2("c_h3_in")
            e_in = sem2("c_e_in")
            e_out = sem2("c_e_out")
            mxp = sb2("mxp", [P, B * QUADS, QT])
            smp = sb2("smp", [P, B * QUADS, QT])
            block = s2.enter_context(nc.Block())

            @block.tensor
            def _(pe):
                ones = con["ones"]
                nc.tensor.matmul(tot_ps[:, 0, 0:3], ones, S["sum3"][:], start=True, stop=True).then_inc(summed, 1)
                pe.wait_ge(cov_in, 1)
                nc.tensor.matmul(tot_ps[:, 1, 0:6], ones, S["cov"][:], start=True, stop=True).then_inc(summed, 1)
                for n, (a, b, w, bank) in enumerate((("pm", "d2", C2, 2), ("pm3", "d3", 1, 3))):
                    pe.wait_ge(pm_in, 2 * n + 1)
                    nc.tensor.matmul(tot_ps[:, bank, 0:w], ones, S[a][:], start=True, stop=True).then_inc(summed, 1)
                    pe.wait_ge(pm_in, 2 * n + 2)
                    nc.tensor.matmul(tot_ps[:, bank, 8:8 + w], ones, S[b][:], start=True, stop=True).then_inc(summed, 1)

            @block.scalar
            def _(act):
                a = nc.scalar
                act.wait_ge(var_in, 1)
                a.activation(S["sd"][:], S["var"][:], ACT.Sqrt, bias=S["eps"][:]).then_inc(sd_out, 1)
                act.wait_ge(mat_in, 1)
                def first_term(n):
                    jj, hf = n % C1, n // C1
                    if n >= 2:
                        act.wait_ge(h_used, n - 1)
                    a.activation(th[:, n % 2, :], planes[:, 0, bass.ts(hf, HN)], ACT.Identity,
                                 scale=S["mat2"][:, jj, 0:1], bias=S["bb"][:, jj:jj + 1]).then_inc(t_out, 1)

                for hf in range(2):
                    for jj in range(C1):
                        first_term(hf * C1 + jj)
                    for i in range(C2):
                        act.wait_ge(h2_in, hf * C2 + i + 1)
                        a.copy(planes[:, i, bass.ts(hf, HN)], h2[:, i, :]).then_inc(w_out_, 1)
                act.wait_ge(var_in, 2)
                a.activation(S["sd2"][:], S["vv"][:], ACT.Sqrt, bias=S["eps"][:]).then_inc(sd_out, 1)
                act.wait_ge(bn_in, 1)
                for i in range(C2):
                    a.activation(planes[:, i, :], planes[:, i, :], ACT.Identity,
                                 scale=S["a2"][:, i:i + 1], bias=S["bb2"][:, i:i + 1]).then_inc(g_out, 1)
                act.wait_ge(var_in, 3)
                a.activation(S["sd3"][:], S["vv3"][:], ACT.Sqrt, bias=S["eps"][:]).then_inc(sd_out, 1)
                act.wait_ge(bn_in, 2)
                a.activation(planes[:, 0, :], planes[:, 0, :], ACT.Identity,
                             scale=S["a3"][:], bias=S["bb3"][:]).then_inc(g_out, 1)
                act.wait_ge(e_in, 1)
                a.activation(planes[:, 0, :], planes[:, 0, :], ACT.Exp).then_inc(e_out, 1)

            @block.vector
            def _(dve):
                v = nc.vector
                tick = Ticks(dve, vs)

                def do(ins):
                    tick(ins)
                    tick.settle()

                def over(ap, shape):
                    return ap.to_broadcast(shape)

                def inner(ap, w):
                    return ap.rearrange("p (n o) -> p n o", o=1).to_broadcast([P, ap.shape[1], w])

                A, Bm = w1b[:, :, 0, :], w1b[:, :, 1, :]
                do(v.tensor_reduce(S["rs"][:], Bm, AX.X, ALU.add))
                do(v.tensor_scalar(S["rs"][:], S["rs"][:], 1.0 / 3.0, None, ALU.mult))
                do(v.tensor_tensor(S["ab"][:], A, Bm, ALU.add))
                do(v.tensor_tensor(S["mat"][:], S["ab"][:], inner(S["rs"][:], 3), ALU.subtract))
                dve.wait_ge(summed, 1)
                do(v.tensor_scalar(S["mean"][:], tot_ps[:, 0, 0:3], 1.0 / PAIRS, None, ALU.mult))
                junk = th[:].rearrange("p a w -> p (a w)")
                order = [(0, 0), (0, 1), (0, 2), (1, 1), (1, 2), (2, 2)]
                for n, (i, k) in enumerate(order):
                    do(v.scalar_tensor_tensor(junk, planes[:, i, :], S["mean"][:, i:i + 1], planes[:, k, :],
                                              ALU.subtract, ALU.mult, accum_out=S["cov"][:, n:n + 1]))
                v.memset(S["tot"][:], 0.0).then_inc(cov_in, 1)
                dve.wait_ge(summed, 2)
                for n, (i, k) in enumerate(order):
                    do(v.tensor_scalar(S["covf"][:, i, k:k + 1], tot_ps[:, 1, n:n + 1], 1.0 / PAIRS, None, ALU.mult))
                    if i != k:
                        do(v.tensor_scalar(S["covf"][:, k, i:i + 1], tot_ps[:, 1, n:n + 1], 1.0 / PAIRS, None, ALU.mult))
                do(v.tensor_tensor(S["mm"][:], S["mat"][:], over(S["mean"][:].rearrange("p (o i) -> p o i", o=1), [P, C1, 3]), ALU.mult))
                do(v.tensor_reduce(S["mh"][:], S["mm"][:], AX.X, ALU.add))
                for k in range(3):
                    do(v.tensor_tensor(S["tri"][:, :, k, :], S["mat"][:],
                                       over(S["covf"][:, k, :].rearrange("p (o i) -> p o i", o=1), [P, C1, 3]), ALU.mult))
                do(v.tensor_reduce(S["tm"][:], S["tri"][:], AX.X, ALU.add))
                do(v.tensor_tensor(S["tv"][:], S["tm"][:], S["mat"][:], ALU.mult))
                do(v.tensor_reduce(S["var"][:], S["tv"][:], AX.X, ALU.add))
                do(v.tensor_scalar(S["var"][:], S["var"][:], 0.0, None, ALU.max))
                v.memset(S["tot"][:], 0.0).then_inc(var_in, 1)
                dve.wait_ge(sd_out, 1)
                do(v.reciprocal(S["a1"][:], S["sd"][:]))
                do(v.tensor_tensor(S["a1"][:], S["a1"][:], gb1[:, 0, :], ALU.mult))
                do(v.tensor_tensor(S["ma"][:], S["mh"][:], S["a1"][:], ALU.mult))
                do(v.tensor_tensor(S["bb"][:], gb1[:, 1, :], S["ma"][:], ALU.subtract))
                do(v.tensor_tensor(S["mat2"][:], S["mat"][:], inner(S["a1"][:], 3), ALU.mult))
                v.memset(S["tot"][:], 0.0).then_inc(mat_in, 1)
                n = 0
                for hf in range(2):
                    cols = bass.ts(hf, HN)

                    for jj in range(C1):
                        dve.wait_ge(t_out, n + 1)
                        t = th[:, n % 2, :]
                        for i in (1, 2):
                            do(v.scalar_tensor_tensor(t, planes[:, i, cols], S["mat2"][:, jj, i:i + 1], t, ALU.mult, ALU.add))
                        do(v.scalar_tensor_tensor(t, t, SLOPE, t, ALU.mult, ALU.max))
                        if jj == 0 and hf == 1:
                            dve.wait_ge(w_out_, C2)
                        for i in range(C2):
                            wij = w2b[:, i, jj:jj + 1]
                            if jj == 0:
                                ins = v.tensor_scalar(h2[:, i, :], t, wij, None, ALU.mult)
                            else:
                                ins = v.scalar_tensor_tensor(h2[:, i, :], t, wij, h2[:, i, :], ALU.mult, ALU.add)
                            if jj < C1 - 1:
                                tick(ins)
                            else:
                                ins.then_inc(h2_in, 1)
                        if jj < C1 - 1:
                            tick.settle()
                        else:
                            dve.wait_ge(h2_in, (hf + 1) * C2)
                        v.memset(S["tot"][:], 0.0).then_inc(h_used, 1)
                        n += 1

                def batch_norm(planes_n, mvx, pm, dv, d2, vv, sd, a, ma, bb, gb, at, base, bank, w):
                    for i in range(planes_n):
                        for s in range(NB):
                            tick(v.bn_stats(bst[:, i, s, :], planes[:, i, bass.ts(s, BN)]))
                    tick.settle()
                    for i in range(planes_n):
                        tick(v.bn_aggr(mvx[:, i, :], bst[:, i].rearrange("p s e -> p (s e)")))
                    tick.settle()
                    v.tensor_scalar(pm, mvx[:, :, 0], 1.0 / P, None, ALU.mult).then_inc(pm_in, 1)
                    dve.wait_ge(summed, base)
                    do(v.tensor_tensor(dv, mvx[:, :, 0], tot_ps[:, bank, 0:w], ALU.subtract))
                    do(v.tensor_tensor(d2, dv, dv, ALU.mult))
                    do(v.tensor_tensor(d2, d2, mvx[:, :, 1], ALU.add))
                    v.tensor_scalar(d2, d2, 1.0 / P, None, ALU.mult).then_inc(pm_in, 1)
                    dve.wait_ge(summed, base + 1)
                    v.tensor_copy(vv, tot_ps[:, bank, 8:8 + w]).then_inc(var_in, 1)
                    dve.wait_ge(sd_out, at)
                    do(v.reciprocal(a, sd))
                    do(v.tensor_tensor(a, a, gb[0], ALU.mult))
                    do(v.tensor_tensor(ma, tot_ps[:, bank, 0:w], a, ALU.mult))
                    v.tensor_tensor(bb, gb[1], ma, ALU.subtract).then_inc(bn_in, 1)

                dve.wait_ge(w_out_, 2 * C2)
                batch_norm(C2, S["mv2"][:], S["pm"][:], S["dv"][:], S["d2"][:], S["vv"][:], S["sd2"][:], S["a2"][:], S["ma2"][:],
                           S["bb2"][:], (gb2[:, 0, :], gb2[:, 1, :]), 2, 3, 2, C2)
                dve.wait_ge(g_out, 1)
                do(v.scalar_tensor_tensor(planes[:, 0, :], planes[:, 0, :], SLOPE, planes[:, 0, :], ALU.mult, ALU.max))
                do(v.tensor_scalar(planes[:, 0, :], planes[:, 0, :], w3b[:, 0:1], None, ALU.mult))
                for i in (1, 2):
                    dve.wait_ge(g_out, i + 1)
                    do(v.scalar_tensor_tensor(planes[:, i, :], planes[:, i, :], SLOPE, planes[:, i, :], ALU.mult, ALU.max))
                    do(v.scalar_tensor_tensor(planes[:, 0, :], planes[:, i, :], w3b[:, i:i + 1], planes[:, 0, :], ALU.mult, ALU.add))
                batch_norm(1, S["mv3"][:].rearrange("p (o s) -> p o s", o=1), S["pm3"][:], S["dv3"][:], S["d3"][:], S["vv3"][:], S["sd3"][:],
                           S["a3"][:], S["ma3"][:], S["bb3"][:], (gb3[:, 0:1], gb3[:, 1:2]), 3, 5, 3, 1)
                dve.wait_ge(g_out, C2 + 1)
                do(v.scalar_tensor_tensor(planes[:, 0, :], planes[:, 0, :], SLOPE, planes[:, 0, :], ALU.mult, ALU.max))
                m = B * QUADS
                att = planes[:, 0, :].rearrange("p (m k t) -> p m t k", m=m, t=QT)
                flat = planes[:, 0, :].rearrange("p (m k t) -> p m k t", m=m, t=QT)
                do(v.tensor_reduce(mxp[:], att, AX.X, ALU.max))
                v.tensor_tensor(flat, flat, mxp[:].rearrange("p m (o t) -> p m o t", o=1).to_broadcast([P, m, K, QT]),
                                ALU.subtract).then_inc(e_in, 1)
                dve.wait_ge(e_out, 1)
                do(v.tensor_reduce(smp[:], att, AX.X, ALU.add))
                do(v.reciprocal(smp[:], smp[:]))
                do(v.tensor_tensor(flat, flat, smp[:].rearrange("p m (o t) -> p m o t", o=1).to_broadcast([P, m, K, QT]), ALU.mult))


def stage_e(nc, con, planes, idx_all, stats_all, y_dram, out):
    NB = 16
    NGR = P // NB
    RING = 4
    DIGITS = 2
    ROWS = DIGITS + PARTS
    with ExitStack() as st:
        def sb(name, shape, dt=F32):
            return st.enter_context(nc.sbuf_tensor(name, shape, dt))

        def sem(name):
            return st.enter_context(nc.semaphore(name))

        y_s = sb("e_y", [P, 2, T])
        x1 = sb("e_x1", [P, 2, T])
        xT = sb("e_xT", [P, 2, TILES, C])
        rstd = sb("e_rstd", [P, B])
        nmr = sb("e_nmr", [P, B])
        nrm = sb("e_nrm", [P, 2])
        epsc = sb("e_eps", [P, 1])
        iotab = sb("e_iotab", [P, LO], BF16)
        identb = sb("e_identb", [P, P], BF16)
        dig16 = sb("e_dig16", [P, DIGITS, BCOLS], U16)
        rest = sb("e_rest", [P, BCOLS])
        rowsb = sb("e_rowsb", [P, ROWS, BCOLS], BF16)
        pr_lo = sb("e_pr_lo", [P, 2, P])
        pr_hi = sb("e_pr_hi", [P, 2, 1 + PARTS, P], BF16)
        hot = sb("e_hot", [P, P, HI], BF16)
        wgt = sb("e_wgt", [P, PARTS, P, HI], BF16)
        oh = sb("e_oh", [P, RING, NB, LO], BF16)
        at = sb("e_at", [P, 2, HI, QT, P])
        o_s = sb("e_o", [P, 2, HALF])
        spr = [planes[:, 1 + i, :].bitcast(BF16)[:, 0:P * PARTS * QT * HI].rearrange("p (n a t e) -> p n a t e", a=PARTS, t=QT, e=HI)
               for i in range(2)]
        tr_ps = st.enter_context(nc.psum_tensor("e_tr_ps", [P, 2, 512], F32))
        pr_ps = st.enter_context(nc.psum_tensor("e_pr_ps", [P, 512], F32))
        pairs_ps = pr_ps[:].bitcast(BF16)[:, 0:ROWS * P].rearrange("p (r n) -> p r n", r=ROWS)
        a_ps = [st.enter_context(nc.psum_tensor(f"e_a_ps{i}", [P, NB, QT, HI], F32)) for i in range(2)]
        o_ps = [st.enter_context(nc.psum_tensor(f"e_o_ps{i}", [P, HALF], F32)) for i in range(2)]
        y_landed = [sem(f"e_y_landed{i}") for i in range(2)]
        ln_step = sem("e_ln_step")
        sd_ready = sem("e_sd_ready")
        norm_ready = sem("e_norm_ready")
        x1_ready = sem("e_x1_ready")
        x1_turned = sem("e_x1_turned")
        xT_ready = sem("e_xT_ready")
        digits_cut = sem("e_digits_cut")
        part_step = sem("e_part_step")
        rows_ready = sem("e_rows_ready")
        pairs_turned = sem("e_pairs_turned")
        pairs_ready = sem("e_pairs_ready")
        hot_ready = sem("e_hot_ready")
        weighted = sem("e_weighted")
        spread_first = sem("e_spread_first")
        spread_last = sem("e_spread_last")
        oh_ready = sem("e_oh_ready")
        a_ready = sem("e_a_ready")
        a_moved = sem("e_a_moved")
        o_ready = sem("e_o_ready")
        o_added = sem("e_o_added")
        e_sp_gates = sem("e_sp_gates")
        e_pool_gates = sem("e_pool_gates")
        stored = [sem(f"e_stored{i}") for i in range(2)]
        pp = slice(0, QCOLS)
        ROW_STEPS = 2

        def passed(value):
            return not isinstance(value, int) or value > 0

        def batches(eng, emit):
            emit(0, 0, 0, False)
            emit(1, 0, 1, False)
            with eng.Fori(1, B // 2 - 1) as j:
                emit(j * 2, j, 0, False)
                emit(j * 2 + 1, j, 1, False)
            emit(B - 2, B // 2 - 1, 0, False)
            emit(B - 1, B // 2 - 1, 1, True)

        block = st.enter_context(nc.Block())

        @block.sync
        def _(sp):
            def load(b, par):
                if passed(b - 1):
                    gate(sp, x1_ready, b - 1, e_sp_gates)
                sp.dma_start(y_s[:, par, :], y_dram[b]).then_inc(y_landed[par], 16)

            def store(b, q):
                gate(sp, o_added, b * QUADS + q + 1, e_sp_gates)
                sp.dma_start(out[b][:, bass.ts(q, HALF)], o_s[:, q, :]).then_inc(stored[q], 16)

            def emit(b, j, par, last):
                if not last:
                    load(b + 1, 1 - par)
                if passed(b):
                    store(b - 1, 1)
                store(b, 0)

            load(0, 0)
            batches(sp, emit)
            store(B - 1, 1)
            for q in range(QUADS):
                sp.wait_ge(stored[q], 16 * B)

        @block.scalar
        def _(act):
            a = nc.scalar
            act.wait_ge(ln_step, 1)
            a.activation(rstd[:], stats_all[:, :, 1], ACT.Sqrt, bias=epsc[:]).then_inc(sd_ready, 1)

            def normalise(b, j, par):
                act.wait_ge(y_landed[par], (j + 1) * 16)
                act.wait_ge(norm_ready, b + 1)
                if passed(b - 1):
                    act.wait_ge(o_added, (b - 1) * QUADS)
                a.activation(x1[:, par, :], y_s[:, par, :], ACT.Identity, scale=nrm[:, 0:1], bias=nrm[:, 1:2]).then_inc(x1_ready, 1)

            def turned_rows(b, par):
                act.wait_ge(x1_turned, b + 1)
                if passed(b - 1):
                    act.wait_ge(o_ready, (b - 1) * QUADS)
                a.copy(xT[:, par].rearrange("p t c -> p (t c)"), tr_ps[:].rearrange("p a b -> p (a b)")).then_inc(xT_ready, 1)

            def pairs(n, q):
                act.wait_ge(pairs_turned, n + 1)
                a.copy(pr_lo[pp, q], pairs_ps[pp, 0])
                a.copy(pr_hi[pp, q], pairs_ps[pp, 1:ROWS]).then_inc(pairs_ready, 1)

            def spread(n, q, tiles):
                act.wait_ge(weighted, n * PARTS + PARTS - 1)
                for t in tiles:
                    for part in range(PARTS - 1):
                        m = a.activation(spr[q][pp, :, part, t, :], wgt[pp, part], ACT.Copy, scale=con["tmask"][pp, t:t + 1])
                m.then_inc(spread_first, 1)

            def moved(n, q, g):
                act.wait_ge(a_ready, n * NGR + g + 1)
                if g == 0 and passed(n - 1):
                    act.wait_ge(o_ready, n - 1)
                dst = at[:, q, :, :, bass.ts(g, NB)].rearrange("p e t n -> p n t e")
                a.copy(dst, a_ps[g % 2][:]).then_inc(a_moved, 1)

            def emit(b, j, par, last):
                for q in range(QUADS):
                    n = b * QUADS + q
                    ahead = not (last and q == QUADS - 1)
                    if ahead:
                        pairs(n + 1, 1 - q)
                    if q == QUADS - 1 and not last:
                        normalise(b + 1, j if par == 0 else j + 1, 1 - par)
                    for g in range(NGR):
                        moved(n, q, g)
                        if g == 3 and q == QUADS - 1 and not last:
                            turned_rows(b + 1, 1 - par)
                        if g >= NGR - QT and ahead:
                            spread(n + 1, 1 - q, (g - NGR + QT,))

            normalise(0, 0, 0)
            pairs(0, 0)
            turned_rows(0, 0)
            for t in range(QT):
                spread(0, 0, (t,))
            batches(act, emit)

        @block.gpsimd
        def _(pool):
            v = nc.gpsimd

            def norm(b):
                if passed(b):
                    gate(pool, x1_ready, b, e_pool_gates)
                v.tensor_copy(nrm[:, 0:1], rstd[:, bass.ds(b, 1)])
                v.tensor_copy(nrm[:, 1:2], nmr[:, bass.ds(b, 1)]).then_inc(norm_ready, 1)

            def rows(b):
                whole = planes[:, 0, bass.ds(b * BCOLS, BCOLS)]
                n = b * (PARTS - 1) + b
                if passed(b):
                    gate(pool, pairs_turned, b * QUADS, e_pool_gates)
                v.tensor_copy(rowsb[:, DIGITS, :], whole).then_inc(part_step, 1)
                gate(pool, part_step, n + 1, e_pool_gates)
                v.tensor_tensor(rest[:], whole, rowsb[:, DIGITS, :], ALU.subtract).then_inc(part_step, 1)
                gate(pool, part_step, n + 2, e_pool_gates)
                v.tensor_copy(rowsb[:, DIGITS + 1, :], rest[:]).then_inc(part_step, 1)
                pool.wait_ge(part_step, n + 3)
                v.tensor_tensor(rowsb[:, DIGITS + 2, :], rest[:], rowsb[:, DIGITS + 1, :], ALU.subtract).then_inc(rows_ready, 1)
                gate(pool, digits_cut, (b + 1) * DIGITS, e_pool_gates)
                v.tensor_copy(rowsb[:, 0:DIGITS, :], dig16[:]).then_inc(rows_ready, 1)

            def weigh(n, q):
                pool.wait_ge(hot_ready, n + 1)
                if passed(n):
                    pool.wait_ge(spread_first, n * QT)
                    pool.wait_ge(spread_last, n)
                for part in range(PARTS):
                    att = pr_hi[pp, q, 1 + part, :].rearrange("p (n o) -> p n o", o=1)
                    v.tensor_tensor(wgt[pp, part], hot[pp], att.to_broadcast([QCOLS, P, HI]), ALU.mult).then_inc(weighted, 1)

            def emit(b, j, par, last):
                for q in range(QUADS):
                    if not (last and q == QUADS - 1):
                        weigh(b * QUADS + q + 1, 1 - q)
                    if q == 0 and not last:
                        norm(b + 1)
                        rows(b + 1)

            pool.wait_ge(ln_step, 5)
            norm(0)
            rows(0)
            weigh(0, 0)
            batches(pool, emit)

        @block.vector
        def _(dve):
            v = nc.vector
            v.memset(epsc[:], EPS).then_inc(ln_step, 1)
            v.tensor_copy(iotab[:], con["iota"]).then_inc(ln_step, 1)
            v.tensor_copy(identb[:], con["ident"]).then_inc(ln_step, 1)
            dve.wait_ge(sd_ready, 1)
            v.reciprocal(rstd[:], rstd[:]).then_inc(ln_step, 1)
            dve.wait_ge(ln_step, 4)
            v.scalar_tensor_tensor(nmr[:], stats_all[:, :, 0], -1.0, rstd[:], ALU.mult, ALU.mult).then_inc(ln_step, 1)

            def cut(b):
                cols = bass.ds(b * BCOLS, BCOLS)
                if passed(b):
                    dve.wait_ge(rows_ready, b * ROW_STEPS)
                v.tensor_scalar(dig16[:, 0, :], idx_all[:, cols], LO - 1, None, ALU.bitwise_and).then_inc(digits_cut, 1)
                v.tensor_scalar(dig16[:, 1, :], idx_all[:, cols], 7, None, ALU.logical_shift_right).then_inc(digits_cut, 1)

            def heat(n, q):
                dve.wait_ge(pairs_ready, n + 1)
                if passed(n):
                    dve.wait_ge(weighted, n * PARTS)
                high = pr_hi[pp, q, 0, :].rearrange("p (n o) -> p n o", o=1)
                v.tensor_tensor(hot[pp], high.to_broadcast([QCOLS, P, HI]),
                                con["hiiota"][pp].rearrange("p (o e) -> p o e", o=1).to_broadcast([QCOLS, P, HI]),
                                ALU.is_equal).then_inc(hot_ready, 1)

            def spread(n, q):
                dve.wait_ge(weighted, (n + 1) * PARTS)
                for t in range(QT):
                    m = v.tensor_scalar(spr[q][pp, :, PARTS - 1, t, :], wgt[pp, PARTS - 1], con["tmask"][pp, t:t + 1], None, ALU.mult)
                m.then_inc(spread_last, 1)

            def add(n, b, q, par):
                dve.wait_ge(o_ready, n + 1)
                if passed(b):
                    dve.wait_ge(stored[q], b * 16)
                v.tensor_tensor(o_s[:, q, :], o_ps[q][:], x1[:, par, bass.ts(q, HALF)], ALU.add).then_inc(o_added, 1)

            def emit(b, j, par, last):
                for q in range(QUADS):
                    n = b * QUADS + q
                    if q == 0 and not last:
                        cut(b + 1)
                    dve.wait_ge(pairs_ready, n + 1)
                    for g in range(NGR):
                        gg = n * NGR + g
                        if passed(gg - RING + 1):
                            dve.wait_ge(a_ready, gg - RING + 1)
                        for i in range(NB):
                            at_n = g * NB + i
                            m = v.tensor_scalar(oh[pp, g % RING, i, :], iotab[pp], pr_lo[pp, q, at_n:at_n + 1], None, ALU.is_equal)
                        m.then_inc(oh_ready, 1)
                        if g == 4 and passed(n):
                            add(n - 1, b if q == 1 else b - 1, 1 - q, par if q == 1 else 1 - par)
                        if g == 0 and not (last and q == QUADS - 1):
                            heat(n + 1, 1 - q)
                        if g == 5 and not (last and q == QUADS - 1):
                            spread(n + 1, 1 - q)

            cut(0)
            heat(0, 0)
            spread(0, 0)
            batches(dve, emit)
            add(B * QUADS - 1, B - 1, 1, 1)

        @block.tensor
        def _(pe):
            def turn_pairs(n, q, b):
                pe.wait_ge(rows_ready, (b + 1) * ROW_STEPS)
                if passed(n):
                    pe.wait_ge(pairs_ready, n)
                for r in range(ROWS):
                    m = nc.tensor.transpose(pairs_ps[pp, r], rowsb[:, r, bass.ts(q, QCOLS)], identb[:])
                m.then_inc(pairs_turned, 1)

            def turn_rows(b, par):
                pe.wait_ge(x1_ready, b + 1)
                if passed(b):
                    pe.wait_ge(xT_ready, b)
                for t in range(TILES):
                    m = nc.tensor.transpose(tr_ps[:, t // 4, bass.ts(t % 4, C)], x1[:, par, bass.ts(t, P)], con["ident"])
                m.then_inc(x1_turned, 1)

            def attend(n, q, g):
                gg = n * NGR + g
                pe.wait_ge(oh_ready, gg + 1)
                if passed(gg - 1):
                    pe.wait_ge(a_moved, gg - 1)
                for i in range(NB):
                    for part in range(PARTS):
                        m = nc.tensor.matmul(a_ps[g % 2][:, i].rearrange("p t e -> p (t e)"), oh[pp, g % RING, i, :],
                                             spr[q][pp, g * NB + i, part].rearrange("p t e -> p (t e)"),
                                             start=(part == 0), stop=(part == PARTS - 1))
                m.then_inc(a_ready, 1)

            def gathered(n, q, b, par):
                pe.wait_ge(a_moved, (n + 1) * NGR)
                pe.wait_ge(xT_ready, b + 1)
                if passed(n - 1):
                    pe.wait_ge(o_added, n - 1)
                for e in range(HI):
                    m = nc.tensor.matmul(o_ps[q][:], xT[:, par, e, :], at[:, q, e].rearrange("p t n -> p (t n)"),
                                         start=(e == 0), stop=(e == HI - 1))
                m.then_inc(o_ready, 1)

            def emit(b, j, par, last):
                for q in range(QUADS):
                    n = b * QUADS + q
                    if not (last and q == QUADS - 1):
                        turn_pairs(n + 1, 1 - q, b + q)
                    pe.wait_ge(spread_first, (n + 1) * QT)
                    pe.wait_ge(spread_last, n + 1)
                    for g in range(NGR):
                        attend(n, q, g)
                        if g == 1:
                            if passed(n):
                                gathered(n - 1, 1 - q, b if q == 1 else b - 1, par if q == 1 else 1 - par)
                            if q == QUADS - 1 and not last:
                                turn_rows(b + 1, 1 - par)

            pe.wait_ge(ln_step, 3)
            turn_rows(0, 0)
            turn_pairs(0, 0, 0)
            batches(pe, emit)
            gathered(B * QUADS - 1, 1, B - 1, 1)


_INS = ['x', 'ctx_4096', 'mask_Bx1x4096_ff1', 'L0_xattn_W_in', 'L0_xattn_b_in', 'L0_xattn_W_out', 'L0_xattn_b_out',
        'L1_xattn_W1', 'L1_xattn_g1', 'L1_xattn_b1', 'L1_xattn_W2', 'L1_xattn_g2', 'L1_xattn_b2', 'L1_xattn_W3',
        'L1_xattn_g3', 'L1_xattn_b3']


def kernel(**inputs):
    import numpy as _np
    import concourse.bacc as _bacc
    from concourse import mybir as _mybir
    from concourse.bass_utils import run_bass_kernel_spmd as _run

    nc = _bacc.Bacc("TRN2", target_bir_lowering=False, num_devices=1)
    arrays, args = {}, []
    for name in _INS + ["shape_constants"]:
        a = shape_constants() if name == "shape_constants" else _np.ascontiguousarray(inputs[name])
        arrays[f"in_{name}"] = a
        args.append(nc.dram_tensor(f"in_{name}", a.shape, _mybir.dt.from_np(a.dtype), kind="ExternalInput").ap())
    o = nc.dram_tensor("out_0", [B, C, T], _mybir.dt.float32, kind="ExternalOutput").ap()
    build(nc, *args, o)
    r = _run(nc, [arrays], core_ids=[0])
    return r.results[0]["out_0"]
```

```python
from contextlib import ExitStack

import numpy as np
import concourse.bass as bass
from concourse import mybir

ALU = mybir.AluOpType
ACT = mybir.ActivationFunctionType
AX = mybir.AxisListType
F32 = mybir.dt.float32
BF16 = mybir.dt.bfloat16
U16 = mybir.dt.uint16
I32 = mybir.dt.int32

B, C, T = 32, 128, 1024
P = 128
HEADS, CHUNK = 8, 64
DH = C // HEADS
NEG_MASK = -1.0e9
K = 30
EPS = 1e-5
TINY = 1e-20
TILES = T // P
QUADS = 2
QT = TILES // QUADS
KP = 32
RANKS = KP // 8
LO, HI = 128, T // 128
BITS = 8
KT = 16
PARTS = 3
GK = 5
GROUPS = K // GK
QCOLS = K * QT
BCOLS = QUADS * QCOLS
N = B * BCOLS
PAIRS = float(N * P)
HALF = T // 2
HCH = HALF // CHUNK
REMOVED = -3.0e38
PI = float(np.pi)
SIGN = -(1 << 31)
RING = 4
SLOPE = 0.2
DEN_FLOOR = 1e-11

_at = {}
_end = 0
for _name, _w in (("ident", P), ("ones", P), ("iota", LO), ("lobias", 1), ("bitval", BITS),
                  ("hival", HI), ("hiiota", HI), ("tmask", QT), ("negs", CHUNK), ("headmask", HEADS)):
    _at[_name] = (_end, _end + _w)
    _end += _w
NCONST = _end
NCODE = KT * LO


def shape_constants():
    c = np.zeros((P, NCONST + NCODE), np.float32)

    def put(name, a):
        c[:, _at[name][0]:_at[name][1]] = a

    lo = np.arange(LO)
    put("ident", np.eye(P))
    put("ones", 1.0)
    put("iota", lo[None, :])
    code = np.zeros((KT, BITS, KT, LO))
    for k in range(KT):
        for b in range(BITS - 1):
            code[k, b, k, :] = np.where((lo >> b) & 1, 1.0, -1.0) / 2.0 ** b
    c[:, NCONST:] = code.reshape(P, NCODE)
    put("lobias", (1.0 - np.array([bin(v).count("1") for v in lo]))[:, None])
    put("bitval", np.array([2.0 ** b if b < BITS - 1 else 0.0 for b in range(BITS)])[None, :])
    put("hival", (np.arange(HI) * LO)[None, :])
    put("hiiota", np.arange(HI)[None, :])
    put("tmask", (np.arange(P)[:, None] % QT == np.arange(QT)[None, :]))
    m = int(-NEG_MASK)
    parts = []
    for _ in range(3):
        e = max(m.bit_length() - 8, 0)
        parts.append((m >> e) << e)
        m -= parts[-1]
    assert m == 0
    put("negs", -np.repeat(np.array(parts + [0]) / 32.0, 32)[:, None])
    put("headmask", (np.arange(C)[:, None] // DH == np.arange(HEADS)[None, :]))
    return c


def gate(eng, sem, value, passed):
    eng.wait_ge(sem, value)
    eng.sem_inc(passed, 1)


class Ticks:

    def __init__(self, eng, sem, base=0):
        self.eng, self.sem, self.base, self.n = eng, sem, base, 0

    def __call__(self, ins):
        ins.then_inc(self.sem, 1)
        self.n += 1
        return ins

    def settle(self):
        self.eng.wait_ge(self.sem, self.base + self.n)


def build(nc, x, ctx, mask, w_in, b_in, w_out, b_out, w1, g1, b1, w2, g2, b2, w3, g3, b3, consts, out):
    y_dram = nc.dram_tensor("y_spill", [B, C, T], F32, kind="Internal").ap()
    with ExitStack() as whole:
        def held(name, shape, dt=F32):
            return whole.enter_context(nc.sbuf_tensor(name, shape, dt))

        cst = held("cst", [P, NCONST])
        con = {n: cst[:, a:b] for n, (a, b) in _at.items()}
        planes = held("planes", [P, 3, N])
        idx_all = held("idx_all", [P, N], U16)
        stats_all = held("stats_all", [P, B, 2])
        stage_a(nc, x, ctx, mask, w_in, b_in, w_out, b_out, consts, y_dram, cst, con, planes, idx_all, stats_all)
        stage_b(nc, con, planes, w1, g1, b1, w2, g2, b2, w3, g3, b3)
        stage_e(nc, con, planes, idx_all, stats_all, y_dram, out)


def stage_a(nc, x, ctx, mask, w_in, b_in, w_out, b_out, consts, y_dram, cst, con, planes, idx_all, stats_all):
    with ExitStack() as st:
        def sb(name, shape, dt=F32):
            return st.enter_context(nc.sbuf_tensor(name, shape, dt))

        def sem(name):
            return st.enter_context(nc.semaphore(name))

        wT = sb("wT", [P, 4, C])
        bias = sb("bias", [P, 4])
        qbias = sb("qbias", [P, 1])
        code = sb("code", [P, KT, LO], BF16)
        identb = sb("identb", [P, P], BF16)
        negs = sb("negs", [P, CHUNK], BF16)
        neghalf = sb("neghalf", [P, P])
        bitval = sb("bitval", [P, BITS], U16)
        hival = sb("hival", [P, HI], U16)
        ctx_s = sb("ctx_s", [P, 2, T])
        sq = sb("sq", [P, T])
        maskb = sb("maskb", [P, 2, T])
        minv = sb("minv", [P, 2, T], BF16)
        x_s = sb("x_s", [P, T])
        nxx = sb("nxx", [P, 2, TILES])
        table = sb("table", [P, 2, HI * 3])
        tparts = sb("tparts", [P, 2, PARTS, HI * 3], BF16)
        trest = sb("trest", [P, HI * 3])
        pd_sb = sb("pd_sb", [P, RING, T])
        vals = sb("vals", [P, 2, 8])
        idx16 = sb("idx16", [P, 2, TILES, KP], U16)
        bits16 = sb("bits16", [P, QT, KP, BITS], U16)
        bitsb = sb("bitsb", [P, QT, KP * BITS], BF16)
        hi16 = sb("hi16", [P, QT, KP], U16)
        hi1h = sb("hi1h", [P, QUADS, K * QT, HI], BF16)
        bitsT = sb("bitsT", [P, 2, QT * P], BF16)
        ohT = sb("ohT", [P, 2, QT * P], BF16)
        gsb = sb("gsb", [P, 2, GK * QT * HI * 3])
        qs = sb("qs", [P, HALF])
        kt = sb("kt", [P, HALF])
        kz = sb("kz", [P, 2, 2, HEADS, CHUNK])
        vz = sb("vz", [P, 2, HCH, C])
        sS = sb("sS", [P, 2, HEADS, CHUNK])
        mx = sb("mx", [P, 2, HEADS])
        rs = sb("rs", [P, 2, HEADS])
        pT = sb("pT", [P, HEADS // 2, 2 * CHUNK])
        oT = sb("oT", [P, HALF])
        y_s = sb("y_s", [P, 2, HALF])
        bnst = sb("bnst", [P, 2, 6])
        mv = sb("mv", [P, 2])
        pd_ps = st.enter_context(nc.psum_tensor("pd_ps", [P, 2, HALF], F32))
        s_ps = st.enter_context(nc.psum_tensor("s_ps", [P, HEADS, CHUNK], F32))
        g_ps = st.enter_context(nc.psum_tensor("g_ps", [P, GK, QT, HI * 3 + 0], F32))
        oh_ps = [st.enter_context(nc.psum_tensor(f"oh_ps{i}", [P, QT * P], F32)) for i in range(2)]
        mi_ps = [st.enter_context(nc.psum_tensor(f"mi_ps{i}", [P, 512], F32)) for i in range(2)]
        w_in_landed = sem("w_in_landed")
        ctx_landed = [sem(f"ctx_landed{i}") for i in range(2)]
        mask_landed = [sem(f"mask_landed{i}") for i in range(2)]
        x_landed = sem("x_landed")
        y_stored = sem("y_stored")
        setup_done = sem("setup_done")
        act_setup = sem("act_setup")
        w_turned = sem("w_turned")
        dve_gates = sem("dve_gates")
        sp_gates = sem("sp_gates")
        pool_gates = sem("pool_gates")
        sq_ready = sem("sq_ready")
        minv_ready = sem("minv_ready")
        pd_ready = sem("pd_ready")
        pd_moved = sem("pd_moved")
        topk_done = sem("topk_done")
        topk_step = sem("topk_step")
        misc_ready = sem("misc_ready")
        misc_moved = sem("misc_moved")
        kz_ready = sem("kz_ready")
        s_ready = sem("s_ready")
        max_ready = sem("max_ready")
        exp_ready = sem("exp_ready")
        rcp_ready = sem("rcp_ready")
        probs_ready = sem("probs_ready")
        masked_y = sem("masked_y")
        y_ready = sem("y_ready")
        bn_step = sem("bn_step")
        mv_ready = sem("mv_ready")
        mv_kept = sem("mv_kept")
        bits_ready = sem("bits_ready")
        hi_cut = sem("hi_cut")
        hi_ready = sem("hi_ready")
        bitsb_ready = sem("bitsb_ready")
        idx_kept = sem("idx_kept")
        oh_ready = sem("oh_ready")
        oh_moved = sem("oh_moved")
        split_step = sem("split_step")
        g_ready = sem("g_ready")
        g_moved = sem("g_moved")
        pool_step = sem("pool_step")
        g_done = sem("g_done")

        code_in = pd_sb[:].rearrange("p r t -> p (r t)")[:, 0:NCODE]
        wnat = y_s[:].rearrange("p h t -> p (h t)")[:, 0:4 * C].rearrange("p (g c) -> p g c", g=4)
        wi = w_in.rearrange("(g o) c -> o g c", g=3)
        UNITS = QUADS * K
        NG = QUADS * GROUPS
        unit_starts = (0, 4, 15, 21)
        slot_groups = [(4, 5), (0,), (1, 2), (3,)]

        FILLS = 30

        def misc_base(b):
            return 5 if isinstance(b, int) and b == 0 else b * FILLS

        def first_bank(b):
            return 1 if isinstance(b, int) and b == 0 else 0

        TAIL = misc_base(B) - 5
        SPLITS = 4

        def batches(eng, emit):
            emit(0, 0, 0, True, False)
            emit(1, 0, 1, False, False)
            with eng.Fori(1, B // 2 - 1) as j:
                emit(j * 2, j, 0, False, False)
                emit(j * 2 + 1, j, 1, False, False)
            emit(B - 2, B // 2 - 1, 0, False, False)
            emit(B - 1, B // 2 - 1, 1, False, True)

        block = st.enter_context(nc.Block())

        @block.sync
        def _(sp):
            sp.dma_start(cst[:], consts[:, 0:NCONST]).then_inc(w_in_landed, 16)
            sp.dma_start(code_in, consts[:, NCONST:]).then_inc(w_in_landed, 16)
            sp.dma_start(wnat[:, 0:3, :], wi).then_inc(w_in_landed, 16)
            sp.dma_start(wnat[:, 3, :], w_out).then_inc(w_in_landed, 16)
            sp.dma_start(bias[:, 0:3], b_in.rearrange("(g o) -> o g", g=3), allow_slow_non_contiguous=True).then_inc(w_in_landed, 16)
            sp.dma_start(bias[:, 3:4], b_out.rearrange("(o g) -> o g", g=1), allow_slow_non_contiguous=True).then_inc(w_in_landed, 16)

            def load(b, par):
                sp.dma_start(ctx_s[:, par, :], ctx[b]).then_inc(ctx_landed[par], 16)
                sp.dma_start(maskb[:, par, :], mask[b].to_broadcast([P, T])).then_inc(mask_landed[par], 16)

            load(0, 0)

            def emit(b, j, par, first, last):
                if not last:
                    if not first:
                        gate(sp, y_ready, b * 2, sp_gates)
                        gate(sp, misc_ready, misc_base(b), sp_gates)
                    load(b + 1, 1 - par)
                if not first:
                    gate(sp, y_ready, b * 2, sp_gates)
                sp.dma_start(x_s[:], x[b]).then_inc(x_landed, 16)
                gate(sp, y_ready, b * 2 + 2, sp_gates)
                sp.dma_start(y_dram[b], y_s[:].rearrange("p h t -> p (h t)")).then_inc(y_stored, 16)

            batches(sp, emit)
            sp.wait_ge(y_stored, 16 * B)

        @block.tensor
        def _(pe):
            pe.wait_ge(w_in_landed, 96)
            for g in range(4):
                m = nc.tensor.transpose(mi_ps[0][:, g * C:(g + 1) * C], wnat[:, g, :], con["ident"])
            m.then_inc(w_turned, 1)
            pe.wait_ge(act_setup, 5)
            pe.wait_ge(setup_done, 4)

            class Misc:

                def __init__(self, base, bank):
                    self.base, self.bank, self.n = base, bank, 0

                def open(self):
                    if not (isinstance(self.base, int) and self.base + self.n < 2):
                        pe.wait_ge(misc_moved, self.base + self.n - 1)
                    return mi_ps[(self.bank + self.n) % 2]

                def close(self, ins):
                    ins.then_inc(misc_ready, 1)
                    self.n += 1
                    return self.base + self.n

            def norms(misc, b):
                pe.wait_ge(sq_ready, b + 1)
                ps = misc.open()
                for t in range(TILES):
                    m = nc.tensor.matmul(ps[:, t:t + 1], sq[:, bass.ts(t, P)], neghalf[:, 0:1], start=True, stop=True)
                misc.close(m)

            def coordinates(misc, par):
                ps = misc.open()
                for t in range(TILES):
                    m = nc.tensor.matmul(ps[:, 3 * t:3 * t + 3], ctx_s[:, par, bass.ts(t, P)], con["ident"][:, 0:3],
                                         start=True, stop=True)
                misc.close(m)

            def distances(b, par, t, h):
                n = (b * TILES + t) * 2 + h
                if not (isinstance(n, int) and n < 2):
                    pe.wait_ge(pd_moved, n - 1)
                nc.tensor.matmul(pd_ps[:, h, :], ctx_s[:, par, bass.ts(t, P)], ctx_s[:, par, bass.ts(h, HALF)],
                                 start=True, stop=False)
                nc.tensor.matmul(pd_ps[:, h, :], neghalf[:], sq[:, bass.ts(h, HALF)],
                                 start=False, stop=True).then_inc(pd_ready, 1)

            def queries_keys(misc, par, h):
                cols = bass.ts(h, HALF)
                for g in range(2):
                    misc.close(nc.tensor.matmul(misc.open()[:], wT[:, g, :], ctx_s[:, par, cols], start=True, stop=True))

            def project_values(misc, par, h):
                for v in range(2):
                    ps = misc.open()
                    for c in range(4):
                        at = h * HALF + (4 * v + c) * CHUNK
                        for a in range(2):
                            m = nc.tensor.matmul(ps[64 * a:64 * a + 64, c * C:(c + 1) * C],
                                                 ctx_s[:, par, at:at + CHUNK], wT[:, 2, :], start=True, stop=True)
                    misc.close(m)

            def scores(b, par, t):
                s = b * TILES + t
                if not (isinstance(s, int) and s == 0):
                    pe.wait_ge(exp_ready, s)
                pe.wait_ge(kz_ready, s + 1)
                if t == 0:
                    pe.wait_ge(minv_ready, b + 1)
                for e in range(2):
                    ch = 2 * (t % QT) + e
                    keys = minv[:, par, (2 * t + e) * CHUNK:(2 * t + e + 1) * CHUNK]
                    nc.tensor.matmul(s_ps[64 * e:64 * e + 64], negs[:],
                                     keys.rearrange("p (o k) -> p o k", o=1).to_broadcast([P, HEADS, CHUNK]),
                                     start=True, stop=False)
                    m = nc.tensor.matmul(s_ps[64 * e:64 * e + 64], qs[:, bass.ts(ch, CHUNK)], kz[:, t % 2, e],
                                         start=False, stop=True)
                m.then_inc(s_ready, 1)

            def turn_probs(misc, b, t):
                ps = misc.open()
                pe.wait_ge(probs_ready, b * TILES + t + 1)
                for g in range(HEADS // 2):
                    m = nc.tensor.transpose(ps[:, bass.ts(g, P)],
                                            sS[:, t % 2, 2 * g:2 * g + 2, :].rearrange("p a k -> p (a k)"), con["ident"])
                return misc.close(m)

            def values(misc, t, turned):
                ps = misc.open()
                pe.wait_ge(misc_moved, turned)
                for e in range(2):
                    for g in range(HEADS // 2):
                        m = nc.tensor.matmul(ps[32 * g:32 * g + 32, bass.ts(e, CHUNK)],
                                             vz[:, t // QT, 2 * (t % QT) + e, 32 * g:32 * g + 32],
                                             pT[:, g, bass.ts(e, CHUNK)], start=True, stop=True)
                return misc.close(m)

            def turn_bits(misc, b, q):
                pe.wait_ge(bitsb_ready, b * QUADS + q + 1)
                ps = misc.open()[:].bitcast(BF16)
                for kk in range(2):
                    for t in range(QT):
                        m = nc.tensor.transpose(ps[:, (kk * QT + t) * P:(kk * QT + t + 1) * P],
                                                bitsb[:, t, kk * P:(kk + 1) * P], identb[:])
                return misc.close(m)

            def gather(b, par, q, lo, hi, turned):

                def fill(k):
                    gu = b * UNITS + q * K + k
                    if not (isinstance(gu, int) and gu < 2):
                        pe.wait_ge(oh_moved, gu - 1)
                    nc.tensor.matmul(oh_ps[k % 2][:], code[:, k % KT, :], bitsT[:, k // KT, :],
                                     start=True, stop=True).then_inc(oh_ready, 1)

                if lo == 0:
                    pe.wait_ge(misc_moved, turned)
                    pe.wait_ge(split_step, (b + 1) * SPLITS)
                    fill(0)
                for k in range(lo, hi):
                    if k + 1 < K:
                        fill(k + 1)
                    gu = b * UNITS + q * K + k
                    gg = b * NG + q * GROUPS + k // GK
                    if k % GK == 0 and not (isinstance(gg, int) and gg == 0):
                        pe.wait_ge(g_moved, gg)
                    pe.wait_ge(oh_moved, gu + 1)
                    for t in range(QT):
                        for part in range(PARTS):
                            m = nc.tensor.matmul(g_ps[:, k % GK, t, :], ohT[:, k % 2, bass.ts(t, P)], tparts[:, par, part, :],
                                                 start=(part == 0), stop=(part == PARTS - 1))
                    if k % GK == GK - 1:
                        m.then_inc(g_ready, 1)

            def emit(b, j, par, first, last):
                misc = Misc(misc_base(b), first_bank(b))
                turned = None
                for t in range(TILES):
                    h, quarter = divmod(t, QT)
                    at = unit_starts[quarter]

                    def units(n):
                        nonlocal at
                        if not first:
                            gather(b - 1, 1 - par, h, at, at + n, turned)
                        at += n

                    def ahead(i, half):
                        if t + i < TILES:
                            distances(b, par, t + i, half)
                        elif not last:
                            distances(b + 1, 1 - par, t + i - TILES, half)

                    before = t > 0 or not first
                    nb, npar, nh = (b, par, 1) if h == 0 else (b + 1, 1 - par, 0)
                    ongoing = h == 0 or not last

                    def probs():
                        return turn_probs(misc, b if t > 0 else b - 1, (t - 1) % TILES) if before else None

                    if quarter % 2 == 0:
                        if quarter == 0 and not first:
                            turned = turn_bits(misc, b - 1, h)
                        if t == TILES - 2 and not last:
                            norms(misc, b + 1)
                        ahead(2, 0)
                        probs_in = probs()
                        ahead(2, 1)
                        scores(b, par, t + 1)
                        units(1)
                        ahead(3, 0)
                        if before:
                            moved = values(misc, (t - 1) % TILES, probs_in)
                        units(1)
                        ahead(3, 1)
                        if quarter == 0:
                            if before:
                                rows(misc, moved)
                            units(2)
                        else:
                            if ongoing:
                                queries_keys(misc, npar, nh)
                            units(4)
                    elif quarter == 1:
                        probs_in = probs()
                        units(1)
                        scores(b, par, t + 1)
                        units(2)
                        moved = values(misc, t - 1, probs_in)
                        if t == 1:
                            coordinates(misc, par)
                        units(8)
                    else:
                        probs_in = probs()
                        if ongoing:
                            scores(nb, npar, (t + 1) % TILES)
                        units(2)
                        moved = values(misc, t - 1, probs_in)
                        units(2)
                        if ongoing:
                            project_values(misc, npar, nh)
                        units(5)

            def rows(misc, moved):
                ps = misc.open()
                pe.wait_ge(misc_moved, moved)
                misc.close(nc.tensor.matmul(ps[:], wT[:, 3, :], oT[:], start=True, stop=True))

            misc0 = Misc(0, 0)
            norms(misc0, 0)
            for t in range(2):
                for h in range(2):
                    distances(0, 0, t, h)
            queries_keys(misc0, 0, 0)
            project_values(misc0, 0, 0)
            scores(0, 0, 0)
            batches(pe, emit)
            tail = Misc(TAIL, TAIL % 2)
            probs_in = turn_probs(tail, B - 1, TILES - 1)
            rows(tail, values(tail, TILES - 1, probs_in))
            for q in range(QUADS):
                gather(B - 1, 1, q, 0, K, turn_bits(tail, B - 1, q))

        @block.scalar
        def _(act):
            def move(dst, src, scale=1.0, bias=0.0, func=ACT.Identity):
                return nc.scalar.activation(dst, src, func, scale=scale, bias=bias)

            act.wait_ge(w_in_landed, 96)
            move(code[:].rearrange("p a b -> p (a b)"), code_in).then_inc(act_setup, 1)
            move(identb[:], con["ident"]).then_inc(act_setup, 1)
            move(negs[:], con["negs"]).then_inc(act_setup, 1)
            move(qbias[:], bias[:, 0:1], scale=DH ** -0.5).then_inc(act_setup, 1)
            act.wait_ge(w_turned, 1)
            move(wT[:].rearrange("p a b -> p (a b)"), mi_ps[0][:]).then_inc(act_setup, 1)
            act.wait_ge(act_setup, 5)
            act.wait_ge(setup_done, 4)

            class Moves:

                def __init__(self, base, bank):
                    self.base, self.bank, self.n = base, bank, 0

                def next(self):
                    act.wait_ge(misc_ready, self.base + self.n + 1)
                    self.n += 1
                    return mi_ps[(self.bank + self.n - 1) % 2]

            def norms(mv_, par):
                move(nxx[:, par, :], mv_.next()[:, 0:TILES], scale=2.0).then_inc(misc_moved, 1)
                return mv_.base + mv_.n

            def coordinates(mv_, b, par):
                if not (isinstance(b, int) and b < 2):
                    act.wait_ge(g_done, (b - 1) * NG)
                move(table[:, par, :], mv_.next()[:, 0:3 * TILES]).then_inc(misc_moved, 1)

            def distances(b, par, t, h, ready=None):
                s = b * TILES + t
                if ready is not None:
                    act.wait_ge(misc_moved, ready)
                if h == 0 and not (isinstance(s, int) and s < RING):
                    act.wait_ge(topk_done, s - RING + 1)
                act.wait_ge(pd_ready, s * 2 + h + 1)
                move(pd_sb[:, t % RING, bass.ts(h, HALF)], pd_ps[:, h, :], scale=2.0,
                     bias=nxx[:, par, t:t + 1]).then_inc(pd_moved, 1)

            def queries_keys(mv_, b, h):
                move(qs[:], mv_.next()[:], scale=DH ** -0.5, bias=qbias[:]).then_inc(misc_moved, 1)
                if not (isinstance(b, int) and b == 0 and h == 0):
                    act.wait_ge(kz_ready, b * TILES + h * QT)
                move(kt[:], mv_.next()[:], bias=bias[:, 1:2]).then_inc(misc_moved, 1)

            def project_values(mv_, h):
                for v in range(2):
                    ps = mv_.next()[:].rearrange("p (m r) -> p m r", r=2 * DH)
                    for a in range(2):
                        zone = vz[64 * a:64 * a + 64, h, 4 * v:4 * v + 4, :].rearrange("p c (g r) -> p (c g) r", r=2 * DH)
                        m = nc.scalar.copy(zone[:, :, a * DH:(a + 1) * DH], ps[64 * a:64 * a + 64, :, a * DH:(a + 1) * DH])
                    m.then_inc(misc_moved, 1)

            def gather(b, q, lo, hi):
                for k in range(lo, hi):
                    act.wait_ge(oh_ready, b * UNITS + q * K + k + 1)
                    move(ohT[:, k % 2, :], oh_ps[k % 2][:], bias=con["lobias"], func=ACT.Relu).then_inc(oh_moved, 1)
                    if k % GK == GK - 1:
                        gi = q * GROUPS + k // GK
                        gg = b * NG + gi
                        act.wait_ge(g_ready, gg + 1)
                        if not (isinstance(gg, int) and gg < 2):
                            act.wait_ge(g_done, gg - 1)
                        nc.scalar.copy(gsb[:, gi % 2, :], g_ps[:].rearrange("p k t c -> p (k t c)")).then_inc(g_moved, 1)

            def emit(b, j, par, first, last):
                mv_ = Moves(misc_base(b), first_bank(b))
                ready = None
                for t in range(TILES):
                    h, quarter = divmod(t, QT)
                    at = unit_starts[quarter]

                    def units(n):
                        nonlocal at
                        if not first:
                            gather(b - 1, h, at, at + n)
                        at += n

                    def ahead(i, half):
                        if t + i < TILES:
                            distances(b, par, t + i, half)
                        elif not last:
                            distances(b + 1, 1 - par, t + i - TILES, half, ready if (i, half) == (2, 0) else None)

                    before = t > 0 or not first
                    nb, nh = (b, 1) if h == 0 else (b + 1, 0)
                    ongoing = h == 0 or not last
                    exponents(b * TILES + t, t)
                    if quarter % 2 == 0:
                        if quarter == 0 and not first:
                            bits(mv_)
                        if t == TILES - 2 and not last:
                            ready = norms(mv_, 1 - par)
                        ahead(2, 0)
                        if before:
                            turned_probs(mv_)
                        ahead(2, 1)
                        units(1)
                        ahead(3, 0)
                        if before:
                            values(mv_, (t - 1) % TILES)
                        units(1)
                        ahead(3, 1)
                        if quarter == 0:
                            if before:
                                rows(mv_, b if t > 0 else b - 1, 0 if t > 0 else 1)
                            units(2)
                        else:
                            if ongoing:
                                queries_keys(mv_, nb, nh)
                            units(4)
                    elif quarter == 1:
                        turned_probs(mv_)
                        units(3)
                        values(mv_, t - 1)
                        if t == 1:
                            coordinates(mv_, b, par)
                        units(8)
                    else:
                        turned_probs(mv_)
                        units(2)
                        values(mv_, t - 1)
                        units(2)
                        if ongoing:
                            project_values(mv_, nh)
                        units(5)

            def exponents(s, t):
                act.wait_ge(max_ready, s + 1)
                for hd in range(HEADS):
                    m = nc.scalar.activation(sS[:, t % 2, hd, :], s_ps[:, hd, :], ACT.Exp, bias=mx[:, t % 2, hd:hd + 1],
                                             accum_out=rs[:, t % 2, hd:hd + 1])
                m.then_inc(exp_ready, 1)

            def turned_probs(mv_):
                nc.scalar.copy(pT[:].rearrange("p g k -> p (g k)"), mv_.next()[:]).then_inc(misc_moved, 1)

            def values(mv_, t):
                move(oT[:, bass.ts(t % QT, P)], mv_.next()[:, 0:P], bias=bias[:, 2:3]).then_inc(misc_moved, 1)

            def rows(mv_, b, h):
                ps = mv_.next()
                if h == 0 and not (isinstance(b, int) and b == 0):
                    act.wait_ge(y_stored, b * 16)
                move(y_s[:, h, :], ps[:], bias=bias[:, 3:4]).then_inc(misc_moved, 1)

            def bits(mv_):
                nc.scalar.copy(bitsT[:].rearrange("p a b -> p (a b)"), mv_.next()[:].bitcast(BF16)).then_inc(misc_moved, 1)

            mv0 = Moves(0, 0)
            ready = norms(mv0, 0)
            for t in range(2):
                for h in range(2):
                    distances(0, 0, t, h, ready)
            queries_keys(mv0, 0, 0)
            project_values(mv0, 0)
            batches(act, emit)
            tail = Moves(TAIL, TAIL % 2)
            turned_probs(tail)
            values(tail, TILES - 1)
            rows(tail, B - 1, 1)
            for q in range(QUADS):
                bits(tail)
                gather(B - 1, q, 0, K)

        STEPS = TILES * 7

        @block.vector
        def _(dve):
            dve.wait_ge(w_in_landed, 96)
            nc.vector.tensor_scalar(neghalf[:], con["ones"], -0.5, None, ALU.mult).then_inc(setup_done, 1)
            nc.vector.tensor_copy(bitval[:], con["bitval"]).then_inc(setup_done, 1)
            nc.vector.tensor_copy(hival[:], con["hival"]).then_inc(setup_done, 1)
            nc.vector.memset(vz[:], 0.0).then_inc(setup_done, 1)
            dve.wait_ge(setup_done, 4)

            def invert(b, j, par):
                dve.wait_ge(mask_landed[par], (j + 1) * 16)
                nc.vector.tensor_scalar(minv[:, par, :], maskb[:, par, :], 0.0, None, ALU.is_le).then_inc(minv_ready, 1)

            def digits(b, par, q):
                n = b * QUADS + q
                if not (isinstance(n, int) and n == 0):
                    dve.wait_ge(bitsb_ready, n)
                    dve.wait_ge(hi_ready, n)
                if not (isinstance(b, int) and b == 0):
                    dve.wait_ge(g_done, b * NG - (QUADS - 1 - q) * GROUPS)
                dve.wait_ge(topk_done, b * TILES + (q + 1) * QT)
                m = QT * KP
                flat = idx16[:, par, q * QT:(q + 1) * QT].rearrange("p t k -> p (t k)")
                nc.vector.tensor_tensor(bits16[:].rearrange("p t k e -> p (t k) e"),
                                        flat.rearrange("p (m o) -> p m o", o=1).to_broadcast([P, m, BITS]),
                                        bitval[:].rearrange("p (o e) -> p o e", o=1).to_broadcast([P, m, BITS]),
                                        ALU.bitwise_and).then_inc(bits_ready, 1)
                nc.vector.tensor_scalar(hi16[:].rearrange("p t k -> p (t k)"), flat, (HI - 1) * LO, None,
                                        ALU.bitwise_and).then_inc(hi_cut, 1)
                dve.wait_ge(hi_cut, n + 1)
                src = hi16[:, :, 0:K].rearrange("p t (k o) -> p k t o", o=1)
                nc.vector.tensor_tensor(hi1h[:, q].rearrange("p (k t) e -> p k t e", t=QT),
                                        src.to_broadcast([P, K, QT, HI]),
                                        hival[:].rearrange("p (o u e) -> p o u e", o=1, u=1).to_broadcast([P, K, QT, HI]),
                                        ALU.is_equal).then_inc(hi_ready, 1)

            def row_stats(b, h):
                dve.wait_ge(y_ready, b * 2 + h + 1)
                nc.vector.bn_stats(bnst[:, h, :], y_s[:, h, :]).then_inc(bn_step, 1)
                if h == 1:
                    if not (isinstance(b, int) and b == 0):
                        dve.wait_ge(mv_kept, b)
                    gate(dve, bn_step, b * 2 + 2, dve_gates)
                    nc.vector.bn_aggr(mv[:], bnst[:].rearrange("p h s -> p (h s)")).then_inc(mv_ready, 1)

            def emit(b, j, par, first, last):
                step = b * STEPS
                if not (isinstance(b, int) and b < 2):
                    dve.wait_ge(idx_kept, (b - 1) * QUADS)
                for t in range(0, TILES, 2):
                    s = b * TILES + t
                    if t == 4 and not last:
                        invert(b + 1, (b + 1) // 2 if isinstance(b, int) else (j if par == 0 else j + 1), 1 - par)
                    for r in range(RANKS):
                        for i in range(2):
                            if r == 0:
                                if not (isinstance(s, int) and s == 0):
                                    gate(dve, topk_done, s - 1 + i, dve_gates)
                                gate(dve, pd_moved, (s + i) * 2 + 2, dve_gates)
                            else:
                                step = step + 1
                                gate(dve, topk_step, step, dve_gates)
                            nc.vector.max(vals[:, i, :], pd_sb[:, (t + i) % RING, :]).then_inc(topk_step, 1)
                        for i in range(2):
                            work = pd_sb[:, (t + i) % RING, :]
                            step = step + 1
                            gate(dve, topk_step, step, dve_gates)
                            found = nc.vector.max_index(idx16[:, par, t + i, 8 * r:8 * r + 8], vals[:, i, :], work)
                            if r < RANKS - 1:
                                nc.vector.match_replace(work, vals[:, i, :], work, REMOVED).then_inc(topk_step, 1)
                            else:
                                found.then_inc(topk_done, 1)
                        if r % 2 == 0:
                            if r > 0 or t > 0 or not first:
                                inverse(s + r // 2 - 1, t + r // 2 - 1)
                            largest(s + r // 2, t + r // 2)
                        if t == 2 and r == 2 and not first:
                            digits(b - 1, 1 - par, 1)
                            row_stats(b - 1, 1)
                        if t == 6 and r == 2:
                            digits(b, par, 0)
                            row_stats(b, 0)

            def largest(s, t):
                dve.wait_ge(s_ready, s + 1)
                nc.vector.tensor_reduce(mx[:, t % 2, :], s_ps[:], AX.X, ALU.max, negate=True).then_inc(max_ready, 1)

            def inverse(s, t):
                dve.wait_ge(exp_ready, s + 1)
                nc.vector.reciprocal(rs[:, t % 2, :], rs[:, t % 2, :]).then_inc(rcp_ready, 1)

            invert(0, 0, 0)
            batches(dve, emit)
            inverse(B * TILES - 1, TILES - 1)
            digits(B - 1, 1, 1)
            row_stats(B - 1, 1)

        @block.gpsimd
        def _(pool):
            pool.wait_ge(w_in_landed, 96)

            def square(b, j, par):
                pool.wait_ge(ctx_landed[par], (j + 1) * 16)
                if not (isinstance(b, int) and b == 0):
                    pool.wait_ge(pd_ready, b * TILES * 2)
                nc.gpsimd.tensor_tensor(sq[:], ctx_s[:, par, :], ctx_s[:, par, :], ALU.mult).then_inc(sq_ready, 1)

            class Steps:
                def __init__(self, base):
                    self.base, self.n = base, 0

                def __call__(self, ins):
                    ins.then_inc(pool_step, 1)
                    self.n += 1
                    pool.wait_ge(pool_step, self.base + self.n)

            def gather(b, par, q, groups, steps):
                for g in groups:
                    gi = q * GROUPS + g
                    gg = b * NG + gi
                    pool.wait_ge(g_moved, gg + 1)
                    rows = GK * QT
                    hot = hi1h[:, q, g * rows:(g + 1) * rows, :].rearrange("p m (e o) -> p (m e) o", o=1)
                    whole = gsb[:, gi % 2, :]
                    spots = whole.rearrange("p (m c) -> p m c", c=3)
                    steps(nc.gpsimd.tensor_tensor(spots, spots, hot.to_broadcast([P, rows * HI, 3]), ALU.mult))
                    sums = whole.rearrange("p (m c) -> p m c", c=HI * 3)
                    for width in (12, 6, 3):
                        steps(nc.gpsimd.tensor_tensor(sums[:, :, 0:width], sums[:, :, 0:width], sums[:, :, width:2 * width], ALU.add))
                    centre = table[:, par, q * QT * 3:(q + 1) * QT * 3].rearrange("p (o t c) -> p o t c", o=1, c=3)
                    at = b * BCOLS + q * QCOLS + g * rows
                    dst = planes[:, :, bass.ds(at, rows)].rearrange("p c (k t) -> p k t c", t=QT)
                    nc.gpsimd.tensor_tensor(dst, sums[:, :, 0:3].rearrange("p (k t) c -> p k t c", t=QT), centre.to_broadcast([P, GK, QT, 3]),
                                            ALU.subtract).then_inc(g_done, 1)

            def split(b, par, moved):
                n = b * SPLITS
                parts, whole = tparts[:, par], table[:, par, :]
                gate(pool, misc_moved, moved, pool_gates)
                nc.gpsimd.tensor_copy(parts[:, 0, :], whole).then_inc(split_step, 1)
                pool.wait_ge(split_step, n + 1)
                nc.gpsimd.tensor_tensor(trest[:], whole, parts[:, 0, :], ALU.subtract).then_inc(split_step, 1)
                gate(pool, split_step, n + 2, pool_gates)
                nc.gpsimd.tensor_copy(parts[:, 1, :], trest[:]).then_inc(split_step, 1)
                pool.wait_ge(split_step, n + 3)
                nc.gpsimd.tensor_tensor(parts[:, 2, :], trest[:], parts[:, 1, :], ALU.subtract).then_inc(split_step, 1)

            GSTEPS = NG * 4

            def emit(b, j, par, first, last):
                second = isinstance(b, int) and b == 1
                steps = Steps((b - 1) * GSTEPS - (0 if first or second else len(slot_groups[0]) * 4))
                for t in range(TILES):
                    h = t // QT
                    s = b * TILES + t
                    if t > 0 or not first:
                        normalise(s - 1, (t - 1) % TILES)
                    if t % QT != QT - 1:
                        spread_keys(b, t + 1)
                    if t == QT - 1:
                        pool.wait_ge(misc_moved, misc_base(b) + (7 if first else 11))
                        spread_keys(b, t + 1)
                    elif t == TILES - 1 and not last:
                        pool.wait_ge(misc_moved, misc_base(b) + (21 if first else 26))
                        spread_keys(b + 1, 0)
                    if t == QT + 1:
                        rows(b, j, par, 0, misc_base(b) + (14 if first else 19))
                    elif t == 1 and not first:
                        rows(b - 1, (b - 1) // 2 if isinstance(b, int) else (j - 1 if par == 0 else j), 1 - par, 1, misc_base(b) + 4)
                    if t == 0 and not first:
                        keep(b - 1, 1 - par)
                    if t == 2 and not first:
                        convert(b - 1, 1)
                    if t == 6:
                        convert(b, 0)
                    if t > 0 and not first:
                        gather(b - 1, 1 - par, 0 if t <= QT else 1, slot_groups[t % QT], steps)
                    elif t == 0 and not first and not second:
                        gather(b - 2, par, QUADS - 1, slot_groups[0], steps)
                    if t == 2:
                        split(b, par, misc_base(b) + (3 if first else 7))
                    if t == 5 and not first:
                        gate(pool, mv_ready, b, pool_gates)
                        nc.gpsimd.tensor_copy(stats_all[:, bass.ds(b - 1, 1), :].rearrange("p b s -> p (b s)"),
                                              mv[:]).then_inc(mv_kept, 1)
                    if t == TILES - 3 and not last:
                        square(b + 1, (b + 1) // 2 if isinstance(b, int) else (j if par == 0 else j + 1), 1 - par)

            def normalise(s, t):
                pool.wait_ge(rcp_ready, s + 1)
                nc.gpsimd.tensor_tensor(sS[:, t % 2], sS[:, t % 2],
                                        rs[:, t % 2, :].rearrange("p (h o) -> p h o", o=1).to_broadcast([P, HEADS, CHUNK]),
                                        ALU.mult).then_inc(probs_ready, 1)

            def rows(b, j, par, h, moved):
                pool.wait_ge(misc_moved, moved)
                if h == 0:
                    pool.wait_ge(mask_landed[par], (j + 1) * 16)
                    pool.wait_ge(x_landed, b * 16 + 16)
                cols = bass.ts(h, HALF)
                nc.gpsimd.tensor_tensor(y_s[:, h, :], y_s[:, h, :], maskb[:, par, cols], ALU.mult).then_inc(masked_y, 1)
                pool.wait_ge(masked_y, b * 2 + h + 1)
                nc.gpsimd.tensor_tensor(y_s[:, h, :], y_s[:, h, :], x_s[:, cols], ALU.add).then_inc(y_ready, 1)

            def spread_keys(b, t):
                s = b * TILES + t
                if not (isinstance(s, int) and s < 2):
                    pool.wait_ge(s_ready, s - 1)
                c = t % QT
                src = kt[:, 2 * c * CHUNK:2 * (c + 1) * CHUNK].rearrange("p (e o k) -> p e o k", e=2, o=1)
                heads = con["headmask"].rearrange("p (o h u) -> p o h u", o=1, u=1)
                nc.gpsimd.tensor_tensor(kz[:, t % 2], src.to_broadcast([P, 2, HEADS, CHUNK]),
                                        heads.to_broadcast([P, 2, HEADS, CHUNK]), ALU.mult).then_inc(kz_ready, 1)

            def convert(b, q):
                n = b * QUADS + q
                gate(pool, bits_ready, n + 1, pool_gates)
                if not (isinstance(n, int) and n == 0):
                    gate(pool, oh_ready, (n - 1) * K + 1, pool_gates)
                nc.gpsimd.tensor_copy(bitsb[:].rearrange("p t m -> p (t m)"),
                                      bits16[:].rearrange("p t k e -> p (t k e)")).then_inc(bitsb_ready, 1)
                pool.wait_ge(hi_ready, n + 1)

            def keep(b, par):
                gate(pool, topk_done, (b + 1) * TILES, pool_gates)
                for q in range(QUADS):
                    dst = idx_all[:, bass.ds(b * BCOLS + q * QCOLS, QCOLS)].rearrange("p (k t) -> p k t", t=QT)
                    nc.gpsimd.tensor_copy(dst, idx16[:, par, q * QT:(q + 1) * QT, 0:K].rearrange("p t k -> p k t")).then_inc(idx_kept, 1)

            square(0, 0, 0)
            pool.wait_ge(misc_moved, 3)
            spread_keys(0, 0)
            batches(pool, emit)
            normalise(B * TILES - 1, TILES - 1)
            rows(B - 1, B // 2 - 1, 1, 1, TAIL + 3)
            keep(B - 1, 1)
            steps = Steps((B - 1) * GSTEPS - len(slot_groups[0]) * 4)
            gather(B - 2, 0, QUADS - 1, slot_groups[0], steps)
            gather(B - 1, 1, 0, range(GROUPS), steps)
            convert(B - 1, 1)
            gather(B - 1, 1, 1, range(GROUPS), steps)
            pool.wait_ge(mv_ready, B)
            nc.gpsimd.tensor_copy(stats_all[:, B - 1, :], mv[:]).then_inc(mv_kept, 1)
            pool.wait_ge(g_done, B * NG)
            pool.wait_ge(mv_kept, B)


def stage_b(nc, con, planes, w1, g1, b1, w2, g2, b2, w3, g3, b3):
    CH = 4
    W = N // CH
    C1, C2 = 6, 3
    HN = N // 2
    BN = 512
    NB = N // BN
    with ExitStack() as st:
        def sb(name, shape, dt=F32):
            return st.enter_context(nc.sbuf_tensor(name, shape, dt))

        def sem(name):
            return st.enter_context(nc.semaphore(name))

        w1b = sb("w1b", [P, C1, 2, 3])
        gb1 = sb("gb1", [P, 2, C1])
        w2b = sb("w2b", [P, C2, C1])
        gb2 = sb("gb2", [P, 2, C2])
        w3b = sb("w3b", [P, C2])
        gb3 = sb("gb3", [P, 2])
        small = {n: sb("sm_" + n, s) for n, s in dict(
            sum3=[P, 3], mean=[P, 3], cov=[P, 6], covf=[P, 3, 3], rs=[P, C1], mat=[P, C1, 3], ab=[P, C1, 3], mm=[P, C1, 3],
            mh=[P, C1], tri=[P, C1, 3, 3], tm=[P, C1, 3], tv=[P, C1, 3], var=[P, C1], sd=[P, C1], a1=[P, C1], ma=[P, C1],
            bb=[P, C1], mat2=[P, C1, 3], eps=[P, 1], mv2=[P, C2, 2], pm=[P, C2], dv=[P, C2], d2=[P, C2], vv=[P, C2],
            sd2=[P, C2], a2=[P, C2], ma2=[P, C2], bb2=[P, C2], mv3=[P, 2], pm3=[P, 1], dv3=[P, 1], d3=[P, 1], vv3=[P, 1],
            sd3=[P, 1], a3=[P, 1], ma3=[P, 1], bb3=[P, 1], ar2=[P, C2], am2=[P, C2], tot=[P, 8]).items()}
        loaded = sem("b_loaded")
        vstep = sem("b_vstep")
        astep = sem("b_astep")
        pstep = sem("b_pstep")
        tot_ps = st.enter_context(nc.psum_tensor("tot_ps", [P, 4, 512], F32))

        def bc(ap):
            return ap

        with ExitStack() as s1:
            def sb1(name, shape, dt=F32):
                return s1.enter_context(nc.sbuf_tensor(name, shape, dt))

            ab3 = sb1("ab3", [P, 3, W])
            two = sb1("two", [P, 2, W])
            root = sb1("root", [P, 2, W])
            mn = sb1("mn", [P, 2, W])
            mxx = sb1("mxx", [P, 2, W])
            block = s1.enter_context(nc.Block())

            @block.sync
            def _(sp):
                def spread(ap, n):
                    return ap.rearrange("(o n) -> o n", o=1).to_broadcast([P, n])
                sp.dma_start(w1b[:].rearrange("p a b c -> p (a b c)"),
                             spread(w1.rearrange("a b -> (a b)"), C1 * 6)).then_inc(loaded, 16)
                sp.dma_start(gb1[:, 0, :], spread(g1, C1)).then_inc(loaded, 16)
                sp.dma_start(gb1[:, 1, :], spread(b1, C1)).then_inc(loaded, 16)
                sp.dma_start(w2b[:].rearrange("p a b -> p (a b)"),
                             spread(w2.rearrange("a b -> (a b)"), C2 * C1)).then_inc(loaded, 16)
                sp.dma_start(gb2[:, 0, :], spread(g2, C2)).then_inc(loaded, 16)
                sp.dma_start(gb2[:, 1, :], spread(b2, C2)).then_inc(loaded, 16)
                sp.dma_start(w3b[:], spread(w3.rearrange("a b -> (a b)"), C2)).then_inc(loaded, 16)
                sp.dma_start(gb3[:, 0:1], spread(g3, 1)).then_inc(loaded, 16)
                sp.dma_start(gb3[:, 1:2], spread(b3, 1)).then_inc(loaded, 16)
                sp.wait_ge(loaded, 9 * 16)

            A_PER, V_PER = 6, 19

            @block.scalar
            def _(act):
                with act.Fori(0, CH) as c:
                    rel = planes[:, :, bass.ds(c * W, W)]
                    va = c * V_PER + 1
                    act.wait_ge(vstep, va)
                    nc.scalar.activation(ab3[:], rel, ACT.Square).then_inc(astep, 1)
                    act.wait_ge(vstep, va + 3)
                    nc.scalar.activation(root[:], mn[:], ACT.Sqrt).then_inc(astep, 1)
                    nc.scalar.activation(ab3[:], rel, ACT.Abs).then_inc(astep, 1)
                    act.wait_ge(vstep, va + 9)
                    nc.scalar.activation(mn[:], mn[:], ACT.Arctan).then_inc(astep, 1)
                    act.wait_ge(vstep, va + 12)
                    nc.scalar.activation(mn[:], mn[:], ACT.Abs).then_inc(astep, 1)
                    act.wait_ge(vstep, va + 14)
                    nc.scalar.activation(mn[:, 1, :], mxx[:, 1, :], ACT.Abs).then_inc(astep, 1)
                act.wait_ge(vstep, CH * V_PER + 1)
                for i in range(3):
                    nc.scalar.activation(planes[:, i, :], planes[:, i, :], ACT.Identity,
                                         accum_out=small["sum3"][:, i:i + 1]).then_inc(astep, 1)
                act.wait_ge(astep, CH * A_PER + 3)

            @block.vector
            def _(dve):
                v = nc.vector
                v.memset(small["eps"][:], EPS).then_inc(vstep, 1)
                with dve.Fori(0, CH) as c:
                    base, aa = c * V_PER + 1, c * A_PER
                    tick = Ticks(dve, vstep, base)
                    px = planes[:, 0, bass.ds(c * W, W)]
                    py = planes[:, 1, bass.ds(c * W, W)]
                    pz = planes[:, 2, bass.ds(c * W, W)]
                    dve.wait_ge(astep, aa + 1)
                    tick(v.tensor_tensor(two[:, 0, :], ab3[:, 0, :], ab3[:, 1, :], ALU.add))
                    tick.settle()
                    tick(v.tensor_tensor(two[:, 1, :], two[:, 0, :], ab3[:, 2, :], ALU.add))
                    tick.settle()
                    tick(v.tensor_scalar(mn[:], two[:], TINY, None, ALU.max))
                    dve.wait_ge(astep, aa + 3)
                    tick(v.tensor_tensor(mn[:, 0, :], ab3[:, 2, :], root[:, 0, :], ALU.min))
                    tick(v.tensor_tensor(mn[:, 1, :], ab3[:, 1, :], ab3[:, 0, :], ALU.min))
                    tick(v.tensor_tensor(mxx[:, 0, :], ab3[:, 2, :], root[:, 0, :], ALU.max))
                    tick(v.scalar_tensor_tensor(mxx[:, 1, :], ab3[:, 0, :], DEN_FLOOR, ab3[:, 1, :], ALU.max, ALU.max))
                    tick.settle()
                    tick(v.reciprocal(mxx[:], mxx[:]))
                    tick.settle()
                    tick(v.tensor_tensor(mn[:], mn[:], mxx[:], ALU.mult))
                    tick.settle()
                    tick(v.tensor_tensor(mxx[:, 0, :], ab3[:, 2, :], root[:, 0, :], ALU.is_gt))
                    tick(v.tensor_tensor(mxx[:, 1, :], ab3[:, 1, :], ab3[:, 0, :], ALU.is_gt))
                    tick.settle()
                    dve.wait_ge(astep, aa + 4)
                    tick(v.scalar_tensor_tensor(mn[:].rearrange("p a w -> p (a w)"), mxx[:].rearrange("p a w -> p (a w)"),
                                                PI / 2, mn[:].rearrange("p a w -> p (a w)"), ALU.mult, ALU.subtract))
                    tick.settle()
                    tick(v.tensor_scalar(mxx[:, 1, :], px, 0.0, PI, ALU.is_lt, ALU.mult))
                    dve.wait_ge(astep, aa + 5)
                    tick.settle()
                    tick(v.tensor_tensor(mxx[:, 1, :], mxx[:, 1, :], mn[:, 1, :], ALU.subtract))
                    tick(v.scalar_tensor_tensor(mn[:, 0, :].bitcast(I32), pz.bitcast(I32), SIGN, mn[:, 0, :].bitcast(I32),
                                                ALU.bitwise_and, ALU.bitwise_or))
                    dve.wait_ge(astep, aa + 6)
                    tick(v.scalar_tensor_tensor(mn[:, 1, :].bitcast(I32), py.bitcast(I32), SIGN, mn[:, 1, :].bitcast(I32),
                                                ALU.bitwise_and, ALU.bitwise_or))
                    tick.settle()
                    tick(v.scalar_tensor_tensor(py, two[:, 1, :], TINY, mn[:, 0, :], ALU.is_ge, ALU.mult))
                    tick(v.scalar_tensor_tensor(pz, two[:, 0, :], TINY, mn[:, 1, :], ALU.is_ge, ALU.mult))
                    tick(v.tensor_copy(px, root[:, 1, :]))
                    tick.settle()
                    assert tick.n == V_PER, tick.n

        with ExitStack() as s2:
            def sb2(name, shape, dt=F32):
                return s2.enter_context(nc.sbuf_tensor(name, shape, dt))

            def sem2(name):
                return s2.enter_context(nc.semaphore(name))

            th = sb2("th", [P, 2, HN])
            h2 = sb2("h2", [P, C2, HN])
            bst = sb2("bst", [P, C2, NB, 6])
            S = small
            vs = sem2("c_vstep")
            summed = sem2("c_summed")
            mean_in = sem2("c_mean_in")
            cov_in = sem2("c_cov_in")
            var_in = sem2("c_var_in")
            sd_out = sem2("c_sd_out")
            mat_in = sem2("c_mat_in")
            t_out = sem2("c_t_out")
            t_mixed = sem2("c_t_mixed")
            h_out = sem2("c_h_out")
            h_used = sem2("c_h_used")
            w_out_ = sem2("c_w_out")
            h2_in = sem2("c_h2_in")
            pm_in = sem2("c_pm_in")
            bn_in = sem2("c_bn_in")
            g_out = sem2("c_g_out")
            h3_in = sem2("c_h3_in")
            e_in = sem2("c_e_in")
            e_out = sem2("c_e_out")
            mxp = sb2("mxp", [P, B * QUADS, QT])
            smp = sb2("smp", [P, B * QUADS, QT])
            block = s2.enter_context(nc.Block())

            @block.tensor
            def _(pe):
                ones = con["ones"]
                nc.tensor.matmul(tot_ps[:, 0, 0:3], ones, S["sum3"][:], start=True, stop=True).then_inc(summed, 1)
                pe.wait_ge(cov_in, 1)
                nc.tensor.matmul(tot_ps[:, 1, 0:6], ones, S["cov"][:], start=True, stop=True).then_inc(summed, 1)
                for n, (a, b, w, bank) in enumerate((("pm", "d2", C2, 2), ("pm3", "d3", 1, 3))):
                    pe.wait_ge(pm_in, 2 * n + 1)
                    nc.tensor.matmul(tot_ps[:, bank, 0:w], ones, S[a][:], start=True, stop=True).then_inc(summed, 1)
                    pe.wait_ge(pm_in, 2 * n + 2)
                    nc.tensor.matmul(tot_ps[:, bank, 8:8 + w], ones, S[b][:], start=True, stop=True).then_inc(summed, 1)

            @block.scalar
            def _(act):
                a = nc.scalar
                act.wait_ge(var_in, 1)
                a.activation(S["sd"][:], S["var"][:], ACT.Sqrt, bias=S["eps"][:]).then_inc(sd_out, 1)
                act.wait_ge(mat_in, 1)
                def first_term(n):
                    jj, hf = n % C1, n // C1
                    if n >= 2:
                        act.wait_ge(h_used, n - 1)
                    a.activation(th[:, n % 2, :], planes[:, 0, bass.ts(hf, HN)], ACT.Identity,
                                 scale=S["mat2"][:, jj, 0:1], bias=S["bb"][:, jj:jj + 1]).then_inc(t_out, 1)

                for hf in range(2):
                    for jj in range(C1):
                        first_term(hf * C1 + jj)
                    for i in range(C2):
                        act.wait_ge(h2_in, hf * C2 + i + 1)
                        a.copy(planes[:, i, bass.ts(hf, HN)], h2[:, i, :]).then_inc(w_out_, 1)
                act.wait_ge(var_in, 2)
                a.activation(S["sd2"][:], S["vv"][:], ACT.Sqrt, bias=S["eps"][:]).then_inc(sd_out, 1)
                act.wait_ge(bn_in, 1)
                for i in range(C2):
                    a.activation(planes[:, i, :], planes[:, i, :], ACT.Identity,
                                 scale=S["a2"][:, i:i + 1], bias=S["bb2"][:, i:i + 1]).then_inc(g_out, 1)
                act.wait_ge(var_in, 3)
                a.activation(S["sd3"][:], S["vv3"][:], ACT.Sqrt, bias=S["eps"][:]).then_inc(sd_out, 1)
                act.wait_ge(bn_in, 2)
                a.activation(planes[:, 0, :], planes[:, 0, :], ACT.Identity,
                             scale=S["a3"][:], bias=S["bb3"][:]).then_inc(g_out, 1)
                act.wait_ge(e_in, 1)
                a.activation(planes[:, 0, :], planes[:, 0, :], ACT.Exp).then_inc(e_out, 1)

            @block.vector
            def _(dve):
                v = nc.vector
                tick = Ticks(dve, vs)

                def do(ins):
                    tick(ins)
                    tick.settle()

                def over(ap, shape):
                    return ap.to_broadcast(shape)

                def inner(ap, w):
                    return ap.rearrange("p (n o) -> p n o", o=1).to_broadcast([P, ap.shape[1], w])

                A, Bm = w1b[:, :, 0, :], w1b[:, :, 1, :]
                do(v.tensor_reduce(S["rs"][:], Bm, AX.X, ALU.add))
                do(v.tensor_scalar(S["rs"][:], S["rs"][:], 1.0 / 3.0, None, ALU.mult))
                do(v.tensor_tensor(S["ab"][:], A, Bm, ALU.add))
                do(v.tensor_tensor(S["mat"][:], S["ab"][:], inner(S["rs"][:], 3), ALU.subtract))
                dve.wait_ge(summed, 1)
                do(v.tensor_scalar(S["mean"][:], tot_ps[:, 0, 0:3], 1.0 / PAIRS, None, ALU.mult))
                junk = th[:].rearrange("p a w -> p (a w)")
                order = [(0, 0), (0, 1), (0, 2), (1, 1), (1, 2), (2, 2)]
                for n, (i, k) in enumerate(order):
                    do(v.scalar_tensor_tensor(junk, planes[:, i, :], S["mean"][:, i:i + 1], planes[:, k, :],
                                              ALU.subtract, ALU.mult, accum_out=S["cov"][:, n:n + 1]))
                v.memset(S["tot"][:], 0.0).then_inc(cov_in, 1)
                dve.wait_ge(summed, 2)
                for n, (i, k) in enumerate(order):
                    do(v.tensor_scalar(S["covf"][:, i, k:k + 1], tot_ps[:, 1, n:n + 1], 1.0 / PAIRS, None, ALU.mult))
                    if i != k:
                        do(v.tensor_scalar(S["covf"][:, k, i:i + 1], tot_ps[:, 1, n:n + 1], 1.0 / PAIRS, None, ALU.mult))
                do(v.tensor_tensor(S["mm"][:], S["mat"][:], over(S["mean"][:].rearrange("p (o i) -> p o i", o=1), [P, C1, 3]), ALU.mult))
                do(v.tensor_reduce(S["mh"][:], S["mm"][:], AX.X, ALU.add))
                for k in range(3):
                    do(v.tensor_tensor(S["tri"][:, :, k, :], S["mat"][:],
                                       over(S["covf"][:, k, :].rearrange("p (o i) -> p o i", o=1), [P, C1, 3]), ALU.mult))
                do(v.tensor_reduce(S["tm"][:], S["tri"][:], AX.X, ALU.add))
                do(v.tensor_tensor(S["tv"][:], S["tm"][:], S["mat"][:], ALU.mult))
                do(v.tensor_reduce(S["var"][:], S["tv"][:], AX.X, ALU.add))
                do(v.tensor_scalar(S["var"][:], S["var"][:], 0.0, None, ALU.max))
                v.memset(S["tot"][:], 0.0).then_inc(var_in, 1)
                dve.wait_ge(sd_out, 1)
                do(v.reciprocal(S["a1"][:], S["sd"][:]))
                do(v.tensor_tensor(S["a1"][:], S["a1"][:], gb1[:, 0, :], ALU.mult))
                do(v.tensor_tensor(S["ma"][:], S["mh"][:], S["a1"][:], ALU.mult))
                do(v.tensor_tensor(S["bb"][:], gb1[:, 1, :], S["ma"][:], ALU.subtract))
                do(v.tensor_tensor(S["mat2"][:], S["mat"][:], inner(S["a1"][:], 3), ALU.mult))
                v.memset(S["tot"][:], 0.0).then_inc(mat_in, 1)
                n = 0
                for hf in range(2):
                    cols = bass.ts(hf, HN)

                    for jj in range(C1):
                        dve.wait_ge(t_out, n + 1)
                        t = th[:, n % 2, :]
                        for i in (1, 2):
                            do(v.scalar_tensor_tensor(t, planes[:, i, cols], S["mat2"][:, jj, i:i + 1], t, ALU.mult, ALU.add))
                        do(v.scalar_tensor_tensor(t, t, SLOPE, t, ALU.mult, ALU.max))
                        if jj == 0 and hf == 1:
                            dve.wait_ge(w_out_, C2)
                        for i in range(C2):
                            wij = w2b[:, i, jj:jj + 1]
                            if jj == 0:
                                ins = v.tensor_scalar(h2[:, i, :], t, wij, None, ALU.mult)
                            else:
                                ins = v.scalar_tensor_tensor(h2[:, i, :], t, wij, h2[:, i, :], ALU.mult, ALU.add)
                            if jj < C1 - 1:
                                tick(ins)
                            else:
                                ins.then_inc(h2_in, 1)
                        if jj < C1 - 1:
                            tick.settle()
                        else:
                            dve.wait_ge(h2_in, (hf + 1) * C2)
                        v.memset(S["tot"][:], 0.0).then_inc(h_used, 1)
                        n += 1

                def batch_norm(planes_n, mvx, pm, dv, d2, vv, sd, a, ma, bb, gb, at, base, bank, w):
                    for i in range(planes_n):
                        for s in range(NB):
                            tick(v.bn_stats(bst[:, i, s, :], planes[:, i, bass.ts(s, BN)]))
                    tick.settle()
                    for i in range(planes_n):
                        tick(v.bn_aggr(mvx[:, i, :], bst[:, i].rearrange("p s e -> p (s e)")))
                    tick.settle()
                    v.tensor_scalar(pm, mvx[:, :, 0], 1.0 / P, None, ALU.mult).then_inc(pm_in, 1)
                    dve.wait_ge(summed, base)
                    do(v.tensor_tensor(dv, mvx[:, :, 0], tot_ps[:, bank, 0:w], ALU.subtract))
                    do(v.tensor_tensor(d2, dv, dv, ALU.mult))
                    do(v.tensor_tensor(d2, d2, mvx[:, :, 1], ALU.add))
                    v.tensor_scalar(d2, d2, 1.0 / P, None, ALU.mult).then_inc(pm_in, 1)
                    dve.wait_ge(summed, base + 1)
                    v.tensor_copy(vv, tot_ps[:, bank, 8:8 + w]).then_inc(var_in, 1)
                    dve.wait_ge(sd_out, at)
                    do(v.reciprocal(a, sd))
                    do(v.tensor_tensor(a, a, gb[0], ALU.mult))
                    do(v.tensor_tensor(ma, tot_ps[:, bank, 0:w], a, ALU.mult))
                    v.tensor_tensor(bb, gb[1], ma, ALU.subtract).then_inc(bn_in, 1)

                dve.wait_ge(w_out_, 2 * C2)
                batch_norm(C2, S["mv2"][:], S["pm"][:], S["dv"][:], S["d2"][:], S["vv"][:], S["sd2"][:], S["a2"][:], S["ma2"][:],
                           S["bb2"][:], (gb2[:, 0, :], gb2[:, 1, :]), 2, 3, 2, C2)
                dve.wait_ge(g_out, 1)
                do(v.scalar_tensor_tensor(planes[:, 0, :], planes[:, 0, :], SLOPE, planes[:, 0, :], ALU.mult, ALU.max))
                do(v.tensor_scalar(planes[:, 0, :], planes[:, 0, :], w3b[:, 0:1], None, ALU.mult))
                for i in (1, 2):
                    dve.wait_ge(g_out, i + 1)
                    do(v.scalar_tensor_tensor(planes[:, i, :], planes[:, i, :], SLOPE, planes[:, i, :], ALU.mult, ALU.max))
                    do(v.scalar_tensor_tensor(planes[:, 0, :], planes[:, i, :], w3b[:, i:i + 1], planes[:, 0, :], ALU.mult, ALU.add))
                batch_norm(1, S["mv3"][:].rearrange("p (o s) -> p o s", o=1), S["pm3"][:], S["dv3"][:], S["d3"][:], S["vv3"][:], S["sd3"][:],
                           S["a3"][:], S["ma3"][:], S["bb3"][:], (gb3[:, 0:1], gb3[:, 1:2]), 3, 5, 3, 1)
                dve.wait_ge(g_out, C2 + 1)
                do(v.scalar_tensor_tensor(planes[:, 0, :], planes[:, 0, :], SLOPE, planes[:, 0, :], ALU.mult, ALU.max))
                m = B * QUADS
                att = planes[:, 0, :].rearrange("p (m k t) -> p m t k", m=m, t=QT)
                flat = planes[:, 0, :].rearrange("p (m k t) -> p m k t", m=m, t=QT)
                do(v.tensor_reduce(mxp[:], att, AX.X, ALU.max))
                v.tensor_tensor(flat, flat, mxp[:].rearrange("p m (o t) -> p m o t", o=1).to_broadcast([P, m, K, QT]),
                                ALU.subtract).then_inc(e_in, 1)
                dve.wait_ge(e_out, 1)
                do(v.tensor_reduce(smp[:], att, AX.X, ALU.add))
                do(v.reciprocal(smp[:], smp[:]))
                do(v.tensor_tensor(flat, flat, smp[:].rearrange("p m (o t) -> p m o t", o=1).to_broadcast([P, m, K, QT]), ALU.mult))


def stage_e(nc, con, planes, idx_all, stats_all, y_dram, out):
    NB = 16
    NGR = P // NB
    RING = 4
    DIGITS = 2
    ROWS = DIGITS + PARTS
    with ExitStack() as st:
        def sb(name, shape, dt=F32):
            return st.enter_context(nc.sbuf_tensor(name, shape, dt))

        def sem(name):
            return st.enter_context(nc.semaphore(name))

        y_s = sb("e_y", [P, 2, T])
        x1 = sb("e_x1", [P, 2, T])
        xT = sb("e_xT", [P, 2, TILES, C])
        rstd = sb("e_rstd", [P, B])
        nmr = sb("e_nmr", [P, B])
        nrm = sb("e_nrm", [P, 2])
        epsc = sb("e_eps", [P, 1])
        iotan = sb("e_iotan", [P, LO, NB], BF16)
        identb = sb("e_identb", [P, P], BF16)
        dig16 = sb("e_dig16", [P, DIGITS, BCOLS], U16)
        rest = sb("e_rest", [P, BCOLS])
        rowsb = sb("e_rowsb", [P, ROWS, BCOLS], BF16)
        pairs_s = sb("e_pairs", [P, 2, ROWS, P], BF16)
        hot = sb("e_hot", [P, P, HI], BF16)
        wgt = sb("e_wgt", [P, PARTS, P, HI], BF16)
        oh = sb("e_oh", [P, RING, LO, NB], BF16)
        at = sb("e_at", [P, 2, HI, QT, P])
        o_s = sb("e_o", [P, 2, HALF])
        spr = [planes[:, 1 + i, :].bitcast(BF16)[:, 0:P * PARTS * QT * HI].rearrange("p (n a t e) -> p n a t e", a=PARTS, t=QT, e=HI)
               for i in range(2)]
        tr_ps = st.enter_context(nc.psum_tensor("e_tr_ps", [P, 2, 512], F32))
        pr_ps = st.enter_context(nc.psum_tensor("e_pr_ps", [P, 512], F32))
        pairs_ps = pr_ps[:].bitcast(BF16)[:, 0:ROWS * P].rearrange("p (r n) -> p r n", r=ROWS)
        a_ps = [st.enter_context(nc.psum_tensor(f"e_a_ps{i}", [P, NB, QT, HI], F32)) for i in range(2)]
        o_ps = [st.enter_context(nc.psum_tensor(f"e_o_ps{i}", [P, HALF], F32)) for i in range(2)]
        y_landed = [sem(f"e_y_landed{i}") for i in range(2)]
        ln_step = sem("e_ln_step")
        sd_ready = sem("e_sd_ready")
        norm_ready = sem("e_norm_ready")
        x1_ready = sem("e_x1_ready")
        x1_turned = sem("e_x1_turned")
        xT_ready = sem("e_xT_ready")
        digits_cut = sem("e_digits_cut")
        part_step = sem("e_part_step")
        rows_ready = sem("e_rows_ready")
        pairs_turned = sem("e_pairs_turned")
        pairs_ready = sem("e_pairs_ready")
        hot_ready = sem("e_hot_ready")
        weighted = sem("e_weighted")
        spread_first = sem("e_spread_first")
        spread_last = sem("e_spread_last")
        oh_ready = sem("e_oh_ready")
        a_ready = sem("e_a_ready")
        a_moved = sem("e_a_moved")
        o_ready = sem("e_o_ready")
        o_added = sem("e_o_added")
        e_sp_gates = sem("e_sp_gates")
        e_pool_gates = sem("e_pool_gates")
        stored = [sem(f"e_stored{i}") for i in range(2)]
        pp = slice(0, QCOLS)
        ROW_STEPS = 2

        def passed(value):
            return not isinstance(value, int) or value > 0

        def batches(eng, emit):
            emit(0, 0, 0, False)
            emit(1, 0, 1, False)
            with eng.Fori(1, B // 2 - 1) as j:
                emit(j * 2, j, 0, False)
                emit(j * 2 + 1, j, 1, False)
            emit(B - 2, B // 2 - 1, 0, False)
            emit(B - 1, B // 2 - 1, 1, True)

        block = st.enter_context(nc.Block())

        @block.sync
        def _(sp):
            def load(b, par):
                if passed(b - 1):
                    gate(sp, x1_ready, b - 1, e_sp_gates)
                sp.dma_start(y_s[:, par, :], y_dram[b]).then_inc(y_landed[par], 16)

            def store(b, q):
                gate(sp, o_added, b * QUADS + q + 1, e_sp_gates)
                sp.dma_start(out[b][:, bass.ts(q, HALF)], o_s[:, q, :]).then_inc(stored[q], 16)

            def emit(b, j, par, last):
                if not last:
                    load(b + 1, 1 - par)
                if passed(b):
                    store(b - 1, 1)
                store(b, 0)

            load(0, 0)
            batches(sp, emit)
            store(B - 1, 1)
            for q in range(QUADS):
                sp.wait_ge(stored[q], 16 * B)

        @block.scalar
        def _(act):
            a = nc.scalar
            act.wait_ge(ln_step, 1)
            a.activation(rstd[:], stats_all[:, :, 1], ACT.Sqrt, bias=epsc[:]).then_inc(sd_ready, 1)

            def normalise(b, j, par):
                act.wait_ge(y_landed[par], (j + 1) * 16)
                act.wait_ge(norm_ready, b + 1)
                if passed(b - 1):
                    act.wait_ge(o_added, (b - 1) * QUADS)
                a.activation(x1[:, par, :], y_s[:, par, :], ACT.Identity, scale=nrm[:, 0:1], bias=nrm[:, 1:2]).then_inc(x1_ready, 1)

            def turned_rows(b, par):
                act.wait_ge(x1_turned, b + 1)
                if passed(b - 1):
                    act.wait_ge(o_ready, (b - 1) * QUADS)
                a.copy(xT[:, par].rearrange("p t c -> p (t c)"), tr_ps[:].rearrange("p a b -> p (a b)")).then_inc(xT_ready, 1)

            def pairs(n, q):
                act.wait_ge(pairs_turned, n + 1)
                a.copy(pairs_s[pp, q], pairs_ps[pp]).then_inc(pairs_ready, 1)

            def spread(n, q):
                act.wait_ge(weighted, n * PARTS + 1)
                for t in range(QT):
                    m = a.activation(spr[q][pp, :, 0, t, :], wgt[pp, 0], ACT.Copy, scale=con["tmask"][pp, t:t + 1])
                m.then_inc(spread_first, 1)

            def moved(n, q, g):
                act.wait_ge(a_ready, n * NGR + g + 1)
                if g == 0 and passed(n - 1):
                    act.wait_ge(o_ready, n - 1)
                dst = at[:, q, :, :, bass.ts(g, NB)].rearrange("p e t n -> p n t e")
                a.copy(dst, a_ps[g % 2][:]).then_inc(a_moved, 1)

            def emit(b, j, par, last):
                for q in range(QUADS):
                    n = b * QUADS + q
                    ahead = not (last and q == QUADS - 1)
                    if ahead:
                        pairs(n + 1, 1 - q)
                    if q == QUADS - 1 and not last:
                        normalise(b + 1, j if par == 0 else j + 1, 1 - par)
                    for g in range(NGR):
                        moved(n, q, g)
                        if g == 1 and ahead:
                            spread(n + 1, 1 - q)
                        if g == 3 and q == QUADS - 1 and not last:
                            turned_rows(b + 1, 1 - par)

            normalise(0, 0, 0)
            pairs(0, 0)
            turned_rows(0, 0)
            spread(0, 0)
            batches(act, emit)

        @block.gpsimd
        def _(pool):
            v = nc.gpsimd

            def norm(b):
                if passed(b):
                    gate(pool, x1_ready, b, e_pool_gates)
                v.tensor_copy(nrm[:, 0:1], rstd[:, bass.ds(b, 1)])
                v.tensor_copy(nrm[:, 1:2], nmr[:, bass.ds(b, 1)]).then_inc(norm_ready, 1)

            def rows(b):
                whole = planes[:, 0, bass.ds(b * BCOLS, BCOLS)]
                n = b * (PARTS - 1) + b
                if passed(b):
                    gate(pool, pairs_turned, b * QUADS, e_pool_gates)
                v.tensor_copy(rowsb[:, DIGITS, :], whole).then_inc(part_step, 1)
                gate(pool, part_step, n + 1, e_pool_gates)
                v.tensor_tensor(rest[:], whole, rowsb[:, DIGITS, :], ALU.subtract).then_inc(part_step, 1)
                gate(pool, part_step, n + 2, e_pool_gates)
                v.tensor_copy(rowsb[:, DIGITS + 1, :], rest[:]).then_inc(part_step, 1)
                pool.wait_ge(part_step, n + 3)
                v.tensor_tensor(rowsb[:, DIGITS + 2, :], rest[:], rowsb[:, DIGITS + 1, :], ALU.subtract).then_inc(rows_ready, 1)
                gate(pool, digits_cut, (b + 1) * DIGITS, e_pool_gates)
                v.tensor_copy(rowsb[:, 0:DIGITS, :], dig16[:]).then_inc(rows_ready, 1)

            def weigh(n, q):
                pool.wait_ge(hot_ready, n + 1)
                if passed(n):
                    pool.wait_ge(spread_first, n)
                    pool.wait_ge(spread_last, n * (PARTS - 1))
                for part in range(PARTS):
                    att = pairs_s[pp, q, DIGITS + part, :].rearrange("p (n o) -> p n o", o=1)
                    v.tensor_tensor(wgt[pp, part], hot[pp], att.to_broadcast([QCOLS, P, HI]), ALU.mult).then_inc(weighted, 1)

            def emit(b, j, par, last):
                for q in range(QUADS):
                    if not (last and q == QUADS - 1):
                        weigh(b * QUADS + q + 1, 1 - q)
                    if q == 0 and not last:
                        norm(b + 1)
                        rows(b + 1)

            pool.wait_ge(ln_step, 5)
            norm(0)
            rows(0)
            weigh(0, 0)
            batches(pool, emit)

        @block.vector
        def _(dve):
            v = nc.vector
            v.memset(epsc[:], EPS).then_inc(ln_step, 1)
            v.tensor_copy(iotan[:], con["iota"].rearrange("p (l o) -> p l o", o=1).to_broadcast([P, LO, NB])).then_inc(ln_step, 1)
            v.tensor_copy(identb[:], con["ident"]).then_inc(ln_step, 1)
            dve.wait_ge(sd_ready, 1)
            v.reciprocal(rstd[:], rstd[:]).then_inc(ln_step, 1)
            dve.wait_ge(ln_step, 4)
            v.scalar_tensor_tensor(nmr[:], stats_all[:, :, 0], -1.0, rstd[:], ALU.mult, ALU.mult).then_inc(ln_step, 1)

            def cut(b):
                cols = bass.ds(b * BCOLS, BCOLS)
                if passed(b):
                    dve.wait_ge(rows_ready, b * ROW_STEPS)
                v.tensor_scalar(dig16[:, 0, :], idx_all[:, cols], LO - 1, None, ALU.bitwise_and).then_inc(digits_cut, 1)
                v.tensor_scalar(dig16[:, 1, :], idx_all[:, cols], 7, None, ALU.logical_shift_right).then_inc(digits_cut, 1)

            def heat(n, q):
                dve.wait_ge(pairs_ready, n + 1)
                if passed(n):
                    dve.wait_ge(weighted, n * PARTS)
                high = pairs_s[pp, q, 1, :].rearrange("p (n o) -> p n o", o=1)
                v.tensor_tensor(hot[pp], high.to_broadcast([QCOLS, P, HI]),
                                con["hiiota"][pp].rearrange("p (o e) -> p o e", o=1).to_broadcast([QCOLS, P, HI]),
                                ALU.is_equal).then_inc(hot_ready, 1)

            def spread(n, q, part):
                dve.wait_ge(weighted, n * PARTS + part + 1)
                for t in range(QT):
                    m = v.tensor_scalar(spr[q][pp, :, part, t, :], wgt[pp, part], con["tmask"][pp, t:t + 1], None, ALU.mult)
                m.then_inc(spread_last, 1)

            def add(n, b, q, par):
                dve.wait_ge(o_ready, n + 1)
                if passed(b):
                    dve.wait_ge(stored[q], b * 16)
                v.tensor_tensor(o_s[:, q, :], o_ps[q][:], x1[:, par, bass.ts(q, HALF)], ALU.add).then_inc(o_added, 1)

            def emit(b, j, par, last):
                for q in range(QUADS):
                    n = b * QUADS + q
                    if q == 0 and not last:
                        cut(b + 1)
                    dve.wait_ge(pairs_ready, n + 1)
                    for g in range(NGR):
                        gg = n * NGR + g
                        if passed(gg - RING + 1):
                            dve.wait_ge(a_ready, gg - RING + 1)
                        low = pairs_s[pp, q, 0, bass.ts(g, NB)].rearrange("p (o n) -> p o n", o=1)
                        v.tensor_tensor(oh[pp, g % RING], low.to_broadcast([QCOLS, LO, NB]), iotan[pp],
                                        ALU.is_equal).then_inc(oh_ready, 1)
                        if g in (4, 5) and not (last and q == QUADS - 1):
                            spread(n + 1, 1 - q, g - 3)
                        if g == 5 and passed(n):
                            add(n - 1, b if q == 1 else b - 1, 1 - q, par if q == 1 else 1 - par)
                        if g == 2 and not (last and q == QUADS - 1):
                            heat(n + 1, 1 - q)

            cut(0)
            heat(0, 0)
            for part in range(1, PARTS):
                spread(0, 0, part)
            batches(dve, emit)
            add(B * QUADS - 1, B - 1, 1, 1)

        @block.tensor
        def _(pe):
            def turn_pairs(n, q, b):
                pe.wait_ge(rows_ready, (b + 1) * ROW_STEPS)
                if passed(n):
                    pe.wait_ge(pairs_ready, n)
                for r in range(ROWS):
                    m = nc.tensor.transpose(pairs_ps[pp, r], rowsb[:, r, bass.ts(q, QCOLS)], identb[:])
                m.then_inc(pairs_turned, 1)

            def turn_rows(b, par):
                pe.wait_ge(x1_ready, b + 1)
                if passed(b):
                    pe.wait_ge(xT_ready, b)
                for t in range(TILES):
                    m = nc.tensor.transpose(tr_ps[:, t // 4, bass.ts(t % 4, C)], x1[:, par, bass.ts(t, P)], con["ident"])
                m.then_inc(x1_turned, 1)

            def attend(n, q, g):
                gg = n * NGR + g
                pe.wait_ge(oh_ready, gg + 1)
                if passed(gg - 1):
                    pe.wait_ge(a_moved, gg - 1)
                for i in range(NB):
                    for part in range(PARTS):
                        m = nc.tensor.matmul(a_ps[g % 2][:, i].rearrange("p t e -> p (t e)"), oh[pp, g % RING, :, i],
                                             spr[q][pp, g * NB + i, part].rearrange("p t e -> p (t e)"),
                                             start=(part == 0), stop=(part == PARTS - 1))
                m.then_inc(a_ready, 1)

            def gathered(n, q, b, par):
                pe.wait_ge(a_moved, (n + 1) * NGR)
                pe.wait_ge(xT_ready, b + 1)
                if passed(n - 1):
                    pe.wait_ge(o_added, n - 1)
                for e in range(HI):
                    m = nc.tensor.matmul(o_ps[q][:], xT[:, par, e, :], at[:, q, e].rearrange("p t n -> p (t n)"),
                                         start=(e == 0), stop=(e == HI - 1))
                m.then_inc(o_ready, 1)

            def emit(b, j, par, last):
                for q in range(QUADS):
                    n = b * QUADS + q
                    if not (last and q == QUADS - 1):
                        turn_pairs(n + 1, 1 - q, b + q)
                    pe.wait_ge(spread_first, n + 1)
                    pe.wait_ge(spread_last, (n + 1) * (PARTS - 1))
                    for g in range(NGR):
                        attend(n, q, g)
                        if g == 1:
                            if passed(n):
                                gathered(n - 1, 1 - q, b if q == 1 else b - 1, par if q == 1 else 1 - par)
                            if q == QUADS - 1 and not last:
                                turn_rows(b + 1, 1 - par)

            pe.wait_ge(ln_step, 3)
            turn_rows(0, 0)
            turn_pairs(0, 0, 0)
            batches(pe, emit)
            gathered(B * QUADS - 1, 1, B - 1, 1)


_INS = ['x', 'ctx_4096', 'mask_Bx1x4096_ff1', 'L0_xattn_W_in', 'L0_xattn_b_in', 'L0_xattn_W_out', 'L0_xattn_b_out',
        'L1_xattn_W1', 'L1_xattn_g1', 'L1_xattn_b1', 'L1_xattn_W2', 'L1_xattn_g2', 'L1_xattn_b2', 'L1_xattn_W3',
        'L1_xattn_g3', 'L1_xattn_b3']


def kernel(**inputs):
    import numpy as _np
    import concourse.bacc as _bacc
    from concourse import mybir as _mybir
    from concourse.bass_utils import run_bass_kernel_spmd as _run

    nc = _bacc.Bacc("TRN2", target_bir_lowering=False, num_devices=1)
    arrays, args = {}, []
    for name in _INS + ["shape_constants"]:
        a = shape_constants() if name == "shape_constants" else _np.ascontiguousarray(inputs[name])
        arrays[f"in_{name}"] = a
        args.append(nc.dram_tensor(f"in_{name}", a.shape, _mybir.dt.from_np(a.dtype), kind="ExternalInput").ap())
    o = nc.dram_tensor("out_0", [B, C, T], _mybir.dt.float32, kind="ExternalOutput").ap()
    build(nc, *args, o)
    r = _run(nc, [arrays], core_ids=[0])
    return r.results[0]["out_0"]
```
